# Optimizing a Trainium2 kernel written in Bass

```python
import numpy as np
import jax
import jax.numpy as jnp

def _softmax(x, axis=-1):
    return jax.nn.softmax(x, axis=axis)

def _gelu(x):
    return jax.nn.gelu(x, approximate=True)

def _silu(x):
    return jax.nn.silu(x)

def _sigmoid(x):
    return jax.nn.sigmoid(x)

def _layernorm(x, axis=-1, eps=1e-05):
    m = jnp.mean(x, axis=axis, keepdims=True)
    v = jnp.var(x, axis=axis, keepdims=True)
    return (x - m) / jnp.sqrt(v + eps)

def _scatter_add(tgt, idx, src, axis=0):
    return tgt.at[idx].add(src)

def _segment_sum(src, seg, n):
    return jax.ops.segment_sum(src, seg, n)
kernel_name = 'mk_recurrent_d2_jaxref_r8_f4e357'

def setup_inputs(seed: int=0):
    np.random.seed(seed)
    _w = jnp.asarray

    def _L0_attn_setup():
        import jax, jax.numpy as jnp
        import numpy as np
        H = 128
        E = 2 * H
        S_DIM = 128
        B, S = (4, 256)
        key = jax.random.key(seed)
        ks = jax.random.split(key, 6)
        inputs = jax.random.normal(ks[0], (B, S, H), dtype=jnp.float32)
        W_uv = jax.random.normal(ks[1], (H, 2 * E + S_DIM), dtype=jnp.float32) * (1.0 / np.sqrt(H))
        b_uv = jnp.zeros((2 * E + S_DIM,), dtype=jnp.float32)
        gamma = jax.random.normal(ks[2], (2, S_DIM), dtype=jnp.float32) * 0.02
        beta = jnp.zeros((2, S_DIM), dtype=jnp.float32)
        W_out = jax.random.normal(ks[3], (E, H), dtype=jnp.float32) * (1.0 / np.sqrt(E))
        b_out = jnp.zeros((H,), dtype=jnp.float32)
        return {'inputs': inputs, 'W_uv': W_uv, 'b_uv': b_uv, 'gamma': gamma, 'beta': beta, 'W_out': W_out, 'b_out': b_out}
    _L0_attn_in = _L0_attn_setup()

    def _L0_ffn_setup():
        import jax, jax.numpy as jnp
        import numpy as np
        E = 8
        G = 4
        LG = 2
        TOPK = 2
        ROUTE_SCALE = 1.0

        def _grouped_mm(x, w, counts):
            counts = counts.astype(jnp.int32)
            if hasattr(jax.lax, 'ragged_dot'):
                return jax.lax.ragged_dot(x, w, counts)
            offs = jnp.cumsum(counts)
            eid = jnp.searchsorted(offs, jnp.arange(x.shape[0]), side='right')
            oh = jax.nn.one_hot(eid, w.shape[0], dtype=x.dtype)
            return jnp.einsum('nd,ne,edh->nh', x, oh, w)
        key = jax.random.key(seed)
        ks = jax.random.split(key, 8)
        bs, slen, dim, hid, shid = (2, 256, 128, 64, 128)
        std = 0.02
        return {'x': jax.random.normal(ks[0], (bs, slen, dim), jnp.float32), 'w_gate': jax.random.normal(ks[1], (E, dim), jnp.float32) * std, 'w1': jax.random.normal(ks[2], (E, dim, hid), jnp.float32) * std, 'w2': jax.random.normal(ks[3], (E, hid, dim), jnp.float32) * std, 'w3': jax.random.normal(ks[4], (E, dim, hid), jnp.float32) * std, 'sw1': jax.random.normal(ks[5], (shid, dim), jnp.float32) * std, 'sw2': jax.random.normal(ks[6], (dim, shid), jnp.float32) * std, 'sw3': jax.random.normal(ks[7], (shid, dim), jnp.float32) * std, 'expert_bias': jnp.zeros((E,), jnp.float32)}
    _L0_ffn_in = _L0_ffn_setup()

    def _L1_attn_setup():
        import jax, jax.numpy as jnp
        import numpy as np
        B, S = (2, 256)
        HIDDEN, MLP = (128, 256)
        N_STATE, DT_RANK, CONV_K = (16, 64, 4)

        def _causal_depthwise_conv(u, conv_w, conv_b):
            u_pad = jnp.pad(u, ((0, 0), (CONV_K - 1, 0), (0, 0)))
            seq = u.shape[1]
            y = sum((u_pad[:, k:k + seq, :] * conv_w[:, k] for k in range(CONV_K)))
            return y + conv_b

        def _selective_scan(u, A_log, x_proj_w, dt_proj_w, dt_proj_b, D_skip):
            xp = u @ x_proj_w
            delta = jax.nn.softplus(xp[..., :DT_RANK] @ dt_proj_w + dt_proj_b)
            Bm = xp[..., DT_RANK:DT_RANK + N_STATE]
            Cm = xp[..., DT_RANK + N_STATE:]
            A = -jnp.exp(A_log)
            dA = jnp.exp(delta[..., None] * A)
            dBu = delta[..., None] * Bm[:, :, None, :] * u[..., None]

            def step(h, inp):
                dA_t, dBu_t, C_t = inp
                h = dA_t * h + dBu_t
                y = jnp.einsum('bdn,bn->bd', h, C_t)
                return (h, y)
            h0 = jnp.zeros((u.shape[0], u.shape[2], N_STATE), u.dtype)
            _, ys = jax.lax.scan(step, h0, (dA.transpose(1, 0, 2, 3), dBu.transpose(1, 0, 2, 3), Cm.transpose(1, 0, 2)))
            return ys.transpose(1, 0, 2) + u * D_skip
        key = jax.random.key(seed)
        ks = jax.random.split(key, 14)
        s = 0.02
        return {'x': jax.random.normal(ks[0], (B, S, HIDDEN), jnp.float32), 'W1': jax.random.normal(ks[1], (HIDDEN, MLP), jnp.float32) * s, 'b1': jnp.zeros((MLP,), jnp.float32), 'W2': jax.random.normal(ks[2], (HIDDEN, MLP), jnp.float32) * s, 'b2': jnp.zeros((MLP,), jnp.float32), 'conv_w': jax.random.normal(ks[3], (MLP, CONV_K), jnp.float32) * s, 'conv_b': jnp.zeros((MLP,), jnp.float32), 'A_log': jnp.log(jnp.broadcast_to(jnp.arange(1, N_STATE + 1, dtype=jnp.float32), (MLP, N_STATE))), 'x_proj_w': jax.random.normal(ks[4], (MLP, DT_RANK + 2 * N_STATE), jnp.float32) * s, 'dt_proj_w': jax.random.normal(ks[5], (DT_RANK, MLP), jnp.float32) * s, 'dt_proj_b': jnp.full((MLP,), -4.0, jnp.float32), 'D_skip': jnp.ones((MLP,), jnp.float32), 'Wo': jax.random.normal(ks[6], (MLP, HIDDEN), jnp.float32) * s, 'bo': jnp.zeros((HIDDEN,), jnp.float32)}
    _L1_attn_in = _L1_attn_setup()

    def _L1_ffn_setup():
        import jax, jax.numpy as jnp
        import numpy as np
        B, T, D, H, E = (4, 128, 128, 512, 8)
        TOP_K = 2
        key = jax.random.key(seed)
        ks = jax.random.split(key, 7)
        s = 0.02
        return {'x': jax.random.normal(ks[0], (B, T, D), dtype=jnp.float32), 'gate_w': jax.random.normal(ks[1], (D, E), dtype=jnp.float32) * s, 'gate_b': jnp.zeros((E,), dtype=jnp.float32), 'w1': jax.random.normal(ks[2], (E, D, H), dtype=jnp.float32) * s, 'b1': jnp.zeros((E, H), dtype=jnp.float32), 'w2': jax.random.normal(ks[3], (E, H, D), dtype=jnp.float32) * s, 'b2': jnp.zeros((E, D), dtype=jnp.float32)}
    _L1_ffn_in = _L1_ffn_setup()
    _d = {'L0_attn_inputs': _L0_attn_in['inputs'], 'L0_attn_W_uv': _L0_attn_in['W_uv'], 'L0_attn_b_uv': _L0_attn_in['b_uv'], 'L0_attn_gamma': _L0_attn_in['gamma'], 'L0_attn_beta': _L0_attn_in['beta'], 'L0_attn_W_out': _L0_attn_in['W_out'], 'L0_attn_b_out': _L0_attn_in['b_out'], 'L0_ffn_w_gate': _L0_ffn_in['w_gate'], 'L0_ffn_w1': _L0_ffn_in['w1'], 'L0_ffn_w2': _L0_ffn_in['w2'], 'L0_ffn_w3': _L0_ffn_in['w3'], 'L0_ffn_sw1': _L0_ffn_in['sw1'], 'L0_ffn_sw2': _L0_ffn_in['sw2'], 'L0_ffn_sw3': _L0_ffn_in['sw3'], 'L0_ffn_expert_bias': _L0_ffn_in['expert_bias'], 'L1_attn_W1': _L1_attn_in['W1'], 'L1_attn_b1': _L1_attn_in['b1'], 'L1_attn_W2': _L1_attn_in['W2'], 'L1_attn_b2': _L1_attn_in['b2'], 'L1_attn_conv_w': _L1_attn_in['conv_w'], 'L1_attn_conv_b': _L1_attn_in['conv_b'], 'L1_attn_A_log': _L1_attn_in['A_log'], 'L1_attn_x_proj_w': _L1_attn_in['x_proj_w'], 'L1_attn_dt_proj_w': _L1_attn_in['dt_proj_w'], 'L1_attn_dt_proj_b': _L1_attn_in['dt_proj_b'], 'L1_attn_D_skip': _L1_attn_in['D_skip'], 'L1_attn_Wo': _L1_attn_in['Wo'], 'L1_attn_bo': _L1_attn_in['bo'], 'L1_ffn_gate_w': _L1_ffn_in['gate_w'], 'L1_ffn_gate_b': _L1_ffn_in['gate_b'], 'L1_ffn_w1': _L1_ffn_in['w1'], 'L1_ffn_b1': _L1_ffn_in['b1'], 'L1_ffn_w2': _L1_ffn_in['w2'], 'L1_ffn_b2': _L1_ffn_in['b2']}
    _x0 = _d['L0_attn_inputs']
    _d['L0_attn_inputs'] = jax.random.normal(jax.random.fold_in(jax.random.key(seed), 1), (4, 512, 128), dtype=_x0.dtype)
    del _x0
    return _d

def reference(L0_attn_inputs, L0_attn_W_uv, L0_attn_b_uv, L0_attn_gamma, L0_attn_beta, L0_attn_W_out, L0_attn_b_out, L0_ffn_w_gate, L0_ffn_w1, L0_ffn_w2, L0_ffn_w3, L0_ffn_sw1, L0_ffn_sw2, L0_ffn_sw3, L0_ffn_expert_bias, L1_attn_W1, L1_attn_b1, L1_attn_W2, L1_attn_b2, L1_attn_conv_w, L1_attn_conv_b, L1_attn_A_log, L1_attn_x_proj_w, L1_attn_dt_proj_w, L1_attn_dt_proj_b, L1_attn_D_skip, L1_attn_Wo, L1_attn_bo, L1_ffn_gate_w, L1_ffn_gate_b, L1_ffn_w1, L1_ffn_b1, L1_ffn_w2, L1_ffn_b2):

    def _L0_attn_ref(inputs, W_uv, b_uv, gamma, beta, W_out, b_out):
        import jax, jax.numpy as jnp
        import numpy as np
        H = 128
        E = 2 * H
        S_DIM = 128
        B, S = (4, 256)
        seq_len = inputs.shape[1]
        uvb = jax.nn.silu(jnp.einsum('bsh,hf->bsf', inputs, W_uv) + b_uv)
        u = uvb[..., :E]
        v = uvb[..., E:2 * E]
        base = uvb[..., 2 * E:]
        qk = base[..., None, :] * gamma + beta
        q, k = (qk[..., 0, :], qk[..., 1, :])
        scores = jnp.einsum('bns,bms->bnm', q, k) / seq_len
        sq = jnp.square(jax.nn.relu(scores))
        attn_v = jnp.einsum('bnm,bme->bne', sq, v)
        return jnp.einsum('bne,eh->bnh', u * attn_v, W_out) + b_out

    def _L0_ffn_ref(x, w_gate, w1, w2, w3, sw1, sw2, sw3, expert_bias):
        import jax, jax.numpy as jnp
        import numpy as np
        E = 8
        G = 4
        LG = 2
        TOPK = 2
        ROUTE_SCALE = 1.0

        def _grouped_mm(x, w, counts):
            counts = counts.astype(jnp.int32)
            if hasattr(jax.lax, 'ragged_dot'):
                return jax.lax.ragged_dot(x, w, counts)
            offs = jnp.cumsum(counts)
            eid = jnp.searchsorted(offs, jnp.arange(x.shape[0]), side='right')
            oh = jax.nn.one_hot(eid, w.shape[0], dtype=x.dtype)
            return jnp.einsum('nd,ne,edh->nh', x, oh, w)
        bs, slen, dim = x.shape
        xf = x.reshape(-1, dim)
        N = xf.shape[0]
        logits = xf @ w_gate.T
        scores = jax.nn.softmax(logits.astype(jnp.float32), axis=-1)
        original = scores
        s = (scores + expert_bias).reshape(N, G, E // G)
        group_scores = jax.lax.top_k(s, 2)[0].sum(-1)
        top_groups = jax.lax.top_k(group_scores, LG)[1]
        keep = jnp.zeros((N, G), bool).at[jnp.arange(N)[:, None], top_groups].set(True)
        masked = jnp.where(keep[:, :, None], s, -jnp.inf).reshape(N, E)
        topk_idx = jax.lax.top_k(masked, TOPK)[1]
        weights = (jnp.take_along_axis(original, topk_idx, axis=1) * ROUTE_SCALE).astype(x.dtype)
        counts = jnp.bincount(topk_idx.reshape(-1), length=E)
        flat_idx = topk_idx.reshape(-1)
        routed_in = xf[flat_idx]
        routed_in = (routed_in.astype(jnp.float32) * weights.reshape(-1, 1)).astype(x.dtype)
        h = jax.nn.silu(_grouped_mm(routed_in, w1, counts)) * _grouped_mm(routed_in, w3, counts)
        routed_out = _grouped_mm(h, w2, counts)
        shared = jax.nn.silu(xf @ sw1.T) * (xf @ sw3.T) @ sw2.T
        out = shared.at[flat_idx].add(routed_out)
        return out.reshape(bs, slen, dim)

    def _L1_attn_ref(x, W1, b1, W2, b2, conv_w, conv_b, A_log, x_proj_w, dt_proj_w, dt_proj_b, D_skip, Wo, bo):
        import jax, jax.numpy as jnp
        import numpy as np
        B, S = (2, 256)
        HIDDEN, MLP = (128, 256)
        N_STATE, DT_RANK, CONV_K = (16, 64, 4)

        def _causal_depthwise_conv(u, conv_w, conv_b):
            u_pad = jnp.pad(u, ((0, 0), (CONV_K - 1, 0), (0, 0)))
            seq = u.shape[1]
            y = sum((u_pad[:, k:k + seq, :] * conv_w[:, k] for k in range(CONV_K)))
            return y + conv_b

        def _selective_scan(u, A_log, x_proj_w, dt_proj_w, dt_proj_b, D_skip):
            xp = u @ x_proj_w
            delta = jax.nn.softplus(xp[..., :DT_RANK] @ dt_proj_w + dt_proj_b)
            Bm = xp[..., DT_RANK:DT_RANK + N_STATE]
            Cm = xp[..., DT_RANK + N_STATE:]
            A = -jnp.exp(A_log)
            dA = jnp.exp(delta[..., None] * A)
            dBu = delta[..., None] * Bm[:, :, None, :] * u[..., None]

            def step(h, inp):
                dA_t, dBu_t, C_t = inp
                h = dA_t * h + dBu_t
                y = jnp.einsum('bdn,bn->bd', h, C_t)
                return (h, y)
            h0 = jnp.zeros((u.shape[0], u.shape[2], N_STATE), u.dtype)
            _, ys = jax.lax.scan(step, h0, (dA.transpose(1, 0, 2, 3), dBu.transpose(1, 0, 2, 3), Cm.transpose(1, 0, 2)))
            return ys.transpose(1, 0, 2) + u * D_skip
        gate = jax.nn.sigmoid(x @ W2 + b2)
        u = x @ W1 + b1
        u = jax.nn.sigmoid(_causal_depthwise_conv(u, conv_w, conv_b))
        y = _selective_scan(u, A_log, x_proj_w, dt_proj_w, dt_proj_b, D_skip)
        return y * gate @ Wo + bo

    def _L1_ffn_ref(x, gate_w, gate_b, w1, b1, w2, b2):
        import jax, jax.numpy as jnp
        import numpy as np
        B, T, D, H, E = (4, 128, 128, 512, 8)
        TOP_K = 2
        gate_scores = jax.nn.softmax(x @ gate_w + gate_b, axis=-1)
        top_g, top_i = jax.lax.top_k(gate_scores, TOP_K)
        h = jax.nn.relu(jnp.einsum('btd,edh->bteh', x, w1) + b1)
        expert_out = jnp.einsum('bteh,ehd->bted', h, w2) + b2
        sel = jnp.take_along_axis(expert_out, top_i[..., None], axis=2)
        return jnp.sum(top_g[..., None] * sel, axis=2)
    x = L0_attn_inputs
    xn = _layernorm(x, axis=-1)
    s = _L0_attn_ref(xn, L0_attn_W_uv, L0_attn_b_uv, L0_attn_gamma, L0_attn_beta, L0_attn_W_out, L0_attn_b_out)
    g = _silu(_L0_ffn_ref(xn, L0_ffn_w_gate, L0_ffn_w1, L0_ffn_w2, L0_ffn_w3, L0_ffn_sw1, L0_ffn_sw2, L0_ffn_sw3, L0_ffn_expert_bias))
    x = x + s * g
    xn = _layernorm(x, axis=-1)
    s = _L1_attn_ref(xn, L1_attn_W1, L1_attn_b1, L1_attn_W2, L1_attn_b2, L1_attn_conv_w, L1_attn_conv_b, L1_attn_A_log, L1_attn_x_proj_w, L1_attn_dt_proj_w, L1_attn_dt_proj_b, L1_attn_D_skip, L1_attn_Wo, L1_attn_bo)
    g = _silu(_L1_ffn_ref(xn, L1_ffn_gate_w, L1_ffn_gate_b, L1_ffn_w1, L1_ffn_b1, L1_ffn_w2, L1_ffn_b2))
    x = x + s * g
    return x

_drawn_inputs = setup_inputs


def setup_inputs(seed=0):
    import zlib

    import numpy as np

    out = dict(_drawn_inputs(seed))
    spreads = {'L0_attn_b_uv': (0.0, 0.8),
     'L0_attn_beta': (0.0, 0.8),
     'L0_attn_b_out': (0.0, 0.8),
     'L0_ffn_expert_bias': (0.0, 0.8),
     'L1_attn_b1': (0.0, 2.0),
     'L1_attn_b2': (0.0, 2.0),
     'L1_attn_conv_b': (0.0, 2.0),
     'L1_attn_dt_proj_b': (-4.0, 0.6),
     'L1_attn_D_skip': (1.0, 0.6),
     'L1_attn_bo': (0.0, 2.0),
     'L1_ffn_gate_b': (0.0, 0.8),
     'L1_ffn_b1': (0.0, 0.8),
     'L1_ffn_b2': (0.0, 2.0)}
    factors = {'L0_attn_W_uv': 8.0,
     'L0_attn_gamma': 8.0,
     'L0_attn_W_out': 8.0,
     'L0_ffn_w_gate': 64.0,
     'L0_ffn_w1': 8.0,
     'L0_ffn_w2': 8.0,
     'L0_ffn_w3': 8.0,
     'L0_ffn_sw1': 8.0,
     'L0_ffn_sw2': 8.0,
     'L0_ffn_sw3': 8.0,
     'L1_attn_W1': 8.0,
     'L1_attn_W2': 8.0,
     'L1_attn_conv_w': 8.0,
     'L1_attn_A_log': 8.0,
     'L1_attn_x_proj_w': 8.0,
     'L1_attn_dt_proj_w': 8.0,
     'L1_attn_Wo': 8.0,
     'L1_ffn_gate_w': 8.0,
     'L1_ffn_w1': 8.0,
     'L1_ffn_w2': 8.0}
    for name, (base, spread) in spreads.items():
        noise = np.random.default_rng([zlib.crc32(name.encode()), seed]).standard_normal(out[name].shape)
        drawn = base * np.exp(spread * noise) if base else spread * noise
        out[name] = jnp.asarray(drawn.astype(out[name].dtype))
    for name, factor in factors.items():
        out[name] = (out[name] * factor).astype(out[name].dtype)
    return out
```

```python
from contextlib import ExitStack

import concourse.bass as bass
from concourse import mybir

ALU = mybir.AluOpType
ACT = mybir.ActivationFunctionType
AX = mybir.AxisListType
F32 = mybir.dt.float32
BF16 = mybir.dt.bfloat16
I32 = mybir.dt.int32

P = 128
NB = 4
S = 512
D = 128
TB = S // P
NT = NB * TB
E = 8
TOPK = 2
GROUPS = 4
GE = 256
HID0 = 64
MLP = 256
HV = MLP // P
NS = 16
RANK = 64
TAPS = 4
HID1 = 512
HC = HID1 // P
SLOTS = (NT * P * TOPK) // P + E - 1
EPS = 1e-5
BIG = 1e30

BATCHES = [1, 2, 3, 0]
LAST = NB - 1
LAG = 3

A_UV, A_SW1, A_SW3, A_SW2, A_WOUT, A_GATE0, A_GATE1, A_END = (
    0, 640, 768, 896, 1024, 1280, 1288, 1296)
B_W13, B_W1, B_W2, B_XP, B_WO, B_END = 0, 1024, 1280, 1536, 1728, 1984
H_W2, H_DT, H_END = 0, E * D, E * D + MLP
C_BU, C_BB, C_GAM, C_BET, C_B1, C_B2, C_CW, C_CB, C_DTB, C_D, C_ALOG, C_END = (
    0, 2, 3, 5, 7, 9, 11, 19, 21, 23, 25, 57)
R_BV, R_BOUT, R_EB, R_BO, R_GB, R_END = 0, 256, 384, 392, 520, 528
X_W1, X_W2, X_B1, X_B2, X_END = 0, 512, 1024, 1028, 1156


def build_order():

    def attention0(i):
        return ([("base", i), ("u0", i, 0), ("u0", i, 1), ("sh_gate", i), ("sh_up", i), ("v0", i, 0), ("v0", i, 1)]
                + ([("sh_out", i)] if i != LAST else [])
                + [("score", i, m) for m in range(TB)] + [("attn", i, 0), ("attn", i, 1), ("wout", i)])

    def before_scan(i):
        return ([("stats", 1, i), ("norm", 1, i), ("xt", 1, i), ("logits", 1, i), ("u1", i, 0), ("u1", i, 1),
                 ("gate1", i, 0), ("gate1", i, 1), ("u1_sig", i), ("xproj", i), ("dt", i, 0), ("dt", i, 1),
                 ("softplus", i)])

    def scan(i):
        return [("scan", i, s) for s in range(NS + LAG)] + [("scan_out", i), ("wo1", i)]

    def spread(main, extra):
        out, done = [], 0
        for k, item in enumerate(main):
            out.append(item)
            want = (k + 1) * len(extra) // len(main)
            out += extra[done:want]
            done = want
        return out

    order = [("stats", 0, 0), ("norm", 0, 0), ("xt", 0, 0)]
    order += [("stats", 0, i) for i in range(1, NB)] + [("norm", 0, i) for i in range(1, NB)]
    order += [("xt", 0, i) for i in range(1, NB)] + [("logits", 0, i) for i in range(NB)]
    order += attention0(0) + [("x1", 0)] + before_scan(0)
    order += spread([("route0_soft",)] + attention0(1) + [("x1", 1), ("route0_group",)] + before_scan(1), scan(0))
    order += spread(
        [("route0_rank",), ("route0_pick",), ("count0",)] + attention0(2) + [("x1", 2), ("route0_pairs",), ("pair_in",)]
        + before_scan(2), scan(1))
    routed = [("oct", q) for q in range(NT // 4)]
    for n in range(2):
        routed += [("pair_h", q) for q in range(n * NT // 4, (n + 1) * NT // 4)] + [("pair_act", n), ("pair_sum", n)]
    routed += [("sh_out", LAST), ("x1", LAST)]
    order += spread(attention0(LAST) + routed + before_scan(LAST)
                    + [("route1_soft",), ("route1_rank",), ("rank1",), ("count1",), ("route1_slots",), ("scatter",)],
                    scan(2))
    slots = []
    for m in range(SLOTS + 2):
        slots += [("slot_t", m)] if m < SLOTS else []
        slots += [("slot_h", m - 1)] if 0 <= m - 1 < SLOTS else []
        slots += [("slot_y", m - 2)] if 0 <= m - 2 < SLOTS else []
    tail = scan(3)
    order += spread(slots, tail[:12]) + [("gather",)] + tail[12:]
    order += [("combine", i) for i in range(NB)]
    return order


CONSUMER = {
    "xt": "act", "logits": "dve", "base": "act", "u0": "act", "sh_gate": "act", "sh_up": "dve", "v0": "dve",
    "score": "act", "attn": "dve", "wout": "dve", "sh_out": "act", "pair_in": "dve", "oct": "act",
    "pair_h": "dve", "pair_sum": "dve", "u1": "act", "gate1": "act", "xproj": "act", "dt": "act", "wo1": "dve",
    "rank1": "dve", "count0": "dve", "count1": "dve", "slot_t": "dve", "slot_h": "act", "slot_y": "dve",
}
BANKS = 4
N_SET, N_MADE = 14, 7


def build(nc, x, pack_a, pack_b, pack_h, cols, rows, experts, out, slot_in, slot_out):
    order = build_order()
    jobs = [item for item in order if item[0] in CONSUMER]
    job_at = {item: n for n, item in enumerate(jobs)}
    emptied_at, so_far = {}, {"act": 0, "dve": 0}
    for item in jobs:
        so_far[CONSUMER[item[0]]] += 1
        emptied_at[item] = so_far[CONSUMER[item[0]]]

    x_v = x.rearrange("b (t p) d -> p (b t) d", p=P)
    out_v = out.rearrange("b (t p) d -> p (b t) d", p=P)

    with ExitStack() as ctx:
        def sb(name, shape, dt=F32):
            return ctx.enter_context(nc.sbuf_tensor(name, shape, dt))

        def sem(name):
            return ctx.enter_context(nc.semaphore(name))

        wa = sb("wa", [P, A_END])
        wb = sb("wb", [P, B_END])
        wh = sb("wh", [HID0, H_END])
        col = sb("col", [P, C_END])
        row = sb("row", [P, R_END])
        ident = sb("ident", [P, P])
        pick_state = sb("pick_state", [3 * 2 * NS, 2 * NS], BF16)
        upper = sb("upper", [P, P], BF16)
        ones = sb("ones", [P, P], BF16)
        before4 = sb("before4", [P, GROUPS, GROUPS], BF16)
        before8 = sb("before8", [P, E, E], BF16)
        row_no = sb("row_no", [P, NT, TOPK])
        mult128 = sb("mult128", [P, NT])
        slot_no = sb("slot_no", [P, SLOTS])
        neg_a = sb("neg_a", [P, HV, NS])

        X = sb("X", [P, NT, D])
        XN = sb("XN", [P, NT, D])
        XNT = sb("XNT", [P, NT * P])
        XNT1 = sb("XNT1", [P, S])
        stat = sb("stat", [P, TB, 6])
        mv = sb("mv", [P, NT, 2])
        veps = sb("veps", [P, NT])
        sdev = sb("sdev", [P, NT])
        rstd = sb("rstd", [P, NT])

        base = sb("base", [P, S])
        qT = sb("qT", [P, S])
        kT = base
        sh_h = sb("sh_h", [P, S])
        uv = sb("uv", [P, 4 * S])
        uT = uv[:, 0:2 * S].rearrange("p (h t) -> p h t", h=2)
        v = uv[:, 2 * S:4 * S].rearrange("p (t e) -> p t e", t=TB)
        sq = sb("sq", [P, TB, S])
        s0 = sb("s0", [P, TB, D])
        g0 = sb("g0", [P, TB, D])

        upad = sb("upad", [P, HV, TAPS - 1 + S])
        u1 = sb("u1", [P, 2, HV, S])
        g1 = sb("g1", [P, 2, HV, S])
        dtT = sb("dtT", [RANK, S])
        bc = sb("bc", [2 * NS, S])
        bc_mid = sb("bc_mid", [2 * NS, S], BF16)
        bcs = sb("bcs", [3 * 2 * NS, 2, S], BF16)
        delta = sb("delta", [P, 2, HV, S])
        du = sb("du", [P, 2, HV, S])
        N_DA, N_DBU, N_ST, N_CS, N_PR = 3, 3, 2, 2, 3
        decay = sb("decay", [P, N_DA, HV, S])
        drive = sb("drive", [P, N_DBU, HV, S])
        state = sb("state", [P, N_ST, HV, S])
        cs = sb("cs", [P, N_CS, S])
        prod = sb("prod", [P, N_PR, HV, S])
        s1 = XNT[:, :].rearrange("p (t d) -> p t d", t=NT)

        lg = sb("lg", [P, 2, NT, E])
        sc = sb("sc", [P, NT, E])
        sel_s = sb("sel_s", [P, NT, E])
        red = sb("red", [P, NT])
        red2 = sb("red2", [P, NT])
        grp = sb("grp", [P, NT, GROUPS])
        keep = sb("keep", [P, NT, GROUPS])
        cmp_a = sb("cmp_a", [P, NT, E, E], BF16)
        cmp_b = sb("cmp_b", [P, NT, E, E], BF16)
        bc_res = cmp_b[0:2 * NS, :, :, :].rearrange("p t i j -> p (t i j)").bitcast(F32)
        rank = sb("rank", [P, NT, E])
        pick = sb("pick", [P, NT, TOPK, E])
        padded = sb("padded", [P, 2 * NT - 1, E], BF16)
        picked = padded[:, NT - 1:, :]
        tmp8 = sb("tmp8", [P, NT, TOPK, E])
        wgt = sb("wgt", [P, NT, TOPK])
        cnt = sb("cnt", [P, E])
        cum = sb("cum", [P, E + 1])
        ge = sb("ge", [P, NT * TOPK, E + 1])
        seg = sb("seg", [P, NT * TOPK, E])
        ab = sb("ab", [P, TOPK, P])
        ntile = sb("ntile", [P, E])
        cmp_f = cmp_a[:, :, :, :].rearrange("p t i j -> p (t i j)").bitcast(F32)
        cmp_t = cmp_f[:, 0:E * NT].rearrange("p (e t) -> p e t", e=E)
        ctile = sb("ctile", [P, E])
        first_row = sb("first_row", [P, E])
        cmp_s = cmp_f[:, E * NT:E * NT + SLOTS * E].rearrange("p (s e) -> p s e", e=E)
        slot_f = sb("slot_f", [P, SLOTS])
        slot_e = sb("slot_e", [P, SLOTS], I32)
        pos_f = sb("pos_f", [P, NT, TOPK])
        pos = sb("pos", [P, TOPK, NT], I32)

        PAIR = NT * TOPK * HID0
        N_W = 3
        region = sb("region", [P, 3 * PAIR])
        pair = region[:, 0:PAIR].rearrange("p (t k c) -> p t k c", t=NT, k=TOPK)
        pairT = region[:, PAIR:2 * PAIR]
        gate0 = region[:, PAIR:PAIR + PAIR // 2].rearrange("p (j c) -> p j c", c=HID0)
        ph = region[:, 2 * PAIR:3 * PAIR].rearrange("p (j c) -> p j c", c=2 * HID0)
        xm = region[:, 2 * PAIR:2 * PAIR + E * (P + 1)]
        htp = sq[0:HID0, 0:2, :].rearrange("p m t -> p (m t)").rearrange("p (g c) -> p g c", g=E)
        at = 0

        def part(n):
            nonlocal at
            at += n
            return region[:, at - n:at]

        wst = [part(X_END) for _ in range(N_W)]
        xg = [part(D) for _ in range(3)]
        xgT = [part(D) for _ in range(2)]
        hT = [part(HC * P).rearrange("p (c t) -> p c t", c=HC) for _ in range(2)]
        ysb = [part(D) for _ in range(3)]
        assert at <= 3 * PAIR
        yk = [sq[:, :, :].rearrange("p m t -> p (m t)").rearrange("p (t d) -> p t d", t=NT),
              uv[:, :].rearrange("p (t d) -> p t d", t=NT)]

        work = [ctx.enter_context(nc.psum_tensor(f"work{n}", [P, S], F32)) for n in range(BANKS)]
        p_b = ctx.enter_context(nc.psum_tensor("p_b", [P, S], F32))
        p_c = ctx.enter_context(nc.psum_tensor("p_c", [P, S], F32))
        p_y = [ctx.enter_context(nc.psum_tensor(f"p_y{h}", [P, S], F32)) for h in range(HV)]

        x_in = [sem(f"x_in{i}") for i in range(NB)]
        wa_in, wb_in, wh_in, col_in, row_in = (sem(n) for n in ("wa_in", "wb_in", "wh_in", "col_in", "row_in"))
        const_set, const_made = sem("const_set"), sem("const_made")
        slots_zeroed = sem("slots_zeroed")
        a_ready, a_negated = sem("a_ready"), sem("a_negated")
        filled = sem("filled")
        emptied = {"act": sem("emptied_by_act"), "dve": sem("emptied_by_dve")}
        dve_step, act_step = sem("dve_step"), sem("act_step")
        var_ready, sd_ready, xn_ready = sem("var_ready"), sem("sd_ready"), sem("xn_ready")
        qk_ready, v_ready, sq_ready = sem("qk_ready"), sem("v_ready"), sem("sq_ready")
        x1_done = sem("x1_done")
        conv_ready, u1_ready = sem("conv_ready"), sem("u1_ready")
        bcs_ready = sem("bcs_ready")
        na_ready, l_ready, du_ready = sem("na_ready"), sem("l_ready"), sem("du_ready")
        b_cast, c_cast, cs_ready, decay_ready = sem("b_cast"), sem("c_cast"), sem("cs_ready"), sem("decay_ready")
        drive_ready, state_ready, prod_ready, summed = (
            sem("drive_ready"), sem("state_ready"), sem("prod_ready"), sem("summed"))
        y_read, y_ready = sem("y_read"), sem("y_ready")
        soft_in, soft_exp = sem("soft_in"), sem("soft_exp")
        picked_ready = sem("picked_ready")
        xm_ready, pair_ready = sem("xm_ready"), sem("pair_ready")
        pair_sig, pair_out = sem("pair_sig"), sem("pair_out")
        pos_ready = sem("pos_ready")
        scattered = sem("scattered")
        w_in = [sem(f"w_in{n}") for n in range(N_W)]
        xg_in = [sem(f"xg_in{n}") for n in range(3)]
        y_out = [sem(f"y_out{n}") for n in range(3)]
        gathered = [sem(f"gathered{i}") for i in range(NB)]
        mix_ready, mix_silu, out_ready, stored = sem("mix_ready"), sem("mix_silu"), sem("out_ready"), sem("stored")

        def bank(item):
            return work[job_at[item] % BANKS]

        def wait_filled(eng, item):
            eng.wait_ge(filled, job_at[item] + 1)

        def wait_emptied(eng, item):
            eng.wait_ge(emptied[CONSUMER[item[0]]], emptied_at[item])

        def tiles(i):
            b = BATCHES[i]
            return slice(b * TB, (b + 1) * TB)

        def tokens(i):
            b = BATCHES[i]
            return slice(b * S, (b + 1) * S)

        def step_no(i, n):
            return i * NS + n

        block = ctx.enter_context(nc.Block())

        @block.sync
        def _(sp):
            for i in range(NB):
                sp.dma_start(X[:, tiles(i), :], x_v[:, tiles(i), :]).then_inc(x_in[i], 16)
                if i == 0:
                    sp.dma_start(wa[:, :], pack_a).then_inc(wa_in, 16)
            sp.dma_start(wb[:, :], pack_b).then_inc(wb_in, 16)
            sp.wait_ge(const_set, 2)
            sp.dma_start(slot_in.rearrange("s p d -> p s d"),
                         region[:, 0:D].unsqueeze(1).broadcast_to([P, SLOTS, D])).then_inc(slots_zeroed, 16)

            def load_slot(m):
                if m == 0:
                    sp.wait_ge(pos_ready, 1)
                    sp.wait_ge(scattered, 16 * NT * TOPK)
                if m >= N_W:
                    wait_filled(sp, ("slot_y", m - N_W))
                    wait_emptied(sp, ("slot_y", m - N_W))
                which = sp.value_load(slot_e[0:1, m:m + 1], min_val=0, max_val=E - 1)
                sp.dma_start(wst[m % N_W], experts[bass.ds(which, 1), :, :].rearrange("e p f -> (e p) f"))\
                    .then_inc(w_in[m % N_W], 16)
                sp.dma_start(xg[m % 3], slot_in[m]).then_inc(xg_in[m % 3], 16)

            for item in order:
                kind, m = item[0], item[-1]
                if kind == "slot_t":
                    if m == 0:
                        for k in range(N_W):
                            load_slot(k)
                elif kind == "slot_y":
                    wait_emptied(sp, item)
                    sp.dma_start(slot_out[m], ysb[m % 3]).then_inc(y_out[m % 3], 16)
                    if m + N_W < SLOTS:
                        load_slot(m + N_W)
                elif kind == "combine":
                    sp.wait_ge(out_ready, m + 1)
                    sp.dma_start(out_v[:, tiles(m), :], X[:, tiles(m), :]).then_inc(stored, 16)
            sp.wait_ge(stored, 16 * NB)

        @block.gpsimd
        def _(pool):
            pool.memset(ident[:, :], 0.0).then_inc(const_set, 1)
            pool.wait_ge(const_set, 1)
            pool.affine_select(out=ident[:, :], in_=ident[:, :], compare_op=ALU.not_equal, fill=1.0, base=0,
                               pattern=[[-1, P]], channel_multiplier=1).then_inc(const_made, 1)
            pool.memset(region[:, 0:D], 0.0).then_inc(const_set, 1)
            for t, value in ((ones[:, :], 1.0), (upad[:, :, 0:TAPS - 1], 0.0), (decay[:, :, :, 0:1], 0.0),
                             (before4[:, :, :], 1.0), (before8[:, :, :], 1.0), (pick_state[:, :], 0.0), (padded[:, 0:NT - 1, :], 0.0),
                             (xm, 0.0), (ab[:, :, :], 0.0)):
                pool.memset(t, value).then_inc(const_set, 1)
            for t, pattern, step in ((row_no[:, :, :], [[2 * P, NT], [1, TOPK]], 2), (mult128[:, :], [[P, NT]], 0),
                                     (slot_no[:, :], [[1, SLOTS]], 0)):
                pool.iota(t, pattern, base=0, channel_multiplier=step, allow_small_or_imprecise_dtypes=True)\
                    .then_inc(const_set, 1)
            pool.wait_ge(const_set, N_SET)
            pool.affine_select(out=upper[:, :], in_=ones[:, :], compare_op=ALU.is_gt, fill=0.0, base=0,
                               pattern=[[1, P]], channel_multiplier=-1).then_inc(const_made, 1)
            for m, n in ((before4, GROUPS), (before8, E)):
                pool.affine_select(out=m[:, :, :], in_=m[:, :, :], compare_op=ALU.is_gt, fill=0.0, base=0,
                                   pattern=[[1, n], [-1, n]], channel_multiplier=0).then_inc(const_made, 1)
            for j in range(3):
                pool.wait_ge(const_made, 4 + j)
                m = pick_state[2 * NS * j:2 * NS * (j + 1), :]
                pool.affine_select(out=m, in_=m, compare_op=ALU.not_equal, fill=1.0, base=0,
                                   pattern=[[-1, 2 * NS]], channel_multiplier=1).then_inc(const_made, 1)

            for item in order:
                kind = item[0]
                if kind == "scan":
                    _, i, s = item
                    if 1 <= s <= NS:
                        g = step_no(i, s - 1)
                        pool.wait_ge(state_ready, g + 1)
                        pool.wait_ge(cs_ready, g + 1)
                        if g >= N_PR:
                            pool.wait_ge(summed, g - N_PR + 1)
                        c = cs[:, g % N_CS, :].unsqueeze(1).broadcast_to([P, HV, S])
                        pool.tensor_tensor(prod[:, g % N_PR], state[:, g % N_ST], c, ALU.mult)\
                            .then_inc(prod_ready, 1)
                elif kind == "scatter":
                    pool.wait_ge(pos_ready, 1)
                    pool.wait_ge(slots_zeroed, 16)
                    pool.wait_ge(xn_ready, 2 * NB)
                    for t in range(NT):
                        for k in range(TOPK):
                            pool.indirect_dma_start(slot_in.rearrange("s p d -> (s p) d"),
                                                    bass.IndirectOffsetOnAxis(ap=pos[:, k, t:t + 1], axis=0),
                                                    XN[:, t, :], None).then_inc(scattered, 16)
                elif kind == "gather":
                    for n in range(3):
                        pool.wait_ge(y_out[n], 16 * len(range(n, SLOTS, 3)))
                    for i in range(NB):
                        for t in range(tiles(i).start, tiles(i).stop):
                            for k in range(TOPK):
                                pool.indirect_dma_start(yk[k][:, t, :], None,
                                                        slot_out.rearrange("s p d -> (s p) d"),
                                                        bass.IndirectOffsetOnAxis(ap=pos[:, k, t:t + 1], axis=0))\
                                    .then_inc(gathered[i], 16)

        @block.scalar
        def _(act):
            steps = 0

            def link(ins):
                nonlocal steps
                steps += 1
                ins.then_inc(act_step, 1)
                act.wait_ge(act_step, steps)

            act.dma_start(col[:, :], cols).then_inc(col_in, 16)
            act.dma_start(row[:, :], rows.partition_broadcast(P)).then_inc(row_in, 16)
            act.dma_start(wh[:, :], pack_h).then_inc(wh_in, 16)
            act.wait_ge(col_in, 16)
            act.activation(neg_a[:, :, :], col[:, C_ALOG:C_END].rearrange("p (h n) -> p h n", h=HV), ACT.Exp)\
                .then_inc(a_ready, 1)

            for item in order:
                kind = item[0]
                taken = emptied["act"]
                if kind == "stats":
                    _, l, i = item
                    act.wait_ge(var_ready, l * NB + i + 1)
                    act.activation(sdev[:, tiles(i)], veps[:, tiles(i)], ACT.Sqrt).then_inc(sd_ready, 1)
                elif kind == "xt":
                    _, l, i = item
                    wait_filled(act, item)
                    if l == 0:
                        act.activation(XNT[:, tokens(i)], bank(item)[:, :], ACT.Copy).then_inc(taken, 1)
                    else:
                        if i:
                            wait_filled(act, ("gate1", i - 1, 1))
                        act.activation(XNT1[:, :], bank(item)[:, :], ACT.Copy).then_inc(taken, 1)
                elif kind == "base":
                    i = item[1]
                    wait_filled(act, item)
                    if i:
                        wait_filled(act, ("score", i - 1, TB - 1))
                    act.activation(base[:, :], bank(item)[:, :], ACT.Silu, bias=col[:, C_BB:C_BB + 1])\
                        .then_inc(taken, 1)
                elif kind == "u0":
                    _, i, h = item
                    wait_filled(act, item)
                    if i:
                        wait_filled(act, ("wout", i - 1))
                    act.activation(uT[:, h, :], bank(item)[:, :], ACT.Silu, bias=col[:, C_BU + h:C_BU + h + 1])\
                        .then_inc(taken, 1)
                elif kind == "sh_gate":
                    i = item[1]
                    wait_filled(act, item)
                    if i:
                        wait_filled(act, ("sh_out", i - 1))
                    act.activation(sh_h[:, :], bank(item)[:, :], ACT.Silu).then_inc(taken, 1)
                elif kind == "v0":
                    _, i, j = item
                    wait_emptied(act, item)
                    act.activation(v[:, 2 * j:2 * j + 2, :], v[:, 2 * j:2 * j + 2, :], ACT.Silu).then_inc(v_ready, 1)
                elif kind == "score":
                    _, i, m = item
                    wait_filled(act, item)
                    if i:
                        wait_filled(act, ("attn", i - 1, 1))
                    act.activation(sq[:, m, :], bank(item)[:, :], ACT.Relu, scale=1.0 / S).then_inc(taken, 1)
                elif kind == "sh_out":
                    i = item[1]
                    wait_filled(act, item)
                    if i:
                        act.wait_ge(x1_done, i)
                    act.activation(g0[:, :, :], bank(item)[:, :].rearrange("p (t d) -> p t d", t=TB), ACT.Silu)\
                        .then_inc(taken, 1)
                elif kind in ("route0_soft", "route1_soft"):
                    l = int(kind[5])
                    act.wait_ge(soft_in, l + 1)
                    act.activation(sc[:, :, :], lg[:, l], ACT.Exp).then_inc(soft_exp, 1)
                elif kind == "oct":
                    q = item[1]
                    wait_filled(act, item)
                    act.activation(pairT[:, q * S:(q + 1) * S], bank(item)[:, :], ACT.Copy).then_inc(taken, 1)
                elif kind == "pair_act":
                    n = item[1]
                    wait_emptied(act, ("pair_h", (n + 1) * NT // 4 - 1))
                    if n:
                        act.wait_ge(pair_out, n)
                    act.activation(gate0, ph[:, :, 0:HID0], ACT.Silu).then_inc(pair_sig, 1)
                elif kind == "u1":
                    _, i, h = item
                    wait_filled(act, item)
                    if i:
                        act.wait_ge(conv_ready, 2 * (i - 1) + h + 1)
                    act.activation(upad[:, h, TAPS - 1:], bank(item)[:, :], ACT.Identity,
                                   bias=col[:, C_B1 + h:C_B1 + h + 1]).then_inc(taken, 1)
                elif kind == "gate1":
                    _, i, h = item
                    wait_filled(act, item)
                    if i >= 2:
                        act.wait_ge(y_ready, i - 1)
                    act.activation(g1[:, i % 2, h, :], bank(item)[:, :], ACT.Sigmoid,
                                   bias=col[:, C_B2 + h:C_B2 + h + 1]).then_inc(taken, 1)
                elif kind == "u1_sig":
                    i = item[1]
                    act.wait_ge(conv_ready, 2 * i + 2)
                    act.activation(u1[:, i % 2], u1[:, i % 2], ACT.Sigmoid).then_inc(u1_ready, 1)
                elif kind == "xproj":
                    i = item[1]
                    wait_filled(act, item)
                    if i:
                        wait_filled(act, ("dt", i - 1, 1))
                        act.wait_ge(bcs_ready, i)
                    act.activation(dtT[:, :], bank(item)[0:RANK, :], ACT.Copy)
                    act.activation(bc[:, :], bank(item)[RANK:RANK + 2 * NS, :], ACT.Copy).then_inc(taken, 1)
                elif kind == "dt":
                    _, i, h = item
                    wait_filled(act, item)
                    act.activation(delta[:, i % 2, h, :], bank(item)[:, :], ACT.Identity,
                                   bias=col[:, C_DTB + h:C_DTB + h + 1]).then_inc(taken, 1)
                elif kind == "softplus":
                    i = item[1]
                    act.preload_act_table_set("natural_log_exp_and_others")
                    act.wait_ge(na_ready, i + 1)
                    link(act.activation(du[:, i % 2], du[:, i % 2], ACT.Exp))
                    act.activation(du[:, i % 2], du[:, i % 2], ACT.Ln, bias=1.0).then_inc(l_ready, 1)
                elif kind == "scan":
                    _, i, s = item
                    if s < NS:
                        g = step_no(i, s)
                        if s == 0:
                            act.wait_ge(du_ready, i + 1)
                        if g >= N_DA:
                            act.wait_ge(state_ready, g - N_DA + 1)
                        if g == 0:
                            act.wait_ge(a_negated, 1)
                        for h in range(HV):
                            ins = act.activation(decay[:, g % N_DA, h, 1:S], delta[:, i % 2, h, 1:S], ACT.Exp,
                                                 scale=neg_a[:, h, s:s + 1])
                        ins.then_inc(decay_ready, 1)
                        act.wait_ge(c_cast, g + 1)
                        if g >= N_CS:
                            act.wait_ge(prod_ready, g - N_CS + 1)
                        act.activation(cs[:, g % N_CS, :], p_c[:, :], ACT.Copy).then_inc(cs_ready, 1)
                elif kind == "slot_h":
                    m = item[1]
                    wait_filled(act, item)
                    if m >= 2:
                        wait_filled(act, ("slot_y", m - 2))
                    for c in range(HC):
                        ins = act.activation(hT[m % 2][:, c, :], bank(item)[:, c * P:(c + 1) * P], ACT.Relu,
                                             bias=wst[m % N_W][:, X_B1 + c:X_B1 + c + 1])
                    ins.then_inc(taken, 1)
                elif kind == "combine":
                    i = item[1]
                    act.wait_ge(mix_ready, i + 1)
                    act.activation(yk[0][:, tiles(i), :], yk[0][:, tiles(i), :], ACT.Silu).then_inc(mix_silu, 1)

        @block.tensor
        def _(pe):
            pe.wait_ge(const_made, 1)

            for item in order:
                kind = item[0]
                if kind in CONSUMER:
                    n = job_at[item]
                    if n >= BANKS:
                        wait_emptied(pe, jobs[n - BANKS])
                    dst = bank(item)
                if kind == "xt":
                    _, l, i = item
                    pe.wait_ge(xn_ready, l * NB + i + 1)
                    for t in range(TB):
                        ins = pe.transpose(dst[:, t * P:(t + 1) * P], XN[:, tiles(i).start + t, :], ident[:, :])
                    ins.then_inc(filled, 1)
                elif kind == "logits":
                    _, l, i = item
                    wait_emptied(pe, ("xt", l, i))
                    if (l, i) == (0, 0):
                        pe.wait_ge(wa_in, 16)
                    wg = wa[:, A_GATE1:A_END] if l else wa[:, A_GATE0:A_GATE1]
                    for t in range(TB):
                        lhs = XNT1[:, t * P:(t + 1) * P] if l else \
                            XNT[:, tokens(i).start + t * P:tokens(i).start + (t + 1) * P]
                        ins = pe.matmul(dst[:, t * E:(t + 1) * E], lhs, wg, start=True, stop=True)
                    ins.then_inc(filled, 1)
                elif kind in ("base", "u0", "sh_gate", "sh_up"):
                    i = item[1]
                    at_col = {"base": A_UV + 2 * GE, "u0": A_UV + P * item[-1], "sh_gate": A_SW1, "sh_up": A_SW3}[kind]
                    pe.matmul(dst[:, :], wa[:, at_col:at_col + P], XNT[:, tokens(i)], start=True, stop=True)\
                        .then_inc(filled, 1)
                elif kind == "v0":
                    _, i, j = item
                    for t in range(2):
                        tok = tokens(i).start + (2 * j + t) * P
                        ins = pe.matmul(dst[:, t * GE:(t + 1) * GE], XNT[:, tok:tok + P], wa[:, A_UV + GE:A_UV + 2 * GE],
                                        start=True, stop=True)
                    ins.then_inc(filled, 1)
                elif kind == "score":
                    _, i, m = item
                    pe.wait_ge(qk_ready, i + 1)
                    pe.matmul(dst[:, :], kT[:, m * P:(m + 1) * P], qT[:, :], start=True, stop=True)\
                        .then_inc(filled, 1)
                elif kind == "attn":
                    _, i, h = item
                    pe.wait_ge(v_ready, 2 * (i + 1))
                    for m in range(TB):
                        if h == 0:
                            pe.wait_ge(sq_ready, TB * i + m + 1)
                        ins = pe.matmul(dst[:, :], v[:, m, h * P:(h + 1) * P], sq[:, m, :],
                                        start=(m == 0), stop=(m == TB - 1))
                    ins.then_inc(filled, 1)
                elif kind == "wout":
                    i = item[1]
                    wait_emptied(pe, ("attn", i, 1))
                    for t in range(TB):
                        for h in range(2):
                            ins = pe.matmul(dst[:, t * D:(t + 1) * D], uT[:, h, t * P:(t + 1) * P],
                                            wa[:, A_WOUT + h * D:A_WOUT + (h + 1) * D], start=(h == 0), stop=(h == 1))
                    ins.then_inc(filled, 1)
                elif kind == "sh_out":
                    i = item[1]
                    wait_emptied(pe, ("sh_up", i))
                    if i == LAST:
                        wait_emptied(pe, ("pair_sum", 1))
                    for t in range(TB):
                        routed = i == LAST and t == 0
                        ins = pe.matmul(dst[:, t * D:(t + 1) * D], sh_h[:, t * P:(t + 1) * P],
                                        wa[:, A_SW2:A_SW2 + D], start=True, stop=not routed)
                        if routed:
                            for g in range(E):
                                ins = pe.matmul(dst[:, 0:D], htp[:, g, :], wh[:, H_W2 + g * D:H_W2 + (g + 1) * D],
                                                start=False, stop=(g == E - 1))
                    ins.then_inc(filled, 1)
                elif kind == "pair_in":
                    pe.wait_ge(wb_in, 16)
                    pe.wait_ge(wh_in, 16)
                    pe.wait_ge(xm_ready, 1)
                    for g in range(E):
                        ins = pe.matmul(dst[:, 0:P], xm[:, g * P:(g + 1) * P], wb[:, B_W13 + g * P:B_W13 + (g + 1) * P],
                                        start=(g == 0), stop=(g == E - 1))
                    ins.then_inc(filled, 1)
                elif kind == "count0":
                    pe.wait_ge(picked_ready, 1)
                    for t in range(NT):
                        ins = pe.matmul(dst[:, 0:E], ones[:, :], picked[:, t, :], start=(t == 0), stop=(t == NT - 1))
                    ins.then_inc(filled, 1)
                elif kind == "oct":
                    q = item[1]
                    pe.wait_ge(pair_ready, 1)
                    for t in range(4):
                        ins = pe.transpose(dst[:, t * P:(t + 1) * P],
                                           pair[:, 4 * q + t, :, :].rearrange("p k c -> p (k c)"), ident[:, :])
                    ins.then_inc(filled, 1)
                elif kind == "pair_h":
                    q = item[1]
                    wait_emptied(pe, ("oct", q // 2))
                    wait_emptied(pe, ("pair_in",))
                    for t in range(2):
                        tok = (2 * q + t) * P
                        ins = pe.matmul(dst[:, t * 2 * P:(t + 1) * 2 * P], pairT[:, tok:tok + P],
                                        ab[:, :, :].rearrange("p k c -> p (k c)"), start=True, stop=True)
                    ins.then_inc(filled, 1)
                elif kind == "pair_sum":
                    n = item[1]
                    pe.wait_ge(pair_out, n + 1)
                    for j in range(NT):
                        ins = pe.matmul(dst[0:HID0, 0:E * E], ph[:, j, HID0:2 * HID0],
                                        pair[:, n * NT // 2 + j // TOPK, j % TOPK, :],
                                        start=(j == 0), stop=(j == NT - 1))
                    ins.then_inc(filled, 1)
                elif kind in ("u1", "gate1"):
                    _, i, h = item
                    if kind == "u1":
                        wait_emptied(pe, ("xt", 1, i))
                        if i == 0:
                            pe.wait_ge(wb_in, 16)
                            pe.wait_ge(wh_in, 16)
                    at_col = (B_W1 if kind == "u1" else B_W2) + h * P
                    pe.matmul(dst[:, :], wb[:, at_col:at_col + P], XNT1[:, :], start=True, stop=True)\
                        .then_inc(filled, 1)
                elif kind == "xproj":
                    i = item[1]
                    pe.wait_ge(u1_ready, i + 1)
                    n_out = RANK + 2 * NS
                    for h in range(HV):
                        ins = pe.matmul(dst[0:n_out, :], wb[:, B_XP + h * n_out:B_XP + (h + 1) * n_out],
                                        u1[:, i % 2, h, :], start=(h == 0), stop=(h == HV - 1))
                    ins.then_inc(filled, 1)
                elif kind == "dt":
                    _, i, h = item
                    wait_emptied(pe, ("xproj", i))
                    pe.matmul(dst[:, :], wh[:, H_DT + h * P:H_DT + (h + 1) * P], dtT[:, :], start=True, stop=True)\
                        .then_inc(filled, 1)
                elif kind == "scan":
                    _, i, s = item
                    if s < NS:
                        g = step_no(i, s)
                        if g == 0:
                            pe.wait_ge(const_made, N_MADE)
                        if s == 0:
                            pe.wait_ge(bcs_ready, i + 1)
                        if g:
                            pe.wait_ge(drive_ready, g)
                        pe.matmul(p_b[:, :], pick_state[:, s:s + 1].broadcast_to([3 * 2 * NS, P]), bcs[:, i % 2, :], start=True, stop=True)\
                            .then_inc(b_cast, 1)
                        if g:
                            pe.wait_ge(cs_ready, g)
                        pe.matmul(p_c[:, :], pick_state[:, NS + s:NS + s + 1].broadcast_to([3 * 2 * NS, P]), bcs[:, i % 2, :], start=True, stop=True)\
                            .then_inc(c_cast, 1)
                    if s >= LAG:
                        n = s - LAG
                        g = step_no(i, n)
                        if n == 0 and i:
                            pe.wait_ge(y_read, i)
                        pe.wait_ge(prod_ready, g + 1)
                        for h in range(HV):
                            ins = pe.matmul(p_y[h][:, :], ident[:, :], prod[:, g % N_PR, h, :],
                                            start=(n == 0), stop=(n == NS - 1))
                        ins.then_inc(summed, 1)
                elif kind == "wo1":
                    i = item[1]
                    pe.wait_ge(y_ready, i + 1)
                    for t in range(TB):
                        for h in range(HV):
                            ins = pe.matmul(dst[:, t * D:(t + 1) * D], u1[:, i % 2, h, t * P:(t + 1) * P],
                                            wb[:, B_WO + h * D:B_WO + (h + 1) * D], start=(h == 0), stop=(h == HV - 1))
                    ins.then_inc(filled, 1)
                elif kind == "rank1":
                    pe.wait_ge(picked_ready, 2)
                    for back in range(NT):
                        tiles_before = padded[:, NT - 1 - back:2 * NT - 1 - back, :].rearrange("p t e -> p (t e)")
                        ins = pe.matmul(dst[:, 0:NT * E], ones[:, :] if back else upper[:, :], tiles_before,
                                        start=(back == 0), stop=(back == NT - 1))
                    ins.then_inc(filled, 1)
                elif kind == "count1":
                    for t in range(NT):
                        ins = pe.matmul(dst[:, 0:E], ones[:, :], picked[:, t, :], start=(t == 0), stop=(t == NT - 1))
                    ins.then_inc(filled, 1)
                elif kind == "slot_t":
                    m = item[1]
                    pe.wait_ge(xg_in[m % 3], 16 * (m // 3 + 1))
                    pe.transpose(dst[:, 0:P], xg[m % 3], ident[:, :]).then_inc(filled, 1)
                elif kind == "slot_h":
                    m = item[1]
                    pe.wait_ge(w_in[m % N_W], 16 * (m // N_W + 1))
                    wait_emptied(pe, ("slot_t", m))
                    for c in range(HC):
                        ins = pe.matmul(dst[:, c * P:(c + 1) * P], wst[m % N_W][:, X_W1 + c * P:X_W1 + (c + 1) * P],
                                        xgT[m % 2], start=True, stop=True)
                    ins.then_inc(filled, 1)
                elif kind == "slot_y":
                    m = item[1]
                    wait_emptied(pe, ("slot_h", m))
                    for c in range(HC):
                        ins = pe.matmul(dst[:, 0:D], hT[m % 2][:, c, :],
                                        wst[m % N_W][:, X_W2 + c * D:X_W2 + (c + 1) * D],
                                        start=(c == 0), stop=(c == HC - 1))
                    ins.then_inc(filled, 1)

        @block.vector
        def _(dve):
            steps = 0

            def link(ins):
                nonlocal steps
                steps += 1
                ins.then_inc(dve_step, 1)
                dve.wait_ge(dve_step, steps)

            def softmax(l):
                link(dve.tensor_reduce(red[:, :], lg[:, l], AX.X, ALU.max))
                dve.tensor_tensor(lg[:, l], lg[:, l], red[:, :].unsqueeze(2).broadcast_to([P, NT, E]), ALU.subtract)\
                    .then_inc(soft_in, 1)
                dve.wait_ge(soft_exp, l + 1)
                link(dve.tensor_reduce(red2[:, :], sc[:, :, :], AX.X, ALU.add))
                link(dve.reciprocal(red2[:, :], red2[:, :]))
                link(dve.tensor_tensor(sc[:, :, :], sc[:, :, :], red2[:, :].unsqueeze(2).broadcast_to([P, NT, E]),
                                       ALU.mult))

            def ranks(dst, of, n, before):
                a, b = cmp_a[:, :, 0:n, 0:n], cmp_b[:, :, 0:n, 0:n]
                vj = of.unsqueeze(2).broadcast_to([P, NT, n, n])
                vi = of.unsqueeze(3).broadcast_to([P, NT, n, n])
                dve.tensor_tensor(a, vj, vi, ALU.is_gt)
                link(dve.tensor_tensor(b, vj, vi, ALU.is_equal))
                link(dve.tensor_tensor(b, b, before[:, :, :].unsqueeze(1).broadcast_to([P, NT, n, n]), ALU.mult))
                link(dve.tensor_tensor(a, a, b, ALU.add))
                link(dve.tensor_reduce(dst, a, AX.X, ALU.add))

            def picks(l):
                for k in range(TOPK):
                    ins = dve.tensor_scalar(pick[:, :, k, :], rank[:, :, :], float(k), None, ALU.is_equal)
                link(ins)
                link(dve.tensor_tensor(tmp8[:, :, :, :], pick[:, :, :, :],
                                       sc[:, :, :].unsqueeze(2).broadcast_to([P, NT, TOPK, E]), ALU.mult))
                link(dve.tensor_reduce(wgt[:, :, :], tmp8[:, :, :, :], AX.X, ALU.add))
                dve.tensor_tensor(picked[:, :, :], pick[:, :, 0, :], pick[:, :, 1, :], ALU.add)\
                    .then_inc(picked_ready, 1)

            dve.wait_ge(a_ready, 1)
            dve.tensor_scalar(neg_a[:, :, :], neg_a[:, :, :], -1.0, None, ALU.mult).then_inc(a_negated, 1)

            for item in order:
                kind = item[0]
                taken = emptied["dve"]
                if kind == "stats":
                    _, l, i = item
                    if l == 0:
                        dve.wait_ge(x_in[i], 16)
                    for t in range(TB):
                        ins = dve.bn_stats(stat[:, t, :], X[:, tiles(i).start + t, :])
                    link(ins)
                    for t in range(TB):
                        ins = dve.bn_aggr(mv[:, tiles(i).start + t, :], stat[:, t, :])
                    link(ins)
                    dve.tensor_scalar(veps[:, tiles(i)], mv[:, tiles(i), 1], EPS, None, ALU.add).then_inc(var_ready, 1)
                elif kind == "norm":
                    _, l, i = item
                    dve.wait_ge(sd_ready, l * NB + i + 1)
                    link(dve.reciprocal(rstd[:, tiles(i)], sdev[:, tiles(i)]))
                    for t in range(tiles(i).start, tiles(i).stop):
                        ins = dve.tensor_scalar(XN[:, t, :], X[:, t, :], mv[:, t, 0:1], rstd[:, t:t + 1],
                                                ALU.subtract, ALU.mult)
                    ins.then_inc(xn_ready, 1)
                elif kind == "logits":
                    _, l, i = item
                    wait_filled(dve, item)
                    src = bank(item)[:, 0:TB * E].rearrange("p (t e) -> p t e", t=TB)
                    if l == 0:
                        dve.tensor_copy(lg[:, 0, tiles(i), :], src).then_inc(taken, 1)
                    else:
                        dve.tensor_tensor(lg[:, 1, tiles(i), :], src,
                                          row[:, R_GB:R_END].unsqueeze(1).broadcast_to([P, TB, E]), ALU.add)\
                            .then_inc(taken, 1)
                elif kind == "base":
                    i = item[1]
                    wait_emptied(dve, item)
                    for n, t in enumerate((qT, kT)):
                        ins = dve.tensor_scalar(t[:, :], base[:, :], col[:, C_GAM + n:C_GAM + n + 1],
                                                col[:, C_BET + n:C_BET + n + 1], ALU.mult, ALU.add)
                    ins.then_inc(qk_ready, 1)
                elif kind == "sh_up":
                    i = item[1]
                    wait_filled(dve, item)
                    wait_emptied(dve, ("sh_gate", i))
                    dve.tensor_tensor(sh_h[:, :], sh_h[:, :], bank(item)[:, :], ALU.mult).then_inc(taken, 1)
                elif kind == "v0":
                    _, i, j = item
                    wait_filled(dve, item)
                    if i == 0 and j == 0:
                        dve.wait_ge(row_in, 16)
                    if i:
                        wait_filled(dve, ("attn", i - 1, 1))
                    dve.tensor_tensor(v[:, 2 * j:2 * j + 2, :], bank(item)[:, :].rearrange("p (t e) -> p t e", t=2),
                                      row[:, R_BV:R_BV + GE].unsqueeze(1).broadcast_to([P, 2, GE]), ALU.add)\
                        .then_inc(taken, 1)
                elif kind == "score":
                    _, i, m = item
                    wait_emptied(dve, item)
                    dve.tensor_tensor(sq[:, m, :], sq[:, m, :], sq[:, m, :], ALU.mult).then_inc(sq_ready, 1)
                elif kind == "attn":
                    _, i, h = item
                    wait_filled(dve, item)
                    dve.tensor_tensor(uT[:, h, :], uT[:, h, :], bank(item)[:, :], ALU.mult).then_inc(taken, 1)
                elif kind == "wout":
                    wait_filled(dve, item)
                    dve.tensor_tensor(s0[:, :, :], bank(item)[:, :].rearrange("p (t d) -> p t d", t=TB),
                                      row[:, R_BOUT:R_BOUT + D].unsqueeze(1).broadcast_to([P, TB, D]), ALU.add)\
                        .then_inc(taken, 1)
                elif kind == "x1":
                    i = item[1]
                    wait_emptied(dve, ("sh_out", i))
                    wait_emptied(dve, ("wout", i))
                    link(dve.tensor_tensor(s0[:, :, :], s0[:, :, :], g0[:, :, :], ALU.mult))
                    dve.tensor_tensor(X[:, tiles(i), :], X[:, tiles(i), :], s0[:, :, :], ALU.add).then_inc(x1_done, 1)
                    dve.wait_ge(x1_done, i + 1)
                elif kind == "route0_soft":
                    wait_emptied(dve, ("logits", 0, LAST))
                    softmax(0)
                    link(dve.tensor_tensor(sel_s[:, :, :], sc[:, :, :],
                                           row[:, R_EB:R_EB + E].unsqueeze(1).broadcast_to([P, NT, E]), ALU.add))
                elif kind == "route0_group":
                    link(dve.tensor_tensor(grp[:, :, :], sel_s[:, :, 0:E:2], sel_s[:, :, 1:E:2], ALU.add))
                    dve.wait_ge(const_made, N_MADE)
                    ranks(keep[:, :, :], grp[:, :, :], GROUPS, before4)
                    link(dve.tensor_scalar(keep[:, :, :], keep[:, :, :], 2.0, None, ALU.is_lt))
                    link(dve.tensor_scalar(grp[:, :, :], keep[:, :, :], BIG, -BIG, ALU.mult, ALU.add))
                    pairs = sel_s[:, :, :].rearrange("p t (g c) -> p t g c", c=2)
                    link(dve.tensor_tensor(pairs, pairs, keep[:, :, :].unsqueeze(3).broadcast_to([P, NT, GROUPS, 2]),
                                           ALU.mult))
                    link(dve.tensor_tensor(pairs, pairs, grp[:, :, :].unsqueeze(3).broadcast_to([P, NT, GROUPS, 2]),
                                           ALU.add))
                elif kind == "route0_rank":
                    ranks(rank[:, :, :], sel_s[:, :, :], E, before8)
                elif kind == "route0_pick":
                    picks(0)
                    dve.wait_ge(const_set, N_SET)
                    wait_emptied(dve, ("xt", 0, LAST))
                    spread_x = xm.rearrange("p (g r) -> p g r", r=P + 1)[:, :, 0:P]
                    for k in range(TOPK):
                        ins = dve.tensor_copy(spread_x[:, :, k * E * E:(k + 1) * E * E:E],
                                              XNT[:, 0:E].unsqueeze(1).broadcast_to([P, E, E]))
                    ins.then_inc(xm_ready, 1)
                elif kind == "count0":
                    wait_filled(dve, item)
                    dve.tensor_copy(cnt[:, :], bank(item)[:, 0:E]).then_inc(taken, 1)
                elif kind == "route0_pairs":
                    wait_emptied(dve, ("count0",))
                    dve.memset(cum[:, 0:1], 0.0)
                    link(dve.tensor_tensor_scan(cum[:, 1:E + 1], cnt[:, :], cnt[:, :], 0.0, ALU.add, ALU.bypass))
                    link(dve.tensor_tensor(ge[:, :, :],
                                           row_no[:, :, :].rearrange("p t k -> p (t k)").unsqueeze(2)
                                           .broadcast_to([P, NT * TOPK, E + 1]),
                                           cum[:, :].unsqueeze(1).broadcast_to([P, NT * TOPK, E + 1]), ALU.is_ge))
                    link(dve.tensor_tensor(seg[:, :, :], ge[:, :, 0:E], ge[:, :, 1:E + 1], ALU.subtract))
                    dve.wait_ge(slots_zeroed, 16)
                    dve.tensor_tensor(
                        pair.rearrange("p t k (e g) -> p (t k) e g", e=E),
                        pick[:, :, :, :].rearrange("p t k e -> p (t k) e").unsqueeze(3)
                        .broadcast_to([P, NT * TOPK, E, E]),
                        seg[:, :, :].unsqueeze(2).broadcast_to([P, NT * TOPK, E, E]), ALU.mult)\
                        .then_inc(pair_ready, 1)
                elif kind == "pair_in":
                    wait_filled(dve, item)
                    half = E * E
                    dve.tensor_copy(ab[0:half, 0, :], bank(item)[0:half, 0:P])
                    dve.tensor_copy(ab[half:2 * half, 1, :], bank(item)[half:2 * half, 0:P]).then_inc(taken, 1)
                elif kind == "pair_h":
                    q = item[1]
                    wait_filled(dve, item)
                    w = wgt[:, 2 * q:2 * q + 2, :].rearrange("p t k -> p (t k)").unsqueeze(2)
                    if q == NT // 4:
                        wait_filled(dve, ("pair_sum", 0))
                    j = 4 * q % NT
                    dve.tensor_tensor(ph[:, j:j + 4, :], bank(item)[:, :].rearrange("p (j c) -> p j c", j=4),
                                      w.broadcast_to([P, 4, 2 * HID0]), ALU.mult).then_inc(taken, 1)
                elif kind == "pair_act":
                    dve.wait_ge(pair_sig, item[1] + 1)
                    dve.tensor_tensor(ph[:, :, HID0:2 * HID0], ph[:, :, HID0:2 * HID0], gate0, ALU.mult)\
                        .then_inc(pair_out, 1)
                elif kind == "pair_sum":
                    n = item[1]
                    wait_filled(dve, item)
                    sums = bank(item)[0:HID0, 0:E * E].rearrange("p (e g) -> p g e", e=E)
                    if n == 0:
                        link(dve.memset(htp, 0.0))
                        dve.tensor_copy(htp[:, :, 0:E], sums).then_inc(taken, 1)
                    else:
                        wait_emptied(dve, ("pair_sum", 0))
                        dve.tensor_tensor(htp[:, :, 0:E], htp[:, :, 0:E], sums, ALU.add).then_inc(taken, 1)
                elif kind == "u1":
                    _, i, h = item
                    wait_emptied(dve, item)
                    if i >= 2:
                        wait_filled(dve, ("wo1", i - 2))
                    if i == 0:
                        dve.wait_ge(const_set, N_SET)
                    dst = u1[:, i % 2, h, :]

                    def tap(k):
                        return col[:, C_CW + TAPS * h + k:C_CW + TAPS * h + k + 1]
                    link(dve.tensor_scalar(dst, upad[:, h, TAPS - 1:TAPS - 1 + S], tap(TAPS - 1),
                                           col[:, C_CB + h:C_CB + h + 1], ALU.mult, ALU.add))
                    for k in range(TAPS - 1):
                        ins = dve.scalar_tensor_tensor(dst, upad[:, h, k:k + S], tap(k), dst, ALU.mult, ALU.add)
                        if k < TAPS - 2:
                            link(ins)
                    ins.then_inc(conv_ready, 1)
                elif kind == "xproj":
                    i = item[1]
                    wait_emptied(dve, item)
                    if i >= 2:
                        dve.wait_ge(c_cast, step_no(i - 2, NS - 1) + 1)
                    n = 2 * NS
                    hi = bcs[0:n, i % 2, :]
                    link(dve.tensor_copy(hi, bc[:, :]))
                    link(dve.tensor_tensor(bc_res, bc[:, :], hi, ALU.subtract))
                    link(dve.tensor_copy(bc_mid[:, :], bc_res))
                    dve.tensor_copy(bcs[n:2 * n, i % 2, :], bc_mid[:, :])
                    dve.tensor_tensor(bcs[2 * n:3 * n, i % 2, :], bc_res, bc_mid[:, :], ALU.subtract)\
                        .then_inc(bcs_ready, 1)
                elif kind == "softplus":
                    i = item[1]
                    wait_emptied(dve, ("dt", i, 1))
                    z, l, uu = delta[:, i % 2], du[:, i % 2], u1[:, i % 2]
                    dve.scalar_tensor_tensor(l, z, -1.0, z, ALU.mult, ALU.min).then_inc(na_ready, 1)
                    dve.wait_ge(l_ready, i + 1)
                    link(dve.scalar_tensor_tensor(z, z, 0.0, l, ALU.max, ALU.add))
                    dve.wait_ge(u1_ready, i + 1)
                    dve.tensor_tensor(l, z, uu, ALU.mult).then_inc(du_ready, 1)
                    dve.wait_ge(du_ready, i + 1)
                elif kind == "scan":
                    _, i, s = item
                    if s < NS:
                        g = step_no(i, s)
                        dve.wait_ge(b_cast, g + 1)
                        if g >= N_DBU:
                            dve.wait_ge(state_ready, g - N_DBU + 1)
                        dve.tensor_tensor(drive[:, g % N_DBU], du[:, i % 2],
                                          p_b[:, :].unsqueeze(1).broadcast_to([P, HV, S]), ALU.mult)\
                            .then_inc(drive_ready, 1)
                    if 1 <= s <= NS:
                        g = step_no(i, s - 1)
                        dve.wait_ge(decay_ready, g + 1)
                        dve.wait_ge(drive_ready, g + 1)
                        if g >= N_ST:
                            dve.wait_ge(prod_ready, g - N_ST + 1)
                        if g == 0:
                            dve.wait_ge(const_set, N_SET)
                        dve.tensor_tensor_scan(state[:, g % N_ST].rearrange("p h t -> p (h t)"),
                                               decay[:, g % N_DA].rearrange("p h t -> p (h t)"),
                                               drive[:, g % N_DBU].rearrange("p h t -> p (h t)"), 0.0,
                                               ALU.mult, ALU.add).then_inc(state_ready, 1)
                elif kind == "scan_out":
                    i = item[1]
                    dve.wait_ge(summed, (i + 1) * NS)
                    for h in range(HV):
                        ins = dve.scalar_tensor_tensor(u1[:, i % 2, h, :], u1[:, i % 2, h, :],
                                                       col[:, C_D + h:C_D + h + 1], p_y[h][:, :], ALU.mult, ALU.add)
                    ins.then_inc(y_read, 1)
                    dve.wait_ge(y_read, i + 1)
                    wait_emptied(dve, ("gate1", i, 1))
                    dve.tensor_tensor(u1[:, i % 2], u1[:, i % 2], g1[:, i % 2], ALU.mult).then_inc(y_ready, 1)
                elif kind == "wo1":
                    i = item[1]
                    wait_filled(dve, item)
                    dve.tensor_tensor(s1[:, tiles(i), :], bank(item)[:, :].rearrange("p (t d) -> p t d", t=TB),
                                      row[:, R_BO:R_BO + D].unsqueeze(1).broadcast_to([P, TB, D]), ALU.add)\
                        .then_inc(taken, 1)
                elif kind == "route1_soft":
                    wait_emptied(dve, ("logits", 1, LAST))
                    softmax(1)
                elif kind == "route1_rank":
                    ranks(rank[:, :, :], sc[:, :, :], E, before8)
                    wait_filled(dve, ("count0",))
                    picks(1)
                elif kind == "rank1":
                    wait_filled(dve, item)
                    dve.tensor_copy(rank[:, :, :], bank(item)[:, 0:NT * E].rearrange("p (t e) -> p t e", t=NT))\
                        .then_inc(taken, 1)
                elif kind == "count1":
                    wait_filled(dve, item)
                    dve.tensor_copy(cnt[:, :], bank(item)[:, 0:E]).then_inc(taken, 1)
                    wait_emptied(dve, item)
                elif kind == "route1_slots":
                    link(dve.tensor_tensor(cmp_t, cnt[:, :].unsqueeze(2).broadcast_to([P, E, NT]),
                                           mult128[:, :].unsqueeze(1).broadcast_to([P, E, NT]), ALU.is_gt))
                    link(dve.tensor_reduce(ntile[:, :], cmp_t, AX.X, ALU.add))
                    link(dve.tensor_tensor_scan(ctile[:, :], ntile[:, :], ntile[:, :], 0.0, ALU.add, ALU.bypass))
                    link(dve.tensor_tensor(cmp_s, slot_no[:, :].unsqueeze(2).broadcast_to([P, SLOTS, E]),
                                           ctile[:, :].unsqueeze(1).broadcast_to([P, SLOTS, E]), ALU.is_ge))
                    link(dve.tensor_reduce(slot_f[:, :], cmp_s, AX.X, ALU.add))
                    dve.tensor_scalar(slot_e[:, :], slot_f[:, :], float(E - 1), None, ALU.min)
                    link(dve.tensor_tensor(first_row[:, :], ctile[:, :], ntile[:, :], ALU.subtract))
                    link(dve.tensor_scalar(first_row[:, :], first_row[:, :], float(P), None, ALU.mult))
                    link(dve.tensor_tensor(rank[:, :, :], rank[:, :, :],
                                           first_row[:, :].unsqueeze(1).broadcast_to([P, NT, E]), ALU.add))
                    link(dve.tensor_tensor(tmp8[:, :, :, :], pick[:, :, :, :],
                                           rank[:, :, :].unsqueeze(2).broadcast_to([P, NT, TOPK, E]), ALU.mult))
                    link(dve.tensor_reduce(pos_f[:, :, :], tmp8[:, :, :, :], AX.X, ALU.add))
                    dve.tensor_copy(pos[:, :, :], pos_f[:, :, :].rearrange("p t k -> p k t")).then_inc(pos_ready, 1)
                elif kind == "slot_t":
                    m = item[1]
                    wait_filled(dve, item)
                    if m >= 2:
                        wait_filled(dve, ("slot_h", m - 2))
                    dve.tensor_copy(xgT[m % 2], bank(item)[:, 0:P]).then_inc(taken, 1)
                elif kind == "slot_y":
                    m = item[1]
                    wait_filled(dve, item)
                    if m >= 3:
                        dve.wait_ge(y_out[m % 3], 16 * (m // 3))
                    dve.tensor_tensor(ysb[m % 3], bank(item)[:, 0:D], wst[m % N_W][:, X_B2:X_END], ALU.add)\
                        .then_inc(taken, 1)
                elif kind == "combine":
                    i = item[1]
                    dve.wait_ge(gathered[i], 16 * TB * TOPK)
                    for t in range(tiles(i).start, tiles(i).stop):
                        ins = dve.tensor_scalar(yk[0][:, t, :], yk[0][:, t, :], wgt[:, t, 0:1], None, ALU.mult)
                    link(ins)
                    for t in range(tiles(i).start, tiles(i).stop):
                        ins = dve.scalar_tensor_tensor(yk[0][:, t, :], yk[1][:, t, :], wgt[:, t, 1:2], yk[0][:, t, :],
                                                       ALU.mult, ALU.add)
                    ins.then_inc(mix_ready, 1)
                    dve.wait_ge(mix_silu, i + 1)
                    wait_emptied(dve, ("wo1", i))
                    link(dve.tensor_tensor(s1[:, tiles(i), :], s1[:, tiles(i), :], yk[0][:, tiles(i), :], ALU.mult))
                    dve.tensor_tensor(X[:, tiles(i), :], X[:, tiles(i), :], s1[:, tiles(i), :], ALU.add)\
                        .then_inc(out_ready, 1)


def _host_layout(inputs):
    import numpy as np

    a = {k: np.asarray(v) for k, v in inputs.items()}

    def cat(*parts):
        return np.ascontiguousarray(np.concatenate(parts, axis=1))

    def chunks(w):
        c = w.shape[0] // P
        return w.reshape(c, P, -1).transpose(1, 0, 2).reshape(P, -1)

    def per_partition(v):
        return v.reshape(-1, P).T

    pack_a = cat(a["L0_attn_W_uv"], a["L0_ffn_sw1"].T, a["L0_ffn_sw3"].T, a["L0_ffn_sw2"].T,
                 chunks(a["L0_attn_W_out"]), a["L0_ffn_w_gate"].T, a["L1_ffn_gate_w"])
    w13 = np.concatenate([a["L0_ffn_w1"], a["L0_ffn_w3"]], axis=2).transpose(1, 0, 2).reshape(D, -1)
    pack_b = cat(w13, a["L1_attn_W1"], a["L1_attn_W2"], chunks(a["L1_attn_x_proj_w"]), chunks(a["L1_attn_Wo"]))
    pack_h = cat(a["L0_ffn_w2"].transpose(1, 0, 2).reshape(HID0, -1), a["L1_attn_dt_proj_w"])
    b_uv = a["L0_attn_b_uv"]
    cols = cat(per_partition(b_uv[0:GE]), per_partition(b_uv[2 * GE:]), a["L0_attn_gamma"].T, a["L0_attn_beta"].T,
               per_partition(a["L1_attn_b1"]), per_partition(a["L1_attn_b2"]), chunks(a["L1_attn_conv_w"]),
               per_partition(a["L1_attn_conv_b"]), per_partition(a["L1_attn_dt_proj_b"]),
               per_partition(a["L1_attn_D_skip"]), chunks(a["L1_attn_A_log"]))
    rows = np.ascontiguousarray(np.concatenate(
        [b_uv[GE:2 * GE], a["L0_attn_b_out"], a["L0_ffn_expert_bias"], a["L1_attn_bo"], a["L1_ffn_gate_b"]]))
    experts = np.ascontiguousarray(np.concatenate([
        a["L1_ffn_w1"],
        a["L1_ffn_w2"].reshape(E, HC, P, D).transpose(0, 2, 1, 3).reshape(E, P, HC * D),
        a["L1_ffn_b1"].reshape(E, HC, P).transpose(0, 2, 1),
        np.broadcast_to(a["L1_ffn_b2"][:, None, :], (E, P, D))], axis=2))
    x = np.ascontiguousarray(a["L0_attn_inputs"])
    return {"x": x, "pack_a": pack_a, "pack_b": pack_b, "pack_h": pack_h, "cols": cols, "rows": rows,
            "experts": experts}


def kernel(**inputs):
    import concourse.bacc as _bacc
    from concourse.bass_utils import run_bass_kernel_spmd as _run

    nc = _bacc.Bacc("TRN2", target_bir_lowering=False, num_devices=1)
    arrays = _host_layout(inputs)
    args = {n: nc.dram_tensor(n, v.shape, mybir.dt.from_np(v.dtype), kind="ExternalInput").ap()
            for n, v in arrays.items()}
    out = nc.dram_tensor("out", (NB, S, D), F32, kind="ExternalOutput").ap()
    slot_in = nc.dram_tensor("slot_in", (SLOTS, P, D), F32, kind="Internal").ap()
    slot_out = nc.dram_tensor("slot_out", (SLOTS, P, D), F32, kind="Internal").ap()
    build(nc, args["x"], args["pack_a"], args["pack_b"], args["pack_h"], args["cols"], args["rows"],
          args["experts"], out, slot_in, slot_out)
    r = _run(nc, [arrays], core_ids=[0])
    return r.results[0]["out"]
```

```python
from contextlib import ExitStack

import concourse.bass as bass
from concourse import mybir

ALU = mybir.AluOpType
ACT = mybir.ActivationFunctionType
AX = mybir.AxisListType
F32 = mybir.dt.float32
BF16 = mybir.dt.bfloat16
I32 = mybir.dt.int32

P = 128
NB = 4
S = 512
D = 128
TB = S // P
NT = NB * TB
E = 8
TOPK = 2
GROUPS = 4
GE = 256
HID0 = 64
MLP = 256
HV = MLP // P
NS = 16
RANK = 64
TAPS = 4
HID1 = 512
HC = HID1 // P
NG = 2
GT = NT // NG
SLOTS = GT * TOPK + E - 1
EPS = 1e-5
BIG = 1e30

BATCHES = [2, 3, 1, 0]
LAST = NB - 1
PAIRED = {2, 3}
LAG = 3

A_UV, A_SW1, A_SW3, A_SW2, A_WOUT, A_GATE0, A_GATE1, A_END = (
    0, 640, 768, 896, 1024, 1280, 1288, 1296)
B_W13, B_W1, B_W2, B_XP, B_WO, B_END = 0, 1024, 1280, 1536, 1728, 1984
H_W2, H_DT, H_END = 0, E * D, E * D + MLP
C_BU, C_BB, C_GAM, C_BET, C_B1, C_B2, C_CW, C_CB, C_DTB, C_D, C_ALOG, C_END = (
    0, 2, 3, 5, 7, 9, 11, 19, 21, 23, 25, 57)
R_BV, R_BOUT, R_EB, R_BO, R_GB, R_END = 0, 256, 384, 392, 520, 528
X_W1, X_W2, X_B1, X_B2, X_END = 0, 512, 1024, 1028, 1156


PE_COST = {
    "xt": 0.5, "logits": 1, "base": 1, "u0": 1, "sh_gate": 1, "sh_up": 1, "v0": 1, "sh_out": 1, "score": 1,
    "attn": 4, "wout": 2, "pair_in": 2, "oct": 0.5, "pair_h": 1, "pair_sum": 3, "u1": 1, "gate1": 1, "xproj": 2,
    "dt": 1, "wo1": 2, "rank1": 1, "count1": 1, "count0": 1, "slot_t": 0.2, "slot_h": 1, "slot_y": 1,
}


def build_order():

    def project(i):
        return [[("base", i), ("u0", i, 0), ("u0", i, 1), ("sh_gate", i), ("sh_up", i), ("v0", i, 0), ("v0", i, 1)]
                + ([("sh_out", i)] if i != LAST else [])]

    def attend(i):
        return ([("score", i, m) for m in range(TB)] + [("attn", i, 0), ("attn", i, 1), ("wout", i)]
                + ([("x1", i)] if i != LAST else []))

    def project1(i):
        return [("stats", 1, i), ("norm", 1, i), ("xt", 1, i), ("logits", 1, i),
                [("u1", i, 0), ("u1", i, 1), ("gate1", i, 0), ("gate1", i, 1), ("u1_sig", i)]]

    def steps1(i):
        return [("xproj", i), ("dt", i, 0), ("dt", i, 1), ("softplus", i)]

    def scan(i):
        return [("scan", i, s) for s in range(NS + LAG)] + [("scan_out", i), ("wo1", i)]

    def slots(g):
        first, end = g * SLOTS, (g + 1) * SLOTS
        out = [("open", g)]
        for m in range(first, end + 2):
            out += [("slot_t", m)] if m < end else []
            out += [("slot_h", m - 1)] if first <= m - 1 < end else []
            out += [("slot_y", m - 2)] if first <= m - 2 < end else []
        return out

    def route1(g):
        return ([("soft_a", 1, g), ("soft_b", 1, g)] + [("rank", 1, g, n) for n in range(5)]
                + [("pick", 1, g, n) for n in range(2)] + [("rank1", g), ("count1", g)]
                + [("route1_slots", g, n) for n in range(2)])

    def spread(main, extra):
        cost = [sum(PE_COST.get(x[0], 0.3) for x in (item if isinstance(item, list) else [item])) for item in main]
        out, done, at = [], 0, 0
        for item, c in zip(main, cost):
            out += item if isinstance(item, list) else [item]
            at += c
            want = round(at * len(extra) / sum(cost))
            out += extra[done:want]
            done = want
        return out

    order = [("stats", 0, 0), ("norm", 0, 0), ("xt", 0, 0), ("stats", 0, 1), ("stats", 0, 2), ("stats", 0, 3),
             ("norm", 0, 1), ("norm", 0, 2), ("norm", 0, 3)]
    order += spread(project(0), []) + [("xt", 0, 1), ("logits", 0, 0)] + attend(0)[:TB]
    order += [("xt", 0, 2), ("xt", 0, 3)] + attend(0)[TB:]
    order += spread(project(1), []) + [("stats", 1, 0), ("logits", 0, 1), ("logits", 0, 2), ("norm", 1, 0)]
    order += [("score", 1, 0), ("score", 1, 1), ("logits", 0, 3)] + spread(project1(0)[2:], [])
    order += attend(1)[2:TB + 2] + steps1(0) + [("soft_a", 0, 0)] + attend(1)[TB + 2:]

    route0 = ([("soft_b", 0, 0)] + [("group", n) for n in range(3)] + [("rank", 0, 0, n) for n in range(5)]
              + [("pick", 0, 0, n) for n in range(2)] + [("count0",), ("pairs", 0), ("pairs", 1)])
    routed = [("pair_in",)] + [("oct", q) for q in range(NT // 4)]
    for n in range(2):
        routed += [("pair_h", q) for q in range(n * NT // 4, (n + 1) * NT // 4)] + [("pair_act", n), ("pair_sum", n)]
    routed += [("sh_out", LAST), ("x1", LAST)]

    def mix(a, b):
        out, done = [], 0
        for n, item in enumerate(a):
            out.append(item)
            want = (n + 1) * len(b) // len(a)
            out += b[done:want]
            done = want
        return out

    order += spread(mix(project(2) + project1(1) + attend(2) + steps1(1), route0), scan(0))
    order += spread(project(3) + project1(2) + mix(attend(3) + routed, route1(0)) + steps1(2)
                    + [("scatter", 0, q) for q in range(4)], scan(1))
    tail2, tail3 = scan(2), scan(3)
    order += spread(project1(3)[:4] + mix(project1(3)[4:] + steps1(3) + slots(0)[:9], route1(1)) + slots(0)[9:30]
                    + mix(slots(0)[30:], [("scatter", 1, q) for q in range(4)]), tail2)
    order += spread(mix(slots(1), [("gather", 0, 0), ("gather", 1, 0), ("mix", 0), ("mix", 1), ("done", 0), ("done", 1)]),
                    tail3[:12])
    order += mix([("gather", 2, 0), ("gather", 3, 0), ("mix", 2), ("done", 2), ("mix", 3)], tail3[12:]) + [("done", 3)]
    return order


CONSUMER = {
    "xt": "act", "logits": "dve", "base": "act", "u0": "act", "sh_gate": "act", "sh_up": "dve", "v0": "dve",
    "score": "act", "attn": "dve", "wout": "dve", "sh_out": "act", "pair_in": "dve", "oct": "act",
    "pair_h": "dve", "pair_sum": "dve", "u1": "act", "gate1": "act", "xproj": "act", "dt": "act", "wo1": "dve",
    "rank1": "dve", "count0": "dve", "count1": "dve", "slot_t": "dve", "slot_h": "act", "slot_y": "dve",
}
BANKS = 4
N_SET, N_MADE = 14, 7


def build(nc, x, pack_a, pack_b, pack_h, cols, rows, experts, out, slot_in, slot_out):
    order = build_order()
    jobs = [item for item in order if item[0] in CONSUMER]
    job_at = {item: n for n, item in enumerate(jobs)}
    emptied_at, so_far = {}, {"act": 0, "dve": 0}
    for item in jobs:
        so_far[CONSUMER[item[0]]] += 1
        emptied_at[item] = so_far[CONSUMER[item[0]]]

    x_v = x.rearrange("b (t p) d -> p (b t) d", p=P)
    out_v = out.rearrange("b (t p) d -> p (b t) d", p=P)

    with ExitStack() as ctx:
        def sb(name, shape, dt=F32):
            return ctx.enter_context(nc.sbuf_tensor(name, shape, dt))

        def sem(name):
            return ctx.enter_context(nc.semaphore(name))

        wa = sb("wa", [P, A_END])
        wb = sb("wb", [P, B_END])
        wh = sb("wh", [HID0, H_END])
        col = sb("col", [P, C_END])
        row = sb("row", [P, R_END])
        ident = sb("ident", [P, P])
        pick_state = sb("pick_state", [3 * 2 * NS, 2 * NS], BF16)
        upper = sb("upper", [P, P], BF16)
        ones = sb("ones", [P, P], BF16)
        before4 = sb("before4", [P, GROUPS, GROUPS], BF16)
        before8 = sb("before8", [P, E, E], BF16)
        row_no = sb("row_no", [P, NT, TOPK])
        mult128 = sb("mult128", [P, GT])
        slot_no = sb("slot_no", [P, SLOTS])
        neg_a = sb("neg_a", [P, HV, NS])

        X = sb("X", [P, NT, D])
        XN = sb("XN", [P, NT, D])
        XNT = sb("XNT", [P, NT * P])
        XNT1 = sb("XNT1", [P, S])
        stat = sb("stat", [P, TB, 6])
        mv = sb("mv", [P, NT, 2])
        veps = sb("veps", [P, NT])
        sdev = sb("sdev", [P, NT])
        rstd = sb("rstd", [P, NT])

        early = sb("early", [P, 5 * S])
        base, qT, sh_h = (early[:, n * S:(n + 1) * S] for n in range(3))
        s0, g0 = (early[:, n * S:(n + 1) * S].rearrange("p (t d) -> p t d", t=TB) for n in (3, 4))
        kT = base
        uv = sb("uv", [P, 4 * S])
        uT = uv[:, 0:2 * S].rearrange("p (h t) -> p h t", h=2)
        v = uv[:, 2 * S:4 * S].rearrange("p (t e) -> p t e", t=TB)
        sq = sb("sq", [P, TB, S])

        upad = sb("upad", [P, HV, TAPS - 1 + S])
        u1 = sb("u1", [P, 2, HV, S])
        g1 = sb("g1", [P, 2, HV, S])
        dtT = sb("dtT", [RANK, S])
        bc = sb("bc", [2 * NS, S])
        bc_mid = sb("bc_mid", [2 * NS, S], BF16)
        bcs = sb("bcs", [3 * 2 * NS, 2, S], BF16)
        delta = sb("delta", [P, 2, HV, S])
        du = sb("du", [P, 2, HV, S])
        N_DA, N_DBU, N_ST, N_CS, N_PR = 3, 3, 2, 2, 4
        decay = sb("decay", [P, N_DA, HV, S])
        drive = sb("drive", [P, N_DBU, HV, S])
        state = sb("state", [P, N_ST, HV, S])
        cs = sb("cs", [P, N_CS, S])
        prod = sb("prod", [P, N_PR, HV, S])
        s1 = XNT[:, :].rearrange("p (t d) -> p t d", t=NT)

        lg = sb("lg", [P, 2, NT, E])
        sc = sb("sc", [P, NT, E])
        sel_s = sb("sel_s", [P, NT, E])
        red = sb("red", [P, NT])
        red2 = sb("red2", [P, NT])
        grp = sb("grp", [P, NT, GROUPS])
        keep = sb("keep", [P, NT, GROUPS])
        cmp_a = sb("cmp_a", [P, NT, E, E], BF16)
        cmp_b = sb("cmp_b", [P, NT, E, E], BF16)
        bc_res = cmp_b[0:2 * NS, :, :, :].rearrange("p t i j -> p (t i j)").bitcast(F32)
        rank = sb("rank", [P, NT, E])
        pick = sb("pick", [P, NT, TOPK, E])
        picked0 = sb("picked0", [P, NT, E], BF16)
        padded = sb("padded", [P, 2 * GT - 1, E], BF16)
        picked1 = padded[:, GT - 1:, :]
        tmp8 = sb("tmp8", [P, NT, TOPK, E])
        wgt = [sb(f"wgt{n}", [P, NT, TOPK]) for n in range(2)]
        cnt = sb("cnt", [P, E])
        cum = sb("cum", [P, E + 1])
        ge = sb("ge", [P, NT * TOPK, E + 1])
        seg = sb("seg", [P, NT * TOPK, E])
        ab = sb("ab", [P, TOPK, P])
        ntile = sb("ntile", [P, E])
        cmp_f = cmp_a[:, :, :, :].rearrange("p t i j -> p (t i j)").bitcast(F32)
        cmp_t = cmp_f[:, 0:E * GT].rearrange("p (e t) -> p e t", e=E)
        ctile = sb("ctile", [P, E])
        first_row = sb("first_row", [P, E])
        cmp_s = cmp_f[:, E * GT:E * GT + SLOTS * E].rearrange("p (s e) -> p s e", e=E)
        slot_f = sb("slot_f", [P, SLOTS])
        slot_e = sb("slot_e", [P, NG * SLOTS], I32)
        pos_f = sb("pos_f", [P, NT, TOPK])
        pos = sb("pos", [P, TOPK, NT], I32)

        PAIR = NT * TOPK * HID0
        N_W, N_X = 5, 7
        REGION = 3 * PAIR
        region = sb("region", [P, REGION])
        pair = region[:, 0:PAIR].rearrange("p (t k c) -> p t k c", t=NT, k=TOPK)
        pairT = region[:, PAIR:2 * PAIR]
        gate0 = region[:, PAIR:PAIR + PAIR // 2].rearrange("p (j c) -> p j c", c=HID0)
        ph = region[:, 2 * PAIR:3 * PAIR].rearrange("p (j c) -> p j c", c=2 * HID0)
        xm = region[:, 2 * PAIR:2 * PAIR + E * (P + 1)]
        htp = sq[0:HID0, 0:2, :].rearrange("p m t -> p (m t)").rearrange("p (g c) -> p g c", g=E)
        at = 0

        def part(n):
            nonlocal at
            at += n
            return region[:, at - n:at]

        wst = [early[:, n * X_END:(n + 1) * X_END] for n in range(2)] + [part(X_END) for _ in range(N_W - 2)]
        xg = [part(D) for _ in range(N_X)]
        xgT = [part(D) for _ in range(2)]
        hT = [part(HC * P).rearrange("p (c t) -> p c t", c=HC) for _ in range(2)]
        ysb = [part(D) for _ in range(3)]
        assert at <= REGION
        yk = [sq[:, :, :].rearrange("p m t -> p (m t)").rearrange("p (t d) -> p t d", t=NT),
              uv[:, :].rearrange("p (t d) -> p t d", t=NT)]

        work = [ctx.enter_context(nc.psum_tensor(f"work{n}", [P, S], F32)) for n in range(BANKS)]
        p_b = ctx.enter_context(nc.psum_tensor("p_b", [P, S], F32))
        p_c = ctx.enter_context(nc.psum_tensor("p_c", [P, S], F32))
        p_y = [ctx.enter_context(nc.psum_tensor(f"p_y{h}", [P, S], F32)) for h in range(HV)]

        x_in = [sem(f"x_in{i}") for i in range(NB)]
        wa_in, wb_in, wh_in, col_in, row_in = (sem(n) for n in ("wa_in", "wb_in", "wh_in", "col_in", "row_in"))
        const_set, const_made = sem("const_set"), sem("const_made")
        slots_zeroed = sem("slots_zeroed")
        a_ready, a_negated = sem("a_ready"), sem("a_negated")
        filled = sem("filled")
        emptied = {"act": sem("emptied_by_act"), "dve": sem("emptied_by_dve")}
        dve_step, act_step = sem("dve_step"), sem("act_step")
        var_ready, sd_ready, xn_ready = sem("var_ready"), sem("sd_ready"), sem("xn_ready")
        qk_ready, v_ready, sq_ready = sem("qk_ready"), sem("v_ready"), sem("sq_ready")
        x1_done = sem("x1_done")
        conv_ready, u1_ready = sem("conv_ready"), sem("u1_ready")
        bcs_ready = sem("bcs_ready")
        na_ready, l_ready, du_ready = sem("na_ready"), sem("l_ready"), sem("du_ready")
        b_cast, c_cast, cs_ready, decay_ready = sem("b_cast"), sem("c_cast"), sem("cs_ready"), sem("decay_ready")
        drive_ready, state_ready, prod_ready, summed = (
            sem("drive_ready"), sem("state_ready"), sem("prod_ready"), sem("summed"))
        y_read, y_ready = sem("y_read"), sem("y_ready")
        soft_in, soft_exp = sem("soft_in"), sem("soft_exp")
        picked_ready = sem("picked_ready")
        xm_ready, pair_ready = sem("xm_ready"), sem("pair_ready")
        pair_sig, pair_out = sem("pair_sig"), sem("pair_out")
        pos_ready = sem("pos_ready")
        paired = sem("paired")
        scattered = [sem(f"scattered{g}") for g in range(NG)]
        w_in = [sem(f"w_in{n}") for n in range(N_W)]
        xg_in = [sem(f"xg_in{n}") for n in range(N_X)]
        y_out = [sem(f"y_out{n}") for n in range(3)]
        gathered = [sem(f"gathered{i}") for i in range(NB)]
        mix_ready, mix_silu, out_ready, stored = sem("mix_ready"), sem("mix_silu"), sem("out_ready"), sem("stored")

        def bank(item):
            return work[job_at[item] % BANKS]

        def wait_filled(eng, item):
            eng.wait_ge(filled, job_at[item] + 1)

        def wait_emptied(eng, item):
            eng.wait_ge(emptied[CONSUMER[item[0]]], emptied_at[item])

        def tiles(i):
            b = BATCHES[i]
            return slice(b * TB, (b + 1) * TB)

        def tokens(i):
            b = BATCHES[i]
            return slice(b * S, (b + 1) * S)

        def step_no(i, n):
            return i * NS + n

        def sums_upto(g):
            return sum(1 for k in range(g + 1) if k // NS not in PAIRED or k % 2)

        def pairs_upto(g):
            return sum(1 for k in range(g + 1) if k // NS in PAIRED and k % 2)

        def group_tiles(g):
            first = min(tiles(2 * g).start, tiles(2 * g + 1).start)
            return slice(first, first + GT)

        softmaxes = {(0, 0): 0, (1, 0): 1, (1, 1): 2}

        block = ctx.enter_context(nc.Block())

        @block.sync
        def _(sp):
            for i in range(NB):
                sp.dma_start(X[:, tiles(i), :], x_v[:, tiles(i), :]).then_inc(x_in[i], 16)
                if i == 0:
                    sp.dma_start(wa[:, :], pack_a).then_inc(wa_in, 16)
            sp.dma_start(wb[:, :], pack_b).then_inc(wb_in, 16)
            sp.wait_ge(const_set, 2)
            for g in range(NG):
                sp.dma_start(slot_in[g].rearrange("s p d -> p s d"),
                             region[:, 0:D].unsqueeze(1).broadcast_to([P, SLOTS, D])).then_inc(slots_zeroed, 16)

            def load_weights(m):
                if m >= N_W:
                    wait_emptied(sp, ("slot_y", m - N_W))
                which = sp.value_load(slot_e[0:1, m:m + 1], min_val=0, max_val=E - 1)
                sp.dma_start(wst[m % N_W], experts[bass.ds(which, 1), :, :].rearrange("e p f -> (e p) f"))\
                    .then_inc(w_in[m % N_W], 16)

            def load_rows(m):
                if m >= N_X:
                    wait_filled(sp, ("slot_t", m - N_X))
                sp.dma_start(xg[m % N_X], slot_in[m // SLOTS][m % SLOTS]).then_inc(xg_in[m % N_X], 16)

            for item in order:
                kind, m = item[0], item[-1]
                if kind == "open":
                    sp.wait_ge(pos_ready, m + 1)
                    for k in range(N_W):
                        load_weights(m * SLOTS + k)
                    sp.wait_ge(scattered[m], 16 * GT * TOPK)
                    for k in range(N_X):
                        load_rows(m * SLOTS + k)
                elif kind == "slot_y":
                    end = (m // SLOTS + 1) * SLOTS
                    wait_emptied(sp, item)
                    if m + N_W < end:
                        load_weights(m + N_W)
                    if m + N_X < end:
                        load_rows(m + N_X)
                    sp.dma_start(slot_out[m // SLOTS][m % SLOTS], ysb[m % 3]).then_inc(y_out[m % 3], 16)
                elif kind == "done":
                    sp.wait_ge(out_ready, m + 1)
                    sp.dma_start(out_v[:, tiles(m), :], X[:, tiles(m), :]).then_inc(stored, 16)
            sp.wait_ge(stored, 16 * NB)

        @block.gpsimd
        def _(pool):
            pool.memset(ident[:, :], 0.0).then_inc(const_set, 1)
            pool.wait_ge(const_set, 1)
            pool.affine_select(out=ident[:, :], in_=ident[:, :], compare_op=ALU.not_equal, fill=1.0, base=0,
                               pattern=[[-1, P]], channel_multiplier=1).then_inc(const_made, 1)
            pool.memset(region[:, 0:D], 0.0).then_inc(const_set, 1)
            for t, value in ((ones[:, :], 1.0), (upad[:, :, 0:TAPS - 1], 0.0), (decay[:, :, :, 0:1], 0.0),
                             (before4[:, :, :], 1.0), (before8[:, :, :], 1.0), (pick_state[:, :], 0.0), (padded[:, 0:GT - 1, :], 0.0),
                             (xm, 0.0), (ab[:, :, :], 0.0)):
                pool.memset(t, value).then_inc(const_set, 1)
            for t, pattern, step in ((row_no[:, :, :], [[2 * P, NT], [1, TOPK]], 2), (mult128[:, :], [[P, GT]], 0),
                                     (slot_no[:, :], [[1, SLOTS]], 0)):
                pool.iota(t, pattern, base=0, channel_multiplier=step, allow_small_or_imprecise_dtypes=True)\
                    .then_inc(const_set, 1)
            pool.wait_ge(const_set, N_SET)
            pool.affine_select(out=upper[:, :], in_=ones[:, :], compare_op=ALU.is_gt, fill=0.0, base=0,
                               pattern=[[1, P]], channel_multiplier=-1).then_inc(const_made, 1)
            for m, n in ((before4, GROUPS), (before8, E)):
                pool.affine_select(out=m[:, :, :], in_=m[:, :, :], compare_op=ALU.is_gt, fill=0.0, base=0,
                                   pattern=[[1, n], [-1, n]], channel_multiplier=0).then_inc(const_made, 1)
            for j in range(3):
                pool.wait_ge(const_made, 4 + j)
                m = pick_state[2 * NS * j:2 * NS * (j + 1), :]
                pool.affine_select(out=m, in_=m, compare_op=ALU.not_equal, fill=1.0, base=0,
                                   pattern=[[-1, 2 * NS]], channel_multiplier=1).then_inc(const_made, 1)

            for item in order:
                kind = item[0]
                if kind == "scan":
                    _, i, s = item
                    if 1 <= s <= NS:
                        g = step_no(i, s - 1)
                        pool.wait_ge(state_ready, g + 1)
                        pool.wait_ge(cs_ready, g + 1)
                        if g >= N_PR:
                            if (g - N_PR) // NS in PAIRED and g % 2 == 0:
                                pool.wait_ge(paired, pairs_upto(g - N_PR + 1))
                            else:
                                pool.wait_ge(summed, sums_upto(g - N_PR))
                        c = cs[:, g % N_CS, :].unsqueeze(1).broadcast_to([P, HV, S])
                        pool.tensor_tensor(prod[:, g % N_PR], state[:, g % N_ST], c, ALU.mult)\
                            .then_inc(prod_ready, 1)
                elif kind == "scatter":
                    _, g, q = item
                    if q == 0:
                        pool.wait_ge(pos_ready, g + 1)
                        pool.wait_ge(slots_zeroed, 16 * NG)
                        pool.wait_ge(xn_ready, NB + 2 * g + 2)
                    for t in range(group_tiles(g).start + 2 * q, group_tiles(g).start + 2 * q + 2):
                        for k in range(TOPK):
                            pool.indirect_dma_start(slot_in[g].rearrange("s p d -> (s p) d"),
                                                    bass.IndirectOffsetOnAxis(ap=pos[:, k, t:t + 1], axis=0),
                                                    XN[:, t, :], None).then_inc(scattered[g], 16)
                elif kind == "gather":
                    i = item[1]
                    end = (i // 2 + 1) * SLOTS
                    for n in range(3):
                        pool.wait_ge(y_out[n], 16 * len(range(n, end, 3)))
                    for t in range(tiles(i).start, tiles(i).stop):
                        for k in range(TOPK):
                            pool.indirect_dma_start(yk[k][:, t, :], None,
                                                    slot_out[i // 2].rearrange("s p d -> (s p) d"),
                                                    bass.IndirectOffsetOnAxis(ap=pos[:, k, t:t + 1], axis=0))\
                                .then_inc(gathered[i], 16)

        @block.scalar
        def _(act):
            steps = 0

            def link(ins):
                nonlocal steps
                steps += 1
                ins.then_inc(act_step, 1)
                act.wait_ge(act_step, steps)

            act.dma_start(col[:, :], cols).then_inc(col_in, 16)
            act.dma_start(row[:, :], rows.partition_broadcast(P)).then_inc(row_in, 16)
            act.dma_start(wh[:, :], pack_h).then_inc(wh_in, 16)
            act.wait_ge(col_in, 16)
            act.activation(neg_a[:, :, :], col[:, C_ALOG:C_END].rearrange("p (h n) -> p h n", h=HV), ACT.Exp)\
                .then_inc(a_ready, 1)

            for item in order:
                kind = item[0]
                taken = emptied["act"]
                if kind == "stats":
                    _, l, i = item
                    act.wait_ge(var_ready, l * NB + i + 1)
                    act.activation(sdev[:, tiles(i)], veps[:, tiles(i)], ACT.Sqrt).then_inc(sd_ready, 1)
                elif kind == "xt":
                    _, l, i = item
                    wait_filled(act, item)
                    if l == 0:
                        act.activation(XNT[:, tokens(i)], bank(item)[:, :], ACT.Copy).then_inc(taken, 1)
                    else:
                        if i:
                            wait_filled(act, ("gate1", i - 1, 1))
                        act.activation(XNT1[:, :], bank(item)[:, :], ACT.Copy).then_inc(taken, 1)
                elif kind == "base":
                    i = item[1]
                    wait_filled(act, item)
                    if i:
                        wait_filled(act, ("score", i - 1, TB - 1))
                    act.activation(base[:, :], bank(item)[:, :], ACT.Silu, bias=col[:, C_BB:C_BB + 1])\
                        .then_inc(taken, 1)
                elif kind == "u0":
                    _, i, h = item
                    wait_filled(act, item)
                    if i:
                        wait_filled(act, ("wout", i - 1))
                    act.activation(uT[:, h, :], bank(item)[:, :], ACT.Silu, bias=col[:, C_BU + h:C_BU + h + 1])\
                        .then_inc(taken, 1)
                elif kind == "sh_gate":
                    i = item[1]
                    wait_filled(act, item)
                    if i:
                        wait_filled(act, ("sh_out", i - 1))
                    act.activation(sh_h[:, :], bank(item)[:, :], ACT.Silu).then_inc(taken, 1)
                elif kind == "v0":
                    _, i, j = item
                    wait_emptied(act, item)
                    act.activation(v[:, 2 * j:2 * j + 2, :], v[:, 2 * j:2 * j + 2, :], ACT.Silu).then_inc(v_ready, 1)
                elif kind == "score":
                    _, i, m = item
                    wait_filled(act, item)
                    if i:
                        wait_filled(act, ("attn", i - 1, 1))
                    act.activation(sq[:, m, :], bank(item)[:, :], ACT.Relu, scale=1.0 / S).then_inc(taken, 1)
                elif kind == "sh_out":
                    i = item[1]
                    wait_filled(act, item)
                    if i:
                        act.wait_ge(x1_done, i)
                    act.activation(g0[:, :, :], bank(item)[:, :].rearrange("p (t d) -> p t d", t=TB), ACT.Silu)\
                        .then_inc(taken, 1)
                elif kind == "soft_a":
                    _, l, g = item
                    ts = group_tiles(g) if l else slice(0, NT)
                    act.wait_ge(soft_in, softmaxes[l, g] + 1)
                    act.activation(sc[:, ts, :], lg[:, l, ts, :], ACT.Exp).then_inc(soft_exp, 1)
                elif kind == "oct":
                    q = item[1]
                    wait_filled(act, item)
                    act.activation(pairT[:, q * S:(q + 1) * S], bank(item)[:, :], ACT.Copy).then_inc(taken, 1)
                elif kind == "pair_act":
                    n = item[1]
                    wait_emptied(act, ("pair_h", (n + 1) * NT // 4 - 1))
                    if n:
                        act.wait_ge(pair_out, n)
                    act.activation(gate0, ph[:, :, 0:HID0], ACT.Silu).then_inc(pair_sig, 1)
                elif kind == "u1":
                    _, i, h = item
                    wait_filled(act, item)
                    if i:
                        act.wait_ge(conv_ready, 2 * (i - 1) + h + 1)
                    act.activation(upad[:, h, TAPS - 1:], bank(item)[:, :], ACT.Identity,
                                   bias=col[:, C_B1 + h:C_B1 + h + 1]).then_inc(taken, 1)
                elif kind == "gate1":
                    _, i, h = item
                    wait_filled(act, item)
                    if i >= 2:
                        act.wait_ge(y_ready, i - 1)
                    act.activation(g1[:, i % 2, h, :], bank(item)[:, :], ACT.Sigmoid,
                                   bias=col[:, C_B2 + h:C_B2 + h + 1]).then_inc(taken, 1)
                elif kind == "u1_sig":
                    i = item[1]
                    act.wait_ge(conv_ready, 2 * i + 2)
                    act.activation(u1[:, i % 2], u1[:, i % 2], ACT.Sigmoid).then_inc(u1_ready, 1)
                elif kind == "xproj":
                    i = item[1]
                    wait_filled(act, item)
                    if i:
                        wait_filled(act, ("dt", i - 1, 1))
                        act.wait_ge(bcs_ready, i)
                    act.activation(dtT[:, :], bank(item)[0:RANK, :], ACT.Copy)
                    act.activation(bc[:, :], bank(item)[RANK:RANK + 2 * NS, :], ACT.Copy).then_inc(taken, 1)
                elif kind == "dt":
                    _, i, h = item
                    wait_filled(act, item)
                    act.activation(delta[:, i % 2, h, :], bank(item)[:, :], ACT.Identity,
                                   bias=col[:, C_DTB + h:C_DTB + h + 1]).then_inc(taken, 1)
                elif kind == "softplus":
                    i = item[1]
                    act.preload_act_table_set("natural_log_exp_and_others")
                    act.wait_ge(na_ready, i + 1)
                    link(act.activation(du[:, i % 2], du[:, i % 2], ACT.Exp))
                    act.activation(du[:, i % 2], du[:, i % 2], ACT.Ln, bias=1.0).then_inc(l_ready, 1)
                elif kind == "scan":
                    _, i, s = item
                    if s < NS:
                        g = step_no(i, s)
                        if s == 0:
                            act.wait_ge(du_ready, i + 1)
                        if g >= N_DA:
                            act.wait_ge(state_ready, g - N_DA + 1)
                        if g == 0:
                            act.wait_ge(a_negated, 1)
                        for h in range(HV):
                            ins = act.activation(decay[:, g % N_DA, h, 1:S], delta[:, i % 2, h, 1:S], ACT.Exp,
                                                 scale=neg_a[:, h, s:s + 1])
                        ins.then_inc(decay_ready, 1)
                        act.wait_ge(c_cast, g + 1)
                        if g >= N_CS:
                            act.wait_ge(prod_ready, g - N_CS + 1)
                        act.activation(cs[:, g % N_CS, :], p_c[:, :], ACT.Copy).then_inc(cs_ready, 1)
                elif kind == "slot_h":
                    m = item[1]
                    wait_filled(act, item)
                    if m >= 2:
                        wait_filled(act, ("slot_y", m - 2))
                    for c in range(HC):
                        ins = act.activation(hT[m % 2][:, c, :], bank(item)[:, c * P:(c + 1) * P], ACT.Relu,
                                             bias=wst[m % N_W][:, X_B1 + c:X_B1 + c + 1])
                    ins.then_inc(taken, 1)
                elif kind == "mix":
                    i = item[1]
                    act.wait_ge(mix_ready, i + 1)
                    act.activation(yk[0][:, tiles(i), :], yk[0][:, tiles(i), :], ACT.Silu).then_inc(mix_silu, 1)

        @block.tensor
        def _(pe):
            pe.wait_ge(const_made, 1)

            for item in order:
                kind = item[0]
                if kind in CONSUMER:
                    n = job_at[item]
                    if n >= BANKS:
                        wait_emptied(pe, jobs[n - BANKS])
                    dst = bank(item)
                if kind == "xt":
                    _, l, i = item
                    pe.wait_ge(xn_ready, l * NB + i + 1)
                    for t in range(TB):
                        ins = pe.transpose(dst[:, t * P:(t + 1) * P], XN[:, tiles(i).start + t, :], ident[:, :])
                    ins.then_inc(filled, 1)
                elif kind == "logits":
                    _, l, i = item
                    wait_emptied(pe, ("xt", l, i))
                    wg = wa[:, A_GATE1:A_END] if l else wa[:, A_GATE0:A_GATE1]
                    for t in range(TB):
                        lhs = XNT1[:, t * P:(t + 1) * P] if l else \
                            XNT[:, tokens(i).start + t * P:tokens(i).start + (t + 1) * P]
                        ins = pe.matmul(dst[:, t * E:(t + 1) * E], lhs, wg, start=True, stop=True)
                    ins.then_inc(filled, 1)
                elif kind in ("base", "u0", "sh_gate", "sh_up"):
                    i = item[1]
                    if item == ("base", 0):
                        pe.wait_ge(wa_in, 16)
                        wait_emptied(pe, ("xt", 0, 0))
                    elif kind == "base":
                        wait_emptied(pe, ("xt", 0, i))
                    at_col = {"base": A_UV + 2 * GE, "u0": A_UV + P * item[-1], "sh_gate": A_SW1, "sh_up": A_SW3}[kind]
                    pe.matmul(dst[:, :], wa[:, at_col:at_col + P], XNT[:, tokens(i)], start=True, stop=True)\
                        .then_inc(filled, 1)
                elif kind == "v0":
                    _, i, j = item
                    for t in range(2):
                        tok = tokens(i).start + (2 * j + t) * P
                        ins = pe.matmul(dst[:, t * GE:(t + 1) * GE], XNT[:, tok:tok + P], wa[:, A_UV + GE:A_UV + 2 * GE],
                                        start=True, stop=True)
                    ins.then_inc(filled, 1)
                elif kind == "score":
                    _, i, m = item
                    pe.wait_ge(qk_ready, i + 1)
                    pe.matmul(dst[:, :], kT[:, m * P:(m + 1) * P], qT[:, :], start=True, stop=True)\
                        .then_inc(filled, 1)
                elif kind == "attn":
                    _, i, h = item
                    pe.wait_ge(v_ready, 2 * (i + 1))
                    for m in range(TB):
                        if h == 0:
                            pe.wait_ge(sq_ready, TB * i + m + 1)
                        ins = pe.matmul(dst[:, :], v[:, m, h * P:(h + 1) * P], sq[:, m, :],
                                        start=(m == 0), stop=(m == TB - 1))
                    ins.then_inc(filled, 1)
                elif kind == "wout":
                    i = item[1]
                    wait_emptied(pe, ("attn", i, 1))
                    for t in range(TB):
                        for h in range(2):
                            ins = pe.matmul(dst[:, t * D:(t + 1) * D], uT[:, h, t * P:(t + 1) * P],
                                            wa[:, A_WOUT + h * D:A_WOUT + (h + 1) * D], start=(h == 0), stop=(h == 1))
                    ins.then_inc(filled, 1)
                elif kind == "sh_out":
                    i = item[1]
                    wait_emptied(pe, ("sh_up", i))
                    if i == LAST:
                        wait_emptied(pe, ("pair_sum", 1))
                    for t in range(TB):
                        routed = i == LAST and t == 0
                        ins = pe.matmul(dst[:, t * D:(t + 1) * D], sh_h[:, t * P:(t + 1) * P],
                                        wa[:, A_SW2:A_SW2 + D], start=True, stop=not routed)
                        if routed:
                            for g in range(E):
                                ins = pe.matmul(dst[:, 0:D], htp[:, g, :], wh[:, H_W2 + g * D:H_W2 + (g + 1) * D],
                                                start=False, stop=(g == E - 1))
                    ins.then_inc(filled, 1)
                elif kind == "pair_in":
                    pe.wait_ge(wb_in, 16)
                    pe.wait_ge(wh_in, 16)
                    pe.wait_ge(xm_ready, 1)
                    for g in range(E):
                        ins = pe.matmul(dst[:, 0:P], xm[:, g * P:(g + 1) * P], wb[:, B_W13 + g * P:B_W13 + (g + 1) * P],
                                        start=(g == 0), stop=(g == E - 1))
                    ins.then_inc(filled, 1)
                elif kind == "count0":
                    pe.wait_ge(picked_ready, 1)
                    for t in range(NT):
                        ins = pe.matmul(dst[:, 0:E], ones[:, :], picked0[:, t, :], start=(t == 0), stop=(t == NT - 1))
                    ins.then_inc(filled, 1)
                elif kind == "oct":
                    q = item[1]
                    pe.wait_ge(pair_ready, 1)
                    for t in range(4):
                        ins = pe.transpose(dst[:, t * P:(t + 1) * P],
                                           pair[:, 4 * q + t, :, :].rearrange("p k c -> p (k c)"), ident[:, :])
                    ins.then_inc(filled, 1)
                elif kind == "pair_h":
                    q = item[1]
                    wait_emptied(pe, ("oct", q // 2))
                    wait_emptied(pe, ("pair_in",))
                    for t in range(2):
                        tok = (2 * q + t) * P
                        ins = pe.matmul(dst[:, t * 2 * P:(t + 1) * 2 * P], pairT[:, tok:tok + P],
                                        ab[:, :, :].rearrange("p k c -> p (k c)"), start=True, stop=True)
                    ins.then_inc(filled, 1)
                elif kind == "pair_sum":
                    n = item[1]
                    pe.wait_ge(pair_out, n + 1)
                    for j in range(NT):
                        ins = pe.matmul(dst[0:HID0, 0:E * E], ph[:, j, HID0:2 * HID0],
                                        pair[:, n * NT // 2 + j // TOPK, j % TOPK, :],
                                        start=(j == 0), stop=(j == NT - 1))
                    ins.then_inc(filled, 1)
                elif kind in ("u1", "gate1"):
                    _, i, h = item
                    if kind == "u1":
                        wait_emptied(pe, ("xt", 1, i))
                        if i == 0:
                            pe.wait_ge(wb_in, 16)
                            pe.wait_ge(wh_in, 16)
                    at_col = (B_W1 if kind == "u1" else B_W2) + h * P
                    pe.matmul(dst[:, :], wb[:, at_col:at_col + P], XNT1[:, :], start=True, stop=True)\
                        .then_inc(filled, 1)
                elif kind == "xproj":
                    i = item[1]
                    pe.wait_ge(u1_ready, i + 1)
                    n_out = RANK + 2 * NS
                    for h in range(HV):
                        ins = pe.matmul(dst[0:n_out, :], wb[:, B_XP + h * n_out:B_XP + (h + 1) * n_out],
                                        u1[:, i % 2, h, :], start=(h == 0), stop=(h == HV - 1))
                    ins.then_inc(filled, 1)
                elif kind == "dt":
                    _, i, h = item
                    wait_emptied(pe, ("xproj", i))
                    pe.matmul(dst[:, :], wh[:, H_DT + h * P:H_DT + (h + 1) * P], dtT[:, :], start=True, stop=True)\
                        .then_inc(filled, 1)
                elif kind == "scan":
                    _, i, s = item
                    if s < NS:
                        g = step_no(i, s)
                        if g == 0:
                            pe.wait_ge(const_made, N_MADE)
                        if s == 0:
                            pe.wait_ge(bcs_ready, i + 1)
                        if g:
                            pe.wait_ge(drive_ready, g)
                        pe.matmul(p_b[:, :], pick_state[:, s:s + 1].broadcast_to([3 * 2 * NS, P]), bcs[:, i % 2, :], start=True, stop=True)\
                            .then_inc(b_cast, 1)
                        if g:
                            pe.wait_ge(cs_ready, g)
                        pe.matmul(p_c[:, :], pick_state[:, NS + s:NS + s + 1].broadcast_to([3 * 2 * NS, P]), bcs[:, i % 2, :], start=True, stop=True)\
                            .then_inc(c_cast, 1)
                    if s >= LAG:
                        n = s - LAG
                        g = step_no(i, n)
                        if i in PAIRED and n % 2 == 0:
                            continue
                        if n <= 1 and i:
                            pe.wait_ge(y_read, i)
                        if i in PAIRED:
                            pe.wait_ge(paired, pairs_upto(g))
                        else:
                            pe.wait_ge(prod_ready, g + 1)
                        for h in range(HV):
                            ins = pe.matmul(p_y[h][:, :], ident[:, :], prod[:, g % N_PR, h, :],
                                            start=(n <= 1 and (i in PAIRED or n == 0)), stop=(n == NS - 1))
                        ins.then_inc(summed, 1)
                elif kind == "wo1":
                    i = item[1]
                    pe.wait_ge(y_ready, i + 1)
                    for t in range(TB):
                        for h in range(HV):
                            ins = pe.matmul(dst[:, t * D:(t + 1) * D], u1[:, i % 2, h, t * P:(t + 1) * P],
                                            wb[:, B_WO + h * D:B_WO + (h + 1) * D], start=(h == 0), stop=(h == HV - 1))
                    ins.then_inc(filled, 1)
                elif kind == "rank1":
                    pe.wait_ge(picked_ready, item[1] + 2)
                    for back in range(GT):
                        tiles_before = padded[:, GT - 1 - back:2 * GT - 1 - back, :].rearrange("p t e -> p (t e)")
                        ins = pe.matmul(dst[:, 0:GT * E], ones[:, :] if back else upper[:, :], tiles_before,
                                        start=(back == 0), stop=(back == GT - 1))
                    ins.then_inc(filled, 1)
                elif kind == "count1":
                    for t in range(GT):
                        ins = pe.matmul(dst[:, 0:E], ones[:, :], picked1[:, t, :], start=(t == 0), stop=(t == GT - 1))
                    ins.then_inc(filled, 1)
                elif kind == "slot_t":
                    m = item[1]
                    pe.wait_ge(xg_in[m % N_X], 16 * (m // N_X + 1))
                    pe.transpose(dst[:, 0:P], xg[m % N_X], ident[:, :]).then_inc(filled, 1)
                elif kind == "slot_h":
                    m = item[1]
                    pe.wait_ge(w_in[m % N_W], 16 * (m // N_W + 1))
                    wait_emptied(pe, ("slot_t", m))
                    for c in range(HC):
                        ins = pe.matmul(dst[:, c * P:(c + 1) * P], wst[m % N_W][:, X_W1 + c * P:X_W1 + (c + 1) * P],
                                        xgT[m % 2], start=True, stop=True)
                    ins.then_inc(filled, 1)
                elif kind == "slot_y":
                    m = item[1]
                    wait_emptied(pe, ("slot_h", m))
                    for c in range(HC):
                        ins = pe.matmul(dst[:, 0:D], hT[m % 2][:, c, :],
                                        wst[m % N_W][:, X_W2 + c * D:X_W2 + (c + 1) * D],
                                        start=(c == 0), stop=(c == HC - 1))
                    ins.then_inc(filled, 1)

        @block.vector
        def _(dve):
            steps = 0

            def link(ins):
                nonlocal steps
                steps += 1
                ins.then_inc(dve_step, 1)
                dve.wait_ge(dve_step, steps)

            def rank_step(n, dst, of, width, before):
                nt = of.shape[1]
                a, b = cmp_a[:, 0:nt, 0:width, 0:width], cmp_b[:, 0:nt, 0:width, 0:width]
                vj = of.unsqueeze(2).broadcast_to([P, nt, width, width])
                vi = of.unsqueeze(3).broadcast_to([P, nt, width, width])
                if n == 0:
                    link(dve.tensor_tensor(a, vj, vi, ALU.is_gt))
                elif n == 1:
                    link(dve.tensor_tensor(b, vj, vi, ALU.is_equal))
                elif n == 2:
                    link(dve.tensor_tensor(b, b, before[:, :, :].unsqueeze(1).broadcast_to([P, nt, width, width]),
                                           ALU.mult))
                elif n == 3:
                    link(dve.tensor_tensor(a, a, b, ALU.add))
                else:
                    link(dve.tensor_reduce(dst, a, AX.X, ALU.add))

            def routed_tiles(l, g):
                return group_tiles(g) if l else slice(0, NT)

            dve.wait_ge(a_ready, 1)
            dve.tensor_scalar(neg_a[:, :, :], neg_a[:, :, :], -1.0, None, ALU.mult).then_inc(a_negated, 1)

            for item in order:
                kind = item[0]
                taken = emptied["dve"]
                if kind == "stats":
                    _, l, i = item
                    if l == 0:
                        dve.wait_ge(x_in[i], 16)
                    for t in range(TB):
                        ins = dve.bn_stats(stat[:, t, :], X[:, tiles(i).start + t, :])
                    link(ins)
                    for t in range(TB):
                        ins = dve.bn_aggr(mv[:, tiles(i).start + t, :], stat[:, t, :])
                    link(ins)
                    dve.tensor_scalar(veps[:, tiles(i)], mv[:, tiles(i), 1], EPS, None, ALU.add).then_inc(var_ready, 1)
                elif kind == "norm":
                    _, l, i = item
                    dve.wait_ge(sd_ready, l * NB + i + 1)
                    link(dve.reciprocal(rstd[:, tiles(i)], sdev[:, tiles(i)]))
                    for t in range(tiles(i).start, tiles(i).stop):
                        ins = dve.tensor_scalar(XN[:, t, :], X[:, t, :], mv[:, t, 0:1], rstd[:, t:t + 1],
                                                ALU.subtract, ALU.mult)
                    ins.then_inc(xn_ready, 1)
                elif kind == "logits":
                    _, l, i = item
                    wait_filled(dve, item)
                    src = bank(item)[:, 0:TB * E].rearrange("p (t e) -> p t e", t=TB)
                    if l == 0:
                        dve.tensor_copy(lg[:, 0, tiles(i), :], src).then_inc(taken, 1)
                    else:
                        dve.tensor_tensor(lg[:, 1, tiles(i), :], src,
                                          row[:, R_GB:R_END].unsqueeze(1).broadcast_to([P, TB, E]), ALU.add)\
                            .then_inc(taken, 1)
                elif kind == "base":
                    i = item[1]
                    wait_emptied(dve, item)
                    for n, t in enumerate((qT, kT)):
                        ins = dve.tensor_scalar(t[:, :], base[:, :], col[:, C_GAM + n:C_GAM + n + 1],
                                                col[:, C_BET + n:C_BET + n + 1], ALU.mult, ALU.add)
                    ins.then_inc(qk_ready, 1)
                elif kind == "sh_up":
                    i = item[1]
                    wait_filled(dve, item)
                    wait_emptied(dve, ("sh_gate", i))
                    dve.tensor_tensor(sh_h[:, :], sh_h[:, :], bank(item)[:, :], ALU.mult).then_inc(taken, 1)
                elif kind == "v0":
                    _, i, j = item
                    wait_filled(dve, item)
                    if i == 0 and j == 0:
                        dve.wait_ge(row_in, 16)
                    if i:
                        wait_filled(dve, ("attn", i - 1, 1))
                    dve.tensor_tensor(v[:, 2 * j:2 * j + 2, :], bank(item)[:, :].rearrange("p (t e) -> p t e", t=2),
                                      row[:, R_BV:R_BV + GE].unsqueeze(1).broadcast_to([P, 2, GE]), ALU.add)\
                        .then_inc(taken, 1)
                elif kind == "score":
                    _, i, m = item
                    wait_emptied(dve, item)
                    dve.tensor_tensor(sq[:, m, :], sq[:, m, :], sq[:, m, :], ALU.mult).then_inc(sq_ready, 1)
                elif kind == "attn":
                    _, i, h = item
                    wait_filled(dve, item)
                    dve.tensor_tensor(uT[:, h, :], uT[:, h, :], bank(item)[:, :], ALU.mult).then_inc(taken, 1)
                elif kind == "wout":
                    wait_filled(dve, item)
                    dve.tensor_tensor(s0[:, :, :], bank(item)[:, :].rearrange("p (t d) -> p t d", t=TB),
                                      row[:, R_BOUT:R_BOUT + D].unsqueeze(1).broadcast_to([P, TB, D]), ALU.add)\
                        .then_inc(taken, 1)
                elif kind == "x1":
                    i = item[1]
                    wait_emptied(dve, ("sh_out", i))
                    wait_emptied(dve, ("wout", i))
                    link(dve.tensor_tensor(s0[:, :, :], s0[:, :, :], g0[:, :, :], ALU.mult))
                    dve.tensor_tensor(X[:, tiles(i), :], X[:, tiles(i), :], s0[:, :, :], ALU.add).then_inc(x1_done, 1)
                    dve.wait_ge(x1_done, i + 1)
                elif kind == "soft_a":
                    _, l, g = item
                    ts = routed_tiles(l, g)
                    wait_emptied(dve, ("logits", l, 2 * g + 1 if l else LAST))
                    link(dve.tensor_reduce(red[:, ts], lg[:, l, ts, :], AX.X, ALU.max))
                    n = ts.stop - ts.start
                    dve.tensor_tensor(lg[:, l, ts, :], lg[:, l, ts, :], red[:, ts].unsqueeze(2).broadcast_to([P, n, E]),
                                      ALU.subtract).then_inc(soft_in, 1)
                elif kind == "soft_b":
                    _, l, g = item
                    ts = routed_tiles(l, g)
                    n = ts.stop - ts.start
                    dve.wait_ge(soft_exp, softmaxes[l, g] + 1)
                    link(dve.tensor_reduce(red2[:, ts], sc[:, ts, :], AX.X, ALU.add))
                    link(dve.reciprocal(red2[:, ts], red2[:, ts]))
                    link(dve.tensor_tensor(sc[:, ts, :], sc[:, ts, :], red2[:, ts].unsqueeze(2).broadcast_to([P, n, E]),
                                           ALU.mult))
                    if l == 0:
                        link(dve.tensor_tensor(sel_s[:, :, :], sc[:, :, :],
                                               row[:, R_EB:R_EB + E].unsqueeze(1).broadcast_to([P, NT, E]), ALU.add))
                elif kind == "group":
                    pairs = sel_s[:, :, :].rearrange("p t (g c) -> p t g c", c=2)
                    if item[1] == 0:
                        dve.wait_ge(const_made, N_MADE)
                        link(dve.tensor_tensor(grp[:, :, :], sel_s[:, :, 0:E:2], sel_s[:, :, 1:E:2], ALU.add))
                        for n in range(2):
                            rank_step(n, keep[:, :, :], grp[:, :, :], GROUPS, before4)
                    elif item[1] == 1:
                        for n in range(2, 5):
                            rank_step(n, keep[:, :, :], grp[:, :, :], GROUPS, before4)
                        link(dve.tensor_scalar(keep[:, :, :], keep[:, :, :], 2.0, None, ALU.is_lt))
                    else:
                        link(dve.tensor_scalar(grp[:, :, :], keep[:, :, :], BIG, -BIG, ALU.mult, ALU.add))
                        link(dve.tensor_tensor(pairs, pairs, keep[:, :, :].unsqueeze(3)
                                               .broadcast_to([P, NT, GROUPS, 2]), ALU.mult))
                        link(dve.tensor_tensor(pairs, pairs, grp[:, :, :].unsqueeze(3)
                                               .broadcast_to([P, NT, GROUPS, 2]), ALU.add))
                elif kind == "rank":
                    _, l, g, n = item
                    ts = routed_tiles(l, g)
                    rank_step(n, rank[:, ts, :], sc[:, ts, :] if l else sel_s[:, :, :], E, before8)
                elif kind == "pick":
                    _, l, g, n = item
                    ts = routed_tiles(l, g)
                    nt = ts.stop - ts.start
                    if n == 0:
                        for k in range(TOPK):
                            ins = dve.tensor_scalar(pick[:, ts, k, :], rank[:, ts, :], float(k), None, ALU.is_equal)
                        link(ins)
                        if l and g:
                            wait_filled(dve, ("count1", g - 1))
                        dve.tensor_tensor(picked1 if l else picked0[:, :, :], pick[:, ts, 0, :], pick[:, ts, 1, :],
                                          ALU.add).then_inc(picked_ready, 1)
                    else:
                        link(dve.tensor_tensor(tmp8[:, ts, :, :], pick[:, ts, :, :],
                                               sc[:, ts, :].unsqueeze(2).broadcast_to([P, nt, TOPK, E]), ALU.mult))
                        link(dve.tensor_reduce(wgt[l][:, ts, :], tmp8[:, ts, :, :], AX.X, ALU.add))
                    if l == 0 and n == 1:
                        dve.wait_ge(const_set, N_SET)
                        wait_emptied(dve, ("xt", 0, LAST))
                        spread_x = xm.rearrange("p (g r) -> p g r", r=P + 1)[:, :, 0:P]
                        for k in range(TOPK):
                            ins = dve.tensor_copy(spread_x[:, :, k * E * E:(k + 1) * E * E:E],
                                                  XNT[:, 0:E].unsqueeze(1).broadcast_to([P, E, E]))
                        ins.then_inc(xm_ready, 1)
                elif kind == "count0":
                    wait_filled(dve, item)
                    dve.tensor_copy(cnt[:, :], bank(item)[:, 0:E]).then_inc(taken, 1)
                elif kind == "pairs":
                    if item[1] == 0:
                        wait_emptied(dve, ("count0",))
                        dve.memset(cum[:, 0:1], 0.0)
                        link(dve.tensor_tensor_scan(cum[:, 1:E + 1], cnt[:, :], cnt[:, :], 0.0, ALU.add, ALU.bypass))
                        link(dve.tensor_tensor(ge[:, :, :],
                                               row_no[:, :, :].rearrange("p t k -> p (t k)").unsqueeze(2)
                                               .broadcast_to([P, NT * TOPK, E + 1]),
                                               cum[:, :].unsqueeze(1).broadcast_to([P, NT * TOPK, E + 1]), ALU.is_ge))
                        link(dve.tensor_tensor(seg[:, :, :], ge[:, :, 0:E], ge[:, :, 1:E + 1], ALU.subtract))
                    else:
                        dve.wait_ge(slots_zeroed, 16 * NG)
                        dve.tensor_tensor(
                            pair.rearrange("p t k (e g) -> p (t k) e g", e=E),
                            pick[:, :, :, :].rearrange("p t k e -> p (t k) e").unsqueeze(3)
                            .broadcast_to([P, NT * TOPK, E, E]),
                            seg[:, :, :].unsqueeze(2).broadcast_to([P, NT * TOPK, E, E]), ALU.mult)\
                            .then_inc(pair_ready, 1)
                elif kind == "pair_in":
                    wait_filled(dve, item)
                    half = E * E
                    dve.tensor_copy(ab[0:half, 0, :], bank(item)[0:half, 0:P])
                    dve.tensor_copy(ab[half:2 * half, 1, :], bank(item)[half:2 * half, 0:P]).then_inc(taken, 1)
                elif kind == "pair_h":
                    q = item[1]
                    wait_filled(dve, item)
                    w = wgt[0][:, 2 * q:2 * q + 2, :].rearrange("p t k -> p (t k)").unsqueeze(2)
                    if q == NT // 4:
                        wait_filled(dve, ("pair_sum", 0))
                    j = 4 * q % NT
                    dve.tensor_tensor(ph[:, j:j + 4, :], bank(item)[:, :].rearrange("p (j c) -> p j c", j=4),
                                      w.broadcast_to([P, 4, 2 * HID0]), ALU.mult).then_inc(taken, 1)
                elif kind == "pair_act":
                    dve.wait_ge(pair_sig, item[1] + 1)
                    dve.tensor_tensor(ph[:, :, HID0:2 * HID0], ph[:, :, HID0:2 * HID0], gate0, ALU.mult)\
                        .then_inc(pair_out, 1)
                elif kind == "pair_sum":
                    n = item[1]
                    wait_filled(dve, item)
                    sums = bank(item)[0:HID0, 0:E * E].rearrange("p (e g) -> p g e", e=E)
                    if n == 0:
                        link(dve.memset(htp, 0.0))
                        dve.tensor_copy(htp[:, :, 0:E], sums).then_inc(taken, 1)
                    else:
                        wait_emptied(dve, ("pair_sum", 0))
                        dve.tensor_tensor(htp[:, :, 0:E], htp[:, :, 0:E], sums, ALU.add).then_inc(taken, 1)
                elif kind == "u1":
                    _, i, h = item
                    wait_emptied(dve, item)
                    if i >= 2:
                        wait_filled(dve, ("wo1", i - 2))
                    if i == 0:
                        dve.wait_ge(const_set, N_SET)
                    dst = u1[:, i % 2, h, :]

                    def tap(k):
                        return col[:, C_CW + TAPS * h + k:C_CW + TAPS * h + k + 1]
                    link(dve.tensor_scalar(dst, upad[:, h, TAPS - 1:TAPS - 1 + S], tap(TAPS - 1),
                                           col[:, C_CB + h:C_CB + h + 1], ALU.mult, ALU.add))
                    for k in range(TAPS - 1):
                        ins = dve.scalar_tensor_tensor(dst, upad[:, h, k:k + S], tap(k), dst, ALU.mult, ALU.add)
                        if k < TAPS - 2:
                            link(ins)
                    ins.then_inc(conv_ready, 1)
                elif kind == "xproj":
                    i = item[1]
                    wait_emptied(dve, item)
                    if i >= 2:
                        dve.wait_ge(c_cast, step_no(i - 2, NS - 1) + 1)
                    n = 2 * NS
                    hi = bcs[0:n, i % 2, :]
                    link(dve.tensor_copy(hi, bc[:, :]))
                    link(dve.tensor_tensor(bc_res, bc[:, :], hi, ALU.subtract))
                    link(dve.tensor_copy(bc_mid[:, :], bc_res))
                    dve.tensor_copy(bcs[n:2 * n, i % 2, :], bc_mid[:, :])
                    dve.tensor_tensor(bcs[2 * n:3 * n, i % 2, :], bc_res, bc_mid[:, :], ALU.subtract)\
                        .then_inc(bcs_ready, 1)
                elif kind == "softplus":
                    i = item[1]
                    wait_emptied(dve, ("dt", i, 1))
                    z, l, uu = delta[:, i % 2], du[:, i % 2], u1[:, i % 2]
                    dve.scalar_tensor_tensor(l, z, -1.0, z, ALU.mult, ALU.min).then_inc(na_ready, 1)
                    dve.wait_ge(l_ready, i + 1)
                    link(dve.scalar_tensor_tensor(z, z, 0.0, l, ALU.max, ALU.add))
                    dve.wait_ge(u1_ready, i + 1)
                    dve.tensor_tensor(l, z, uu, ALU.mult).then_inc(du_ready, 1)
                    dve.wait_ge(du_ready, i + 1)
                elif kind == "scan":
                    _, i, s = item
                    if s < NS:
                        g = step_no(i, s)
                        dve.wait_ge(b_cast, g + 1)
                        if g >= N_DBU:
                            dve.wait_ge(state_ready, g - N_DBU + 1)
                        dve.tensor_tensor(drive[:, g % N_DBU], du[:, i % 2],
                                          p_b[:, :].unsqueeze(1).broadcast_to([P, HV, S]), ALU.mult)\
                            .then_inc(drive_ready, 1)
                    if 1 <= s <= NS:
                        g = step_no(i, s - 1)
                        dve.wait_ge(decay_ready, g + 1)
                        dve.wait_ge(drive_ready, g + 1)
                        if g >= N_ST:
                            dve.wait_ge(prod_ready, g - N_ST + 1)
                        if g == 0:
                            dve.wait_ge(const_set, N_SET)
                        dve.tensor_tensor_scan(state[:, g % N_ST].rearrange("p h t -> p (h t)"),
                                               decay[:, g % N_DA].rearrange("p h t -> p (h t)"),
                                               drive[:, g % N_DBU].rearrange("p h t -> p (h t)"), 0.0,
                                               ALU.mult, ALU.add).then_inc(state_ready, 1)
                    n = s - 2
                    if i in PAIRED and 0 <= n < NS and n % 2:
                        g = step_no(i, n)
                        dve.wait_ge(prod_ready, g + 1)
                        dve.tensor_tensor(prod[:, g % N_PR], prod[:, g % N_PR], prod[:, (g - 1) % N_PR], ALU.add)\
                            .then_inc(paired, 1)
                elif kind == "scan_out":
                    i = item[1]
                    dve.wait_ge(summed, sums_upto(step_no(i, NS - 1)))
                    for h in range(HV):
                        ins = dve.scalar_tensor_tensor(u1[:, i % 2, h, :], u1[:, i % 2, h, :],
                                                       col[:, C_D + h:C_D + h + 1], p_y[h][:, :], ALU.mult, ALU.add)
                    ins.then_inc(y_read, 1)
                    dve.wait_ge(y_read, i + 1)
                    wait_emptied(dve, ("gate1", i, 1))
                    dve.tensor_tensor(u1[:, i % 2], u1[:, i % 2], g1[:, i % 2], ALU.mult).then_inc(y_ready, 1)
                elif kind == "wo1":
                    i = item[1]
                    wait_filled(dve, item)
                    dve.tensor_tensor(s1[:, tiles(i), :], bank(item)[:, :].rearrange("p (t d) -> p t d", t=TB),
                                      row[:, R_BO:R_BO + D].unsqueeze(1).broadcast_to([P, TB, D]), ALU.add)\
                        .then_inc(taken, 1)
                elif kind == "rank1":
                    wait_filled(dve, item)
                    dve.tensor_copy(rank[:, group_tiles(item[1]), :],
                                    bank(item)[:, 0:GT * E].rearrange("p (t e) -> p t e", t=GT)).then_inc(taken, 1)
                elif kind == "count1":
                    wait_filled(dve, item)
                    dve.tensor_copy(cnt[:, :], bank(item)[:, 0:E]).then_inc(taken, 1)
                    wait_emptied(dve, item)
                elif kind == "route1_slots":
                    _, g, n = item
                    ts = group_tiles(g)
                    if n == 0:
                        link(dve.tensor_tensor(cmp_t, cnt[:, :].unsqueeze(2).broadcast_to([P, E, GT]),
                                               mult128[:, :].unsqueeze(1).broadcast_to([P, E, GT]), ALU.is_gt))
                        link(dve.tensor_reduce(ntile[:, :], cmp_t, AX.X, ALU.add))
                        link(dve.tensor_tensor_scan(ctile[:, :], ntile[:, :], ntile[:, :], 0.0, ALU.add, ALU.bypass))
                        link(dve.tensor_tensor(cmp_s, slot_no[:, :].unsqueeze(2).broadcast_to([P, SLOTS, E]),
                                               ctile[:, :].unsqueeze(1).broadcast_to([P, SLOTS, E]), ALU.is_ge))
                        link(dve.tensor_reduce(slot_f[:, :], cmp_s, AX.X, ALU.add))
                        dve.tensor_scalar(slot_e[:, g * SLOTS:(g + 1) * SLOTS], slot_f[:, :], float(E - 1), None,
                                          ALU.min)
                    else:
                        link(dve.tensor_tensor(first_row[:, :], ctile[:, :], ntile[:, :], ALU.subtract))
                        link(dve.tensor_scalar(first_row[:, :], first_row[:, :], float(P), None, ALU.mult))
                        link(dve.tensor_tensor(rank[:, ts, :], rank[:, ts, :],
                                               first_row[:, :].unsqueeze(1).broadcast_to([P, GT, E]), ALU.add))
                        link(dve.tensor_tensor(tmp8[:, ts, :, :], pick[:, ts, :, :],
                                               rank[:, ts, :].unsqueeze(2).broadcast_to([P, GT, TOPK, E]), ALU.mult))
                        link(dve.tensor_reduce(pos_f[:, ts, :], tmp8[:, ts, :, :], AX.X, ALU.add))
                        dve.tensor_copy(pos[:, :, ts], pos_f[:, ts, :].rearrange("p t k -> p k t"))\
                            .then_inc(pos_ready, 1)
                elif kind == "slot_t":
                    m = item[1]
                    wait_filled(dve, item)
                    if m >= 2:
                        wait_filled(dve, ("slot_h", m - 2))
                    dve.tensor_copy(xgT[m % 2], bank(item)[:, 0:P]).then_inc(taken, 1)
                elif kind == "slot_y":
                    m = item[1]
                    wait_filled(dve, item)
                    if m >= 3:
                        dve.wait_ge(y_out[m % 3], 16 * (m // 3))
                    dve.tensor_tensor(ysb[m % 3], bank(item)[:, 0:D], wst[m % N_W][:, X_B2:X_END], ALU.add)\
                        .then_inc(taken, 1)
                elif kind == "mix":
                    i = item[1]
                    dve.wait_ge(gathered[i], 16 * TB * TOPK)
                    for t in range(tiles(i).start, tiles(i).stop):
                        ins = dve.tensor_scalar(yk[0][:, t, :], yk[0][:, t, :], wgt[1][:, t, 0:1], None, ALU.mult)
                    link(ins)
                    for t in range(tiles(i).start, tiles(i).stop):
                        ins = dve.scalar_tensor_tensor(yk[0][:, t, :], yk[1][:, t, :], wgt[1][:, t, 1:2],
                                                       yk[0][:, t, :], ALU.mult, ALU.add)
                    ins.then_inc(mix_ready, 1)
                elif kind == "done":
                    i = item[1]
                    dve.wait_ge(mix_silu, i + 1)
                    wait_emptied(dve, ("wo1", i))
                    link(dve.tensor_tensor(s1[:, tiles(i), :], s1[:, tiles(i), :], yk[0][:, tiles(i), :], ALU.mult))
                    dve.tensor_tensor(X[:, tiles(i), :], X[:, tiles(i), :], s1[:, tiles(i), :], ALU.add)\
                        .then_inc(out_ready, 1)


def _host_layout(inputs):
    import numpy as np

    a = {k: np.asarray(v) for k, v in inputs.items()}

    def cat(*parts):
        return np.ascontiguousarray(np.concatenate(parts, axis=1))

    def chunks(w):
        c = w.shape[0] // P
        return w.reshape(c, P, -1).transpose(1, 0, 2).reshape(P, -1)

    def per_partition(v):
        return v.reshape(-1, P).T

    pack_a = cat(a["L0_attn_W_uv"], a["L0_ffn_sw1"].T, a["L0_ffn_sw3"].T, a["L0_ffn_sw2"].T,
                 chunks(a["L0_attn_W_out"]), a["L0_ffn_w_gate"].T, a["L1_ffn_gate_w"])
    w13 = np.concatenate([a["L0_ffn_w1"], a["L0_ffn_w3"]], axis=2).transpose(1, 0, 2).reshape(D, -1)
    pack_b = cat(w13, a["L1_attn_W1"], a["L1_attn_W2"], chunks(a["L1_attn_x_proj_w"]), chunks(a["L1_attn_Wo"]))
    pack_h = cat(a["L0_ffn_w2"].transpose(1, 0, 2).reshape(HID0, -1), a["L1_attn_dt_proj_w"])
    b_uv = a["L0_attn_b_uv"]
    cols = cat(per_partition(b_uv[0:GE]), per_partition(b_uv[2 * GE:]), a["L0_attn_gamma"].T, a["L0_attn_beta"].T,
               per_partition(a["L1_attn_b1"]), per_partition(a["L1_attn_b2"]), chunks(a["L1_attn_conv_w"]),
               per_partition(a["L1_attn_conv_b"]), per_partition(a["L1_attn_dt_proj_b"]),
               per_partition(a["L1_attn_D_skip"]), chunks(a["L1_attn_A_log"]))
    rows = np.ascontiguousarray(np.concatenate(
        [b_uv[GE:2 * GE], a["L0_attn_b_out"], a["L0_ffn_expert_bias"], a["L1_attn_bo"], a["L1_ffn_gate_b"]]))
    experts = np.ascontiguousarray(np.concatenate([
        a["L1_ffn_w1"],
        a["L1_ffn_w2"].reshape(E, HC, P, D).transpose(0, 2, 1, 3).reshape(E, P, HC * D),
        a["L1_ffn_b1"].reshape(E, HC, P).transpose(0, 2, 1),
        np.broadcast_to(a["L1_ffn_b2"][:, None, :], (E, P, D))], axis=2))
    x = np.ascontiguousarray(a["L0_attn_inputs"])
    return {"x": x, "pack_a": pack_a, "pack_b": pack_b, "pack_h": pack_h, "cols": cols, "rows": rows,
            "experts": experts}


def kernel(**inputs):
    import concourse.bacc as _bacc
    from concourse.bass_utils import run_bass_kernel_spmd as _run

    nc = _bacc.Bacc("TRN2", target_bir_lowering=False, num_devices=1)
    arrays = _host_layout(inputs)
    args = {n: nc.dram_tensor(n, v.shape, mybir.dt.from_np(v.dtype), kind="ExternalInput").ap()
            for n, v in arrays.items()}
    out = nc.dram_tensor("out", (NB, S, D), F32, kind="ExternalOutput").ap()
    slot_in, slot_out = ([nc.dram_tensor(f"slot_{way}{g}", (SLOTS, P, D), F32, kind="Internal").ap()
                          for g in range(NG)] for way in ("in", "out"))
    build(nc, args["x"], args["pack_a"], args["pack_b"], args["pack_h"], args["cols"], args["rows"],
          args["experts"], out, slot_in, slot_out)
    r = _run(nc, [arrays], core_ids=[0])
    return r.results[0]["out"]
```

```python
from contextlib import ExitStack

import concourse.bass as bass
from concourse import mybir

ALU = mybir.AluOpType
ACT = mybir.ActivationFunctionType
AX = mybir.AxisListType
F32 = mybir.dt.float32
BF16 = mybir.dt.bfloat16
I32 = mybir.dt.int32

EXP_LN, SILU, SIGMOID = "natural_log_exp_and_others", "silu_and_others", "sigmoid_and_others"

P = 128
NB = 4
S = 512
D = 128
TB = S // P
NT = NB * TB
E = 8
TOPK = 2
GROUPS = 4
GE = 256
HID0 = 64
MLP = 256
HV = MLP // P
NS = 16
RANK = 64
TAPS = 4
HID1 = 512
HC = HID1 // P
GROUPED = [[0, 1], [2, 3]]
NG = len(GROUPED)
GT = [TB * len(group) for group in GROUPED]
SLOTS = [n * TOPK + E - 1 for n in GT]
SLOT0 = [sum(SLOTS[:g]) for g in range(NG)]
MOST, MOST_SLOTS = max(GT), max(SLOTS)
EPS = 1e-5
BIG = 1e30

BATCHES = [2, 3, 1, 0]
LAST = NB - 1
PAIRED = {0, 1, 2, 3}
PAIRED_BY_POOL = {0, 1, 2}

A_UV, A_SW1, A_SW3, A_SW2, A_WOUT, A_GATE0, A_GATE1, A_END = (
    0, 640, 768, 896, 1024, 1280, 1288, 1296)
B_W13, B_W1, B_W2, B_XP, B_WO, B_END = 0, 1024, 1280, 1536, 1728, 1984
H_W2, H_DT, H_END = 0, E * D, E * D + MLP
C_BU, C_BB, C_GAM, C_BET, C_B1, C_B2, C_CW, C_CB, C_DTB, C_D, C_ALOG, C_END = (
    0, 2, 3, 5, 7, 9, 11, 19, 21, 23, 25, 57)
R_BV, R_BOUT, R_EB, R_BO, R_GB, R_END = 0, 256, 384, 392, 520, 528
X_W1, X_W2, X_B1, X_B2, X_END = 0, 512, 1024, 1028, 1156


SCHEDULE = """
stats.0.0 norm.0.0 xt.0.0 stats.0.1 stats.0.2 u0.0.0 norm.0.1 norm.0.2 v0.0.0 base.0 sh_gate.0 u0.0.1 v0.0.1
score.0.0 xt.0.1 score.0.1 score.0.2 sh_up.0 score.0.3 xt.0.2 logits.0.0 stats.0.3 base.1 norm.0.3 attn.0.0
attn.0.1 logits.0.1 xt.0.3 logits.0.2 sh_out.0 wout.0 logits.0.3 u0.1.0 soft_a.0.0 score.1.0 x1.0 stats.1.0
v0.1.0 v0.1.1 norm.1.0 sh_gate.1 soft_b.0.0 group.0 sh_up.1 group.1 xt.1.0 score.1.1 group.2 u1.0.0 u1.0.1
score.1.2 u0.1.1 rank.0.0.0 score.1.3 base.2 rank.0.0.1 sh_out.1 rank.0.0.2 attn.1.0 rank.0.0.3 rank.0.0.4
u1_sig.0 xproj.0 gate1.0.0 dt.0.0 pick.0.0.0 dt.0.1 pick.0.0.1 attn.1.1 count0 pairs.0 softplus.0 sh_gate.2
cast.0.0 cast.0.1 step.0.0 score.2.0 wout.1 gate1.0.1 logits.1.0 step.0.1 x1.1 cast.0.2 cast.0.3 cast.0.4
score.2.1 sum.0.0 sum.0.1 step.0.2 stats.1.1 step.0.3 step.0.4 norm.1.1 cast.0.5 sum.0.2 cast.0.6 pair_in
step.0.5 step.0.6 xt.1.1 cast.0.7 cast.0.8 step.0.7 logits.1.1 u1.1.0 u1.1.1 cast.0.9 cast.0.10 score.2.2 u0.2.0
u0.2.1 u1_sig.1 v0.2.0 v0.2.1 sum.0.3 sum.0.4 sum.0.5 step.0.8 step.0.9 cast.0.11 sh_up.2 step.0.10 score.2.3
cast.0.12 cast.0.13 step.0.11 step.0.12 pairs.1 base.3 xproj.1 sum.0.6 attn.2.0 cast.0.14 dt.1.0 attn.2.1 dt.1.1
sum.0.7 soft_a.1.0 sum.0.8 sum.0.9 step.0.13 soft_b.1.0 step.0.14 softplus.1 sh_out.2 v0.3.0 cast.0.15 cast.1.0
wout.2 oct.0 score.3.0 rank.1.0.0 sum.0.10 cast.1.1 sum.0.11 gate1.1.0 u0.3.0 sum.0.12 rank.1.0.1 score.3.1
sum.0.13 step.0.15 step.1.0 rank.1.0.2 rank.1.0.3 score.3.2 sum.0.14 rank.1.0.4 pick.1.0.0 u0.3.1 pick.1.0.1
step.1.1 x1.2 cast.1.2 rank1.0 cast.1.3 v0.3.1 pair_h.0 sum.0.15 step.1.2 stats.1.2 count1.0 score.3.3 step.1.3
route1_slots.0.0 oct.1 gate1.1.1 route1_slots.0.1 scan_out.0 oct.2 sum.1.0 norm.1.2 cast.1.4 attn.3.0 pair_h.1
sum.1.1 sum.1.2 sum.1.3 scatter.0.0 step.1.4 cast.1.5 wo1.0 cast.1.6 step.1.5 oct.3 xt.1.2 pair_h.2 step.1.6
cast.1.7 gate1.2.0 pair_h.3 u1.2.0 sum.1.4 u1.2.1 gate1.2.1 attn.3.1 pair_act.0 sum.1.5 scatter.0.1 sh_gate.3
step.1.7 cast.1.8 cast.1.9 pair_sum.0 logits.1.2 pair_h.4 pair_h.5 pair_h.6 sum.1.6 pair_h.7 sum.1.7 scatter.0.2
u1_sig.2 step.1.8 scatter.0.3 step.1.9 pair_act.1 wout.3 sh_up.3 cast.1.10 cast.1.11 pair_sum.1 step.1.10
step.1.11 xproj.2 sh_out.3 sum.1.8 dt.2.0 x1.3 cast.1.12 cast.1.13 dt.2.1 open.0 stats.1.3 sum.1.9 step.1.12
norm.1.3 step.1.13 softplus.2 cast.1.14 xt.1.3 cast.1.15 slot_t.0 logits.1.3 sum.1.10 slot_t.1 soft_a.1.1
cast.2.0 slot_h.0 sum.1.11 slot_h.1 sum.1.12 sum.1.13 step.1.14 step.1.15 slot_t.2 soft_b.1.1 rank.1.1.0
cast.2.1 slot_y.0 cast.2.2 slot_t.3 sum.1.14 slot_y.1 slot_h.2 slot_t.4 slot_h.3 slot_t.5 sum.1.15 step.2.0
step.2.1 step.2.2 cast.2.3 slot_y.2 slot_y.3 cast.2.4 step.2.3 slot_h.4 slot_t.6 slot_h.5 slot_t.7 rank.1.1.1
cast.2.5 slot_y.4 slot_h.6 scan_out.1 slot_y.5 sum.2.0 slot_t.8 slot_h.7 slot_y.6 cast.2.6 slot_h.8 sum.2.1
sum.2.2 sum.2.3 step.2.4 rank.1.1.2 step.2.5 step.2.6 sum.2.4 slot_t.9 slot_t.10 cast.2.7 slot_y.7 cast.2.8
step.2.7 slot_h.9 slot_y.8 slot_t.11 slot_h.10 step.2.8 slot_t.12 cast.2.9 rank.1.1.3 slot_y.9 slot_h.11
slot_t.13 rank.1.1.4 step.2.9 slot_y.10 slot_h.12 pick.1.1.0 slot_t.14 cast.2.10 wo1.1 pick.1.1.1 rank1.1
count1.1 slot_y.11 slot_h.13 route1_slots.1.0 slot_t.15 cast.2.11 route1_slots.1.1 slot_y.12 u1.3.0 slot_h.14
sum.2.5 sum.2.6 u1.3.1 slot_t.16 slot_y.13 slot_h.15 sum.2.7 cast.2.12 u1_sig.3 sum.2.8 gate1.3.0 scatter.1.0
slot_t.17 slot_y.14 slot_h.16 sum.2.9 slot_y.15 slot_t.18 slot_h.17 slot_y.16 slot_h.18 scatter.1.1 slot_t.19
scatter.1.2 slot_t.20 step.2.10 cast.2.13 slot_y.17 slot_y.18 sum.2.10 step.2.11 step.2.12 step.2.13 slot_h.19
slot_t.21 xproj.3 slot_h.20 slot_t.22 slot_y.19 slot_h.21 cast.2.14 slot_y.20 slot_h.22 dt.3.0 slot_y.21
slot_y.22 scatter.1.3 open.1 cast.2.15 dt.3.1 sum.2.11 softplus.3 sum.2.12 sum.2.13 step.2.14 step.2.15 cast.3.0
slot_t.23 cast.3.1 slot_t.24 sum.2.14 slot_h.23 slot_t.25 cast.3.2 slot_h.24 slot_y.23 slot_h.25 sum.2.15
step.3.0 step.3.1 step.3.2 slot_t.26 slot_t.27 slot_y.24 cast.3.3 slot_h.26 step.3.3 slot_y.25 cast.3.4
slot_t.28 slot_h.27 slot_t.29 cast.3.5 slot_y.26 slot_y.27 gather.0.0 slot_h.28 scan_out.2 slot_t.30 slot_h.29
cast.3.6 slot_y.28 step.3.4 slot_h.30 slot_t.31 slot_y.29 cast.3.7 slot_t.32 slot_y.30 slot_h.31 slot_t.33
slot_h.32 sum.3.0 sum.3.1 sum.3.2 sum.3.3 step.3.5 step.3.6 slot_y.31 slot_t.34 cast.3.8 slot_y.32 step.3.7
slot_h.33 sum.3.4 slot_h.34 step.3.8 slot_t.35 gather.1.0 cast.3.9 slot_y.33 slot_t.36 slot_y.34 slot_h.35
slot_h.36 sum.3.5 step.3.9 sum.3.6 cast.3.10 slot_t.37 slot_y.35 slot_y.36 slot_t.38 slot_h.37 slot_h.38
slot_t.39 sum.3.7 step.3.10 sum.3.8 slot_t.40 cast.3.11 slot_y.37 slot_h.39 slot_y.38 slot_t.41 cast.3.12
slot_h.40 step.3.11 slot_t.42 slot_y.39 slot_h.41 slot_y.40 cast.3.13 slot_t.43 step.3.12 slot_h.42 step.3.13
slot_y.41 slot_t.44 cast.3.14 slot_h.43 slot_y.42 slot_t.45 cast.3.15 step.3.14 slot_h.44 slot_y.43 step.3.15
slot_h.45 slot_y.44 slot_y.45 sum.3.9 sum.3.10 gather.2.0 sum.3.11 sum.3.12 mix.0 mix.1 done.0 sum.3.13 sum.3.14
gate1.3.1 sum.3.15 done.1 mix.2 scan_out.3 wo1.2 gather.3.0 done.2 wo1.3 mix.3 done.3
"""


def build_order():
    stages = []
    for word in SCHEDULE.split():
        name, *numbers = word.split(".")
        stages.append((name, *(int(n) for n in numbers)))
    return stages


CONSUMER = {
    "xt": "act", "logits": "dve", "base": "act", "u0": "act", "sh_gate": "act", "sh_up": "dve", "v0": "dve",
    "score": "act", "attn": "dve", "wout": "dve", "sh_out": "act", "pair_in": "dve", "oct": "act",
    "pair_h": "dve", "pair_sum": "dve", "u1": "act", "gate1": "act", "xproj": "act", "dt": "act", "wo1": "dve",
    "rank1": "dve", "count0": "dve", "count1": "dve", "slot_t": "act", "slot_h": "act", "slot_y": "dve",
}
BANKS = 4
N_SET, N_MADE = 15, 7


def build(nc, x, pack_a, pack_b, pack_h, cols, rows, experts, out, slot_in, slot_out, c_rows):
    order = build_order()
    jobs = [item for item in order if item[0] in CONSUMER]
    job_at = {item: n for n, item in enumerate(jobs)}
    emptied_at, so_far = {}, {"act": 0, "dve": 0}
    for item in jobs:
        so_far[CONSUMER[item[0]]] += 1
        emptied_at[item] = so_far[CONSUMER[item[0]]]

    x_v = x.rearrange("b (t p) d -> p (b t) d", p=P)
    out_v = out.rearrange("b (t p) d -> p (b t) d", p=P)

    with ExitStack() as ctx:
        def sb(name, shape, dt=F32):
            return ctx.enter_context(nc.sbuf_tensor(name, shape, dt))

        def sem(name):
            return ctx.enter_context(nc.semaphore(name))

        wa = sb("wa", [P, A_END])
        wb = sb("wb", [P, B_END])
        wh = sb("wh", [HID0, H_END])
        col = sb("col", [P, C_END])
        row = sb("row", [P, R_END])
        ident = sb("ident", [P, P])
        pick_state = sb("pick_state", [3 * 2 * NS, NS], BF16)
        upper = sb("upper", [P, P], BF16)
        ones = sb("ones", [P, P], BF16)
        before4 = sb("before4", [P, GROUPS, GROUPS], BF16)
        before8 = sb("before8", [P, E, E], BF16)
        row_no = sb("row_no", [P, NT, TOPK])
        mult128 = sb("mult128", [P, MOST])
        slot_no = sb("slot_no", [P, MOST_SLOTS])
        neg_a = sb("neg_a", [P, HV, NS])

        X = sb("X", [P, NT, D])
        XN = sb("XN", [P, NT, D])
        XNT = sb("XNT", [P, NT * P])
        XNT1 = sb("XNT1", [P, S])
        stat = sb("stat", [P, TB, 6])
        mv = sb("mv", [P, NT, 2])
        veps = sb("veps", [P, NT])
        rstd = sb("rstd", [P, NT])

        early = sb("early", [P, 5 * S])
        base, qT, sh_h = (early[:, n * S:(n + 1) * S] for n in range(3))
        s0, g0 = (early[:, n * S:(n + 1) * S].rearrange("p (t d) -> p t d", t=TB) for n in (3, 4))
        kT = base
        uv = sb("uv", [P, 4 * S])
        uT = uv[:, 0:2 * S].rearrange("p (h t) -> p h t", h=2)
        v = uv[:, 2 * S:4 * S].rearrange("p (t e) -> p t e", t=TB)
        sq = sb("sq", [P, TB, S])

        upad = sb("upad", [P, HV, TAPS - 1 + S])
        u1 = sb("u1", [P, 2, HV, S])
        g1 = sb("g1", [P, 2, HV, S])
        dtT = sb("dtT", [RANK, S])
        bc = sb("bc", [2 * NS, S])
        bc_mid = sb("bc_mid", [NS, S], BF16)
        bcs = sb("bcs", [3 * 2 * NS, 2, S], BF16)
        delta = sb("delta", [P, 2, HV, S])
        du = sb("du", [P, 2, HV, S])
        N_DA, N_CS, N_RING = 3, 4, 8
        decay = sb("decay", [P, N_DA, HV, S])
        ring = sb("ring", [P, N_RING, HV, S])
        cs = sb("cs", [P, N_CS, S])
        s1 = XNT[:, :].rearrange("p (t d) -> p t d", t=NT)

        lg = sb("lg", [P, 2, NT, E])
        sc = sb("sc", [P, NT, E])
        sel_s = sb("sel_s", [P, NT, E])
        red = sb("red", [P, NT])
        red2 = sb("red2", [P, NT])
        grp = sb("grp", [P, NT, GROUPS])
        keep = sb("keep", [P, NT, GROUPS])
        cmp_a = sb("cmp_a", [P, NT, E, E], BF16)
        cmp_b = sb("cmp_b", [P, NT, E, E], BF16)
        rank = sb("rank", [P, NT, E])
        pick = sb("pick", [P, NT, TOPK, E])
        picked0 = sb("picked0", [P, NT, E], BF16)
        padded = sb("padded", [P, 2 * MOST - 1, E], BF16)
        picked1 = padded[:, MOST - 1:, :]
        tmp8 = sb("tmp8", [P, NT, TOPK, E])
        wgt = [sb(f"wgt{n}", [P, NT, TOPK]) for n in range(2)]
        cnt = sb("cnt", [P, E])
        cum = sb("cum", [P, E + 1])
        ge = sb("ge", [P, NT * TOPK, E + 1])
        seg = sb("seg", [P, NT * TOPK, E])
        ab = sb("ab", [P, TOPK, P])
        ntile = sb("ntile", [P, E])
        cmp_f = cmp_a[:, :, :, :].rearrange("p t i j -> p (t i j)").bitcast(F32)
        cmp_t = cmp_f[:, 0:E * MOST].rearrange("p (e t) -> p e t", e=E)
        ctile = sb("ctile", [P, E])
        first_row = sb("first_row", [P, E])
        cmp_s = cmp_f[:, E * MOST:E * (MOST + MOST_SLOTS)].rearrange("p (s e) -> p s e", e=E)
        slot_f = sb("slot_f", [P, MOST_SLOTS])
        slot_e = sb("slot_e", [P, sum(SLOTS)], I32)
        pos_f = sb("pos_f", [P, NT, TOPK])
        pos = sb("pos", [P, TOPK, NT], I32)

        PAIR = NT * TOPK * HID0
        N_W, N_X = 5, 8
        REGION = 3 * PAIR + D
        region = sb("region", [P, REGION])
        pair = region[:, 0:PAIR].rearrange("p (t k c) -> p t k c", t=NT, k=TOPK)
        pairT = region[:, PAIR:2 * PAIR]
        gate0 = region[:, PAIR:PAIR + PAIR // 2].rearrange("p (j c) -> p j c", c=HID0)
        ph = region[:, 2 * PAIR:3 * PAIR].rearrange("p (j c) -> p j c", c=2 * HID0)
        xm = region[:, 2 * PAIR:2 * PAIR + E * (P + 1)]
        htp = sq[0:HID0, 0:2, :].rearrange("p m t -> p (m t)").rearrange("p (g c) -> p g c", g=E)
        at = 0

        def part(n):
            nonlocal at
            at += n
            return region[:, at - n:at]

        wst = [early[:, n * X_END:(n + 1) * X_END] for n in range(2)] + [part(X_END) for _ in range(N_W - 2)]
        xg = [part(D) for _ in range(N_X)]
        xgT = [part(D) for _ in range(2)]
        hT = [part(HC * P).rearrange("p (c t) -> p c t", c=HC) for _ in range(2)]
        ysb = [part(D) for _ in range(3)]
        assert at <= REGION
        yk = [sq[:, :, :].rearrange("p m t -> p (m t)").rearrange("p (t d) -> p t d", t=NT),
              uv[:, :].rearrange("p (t d) -> p t d", t=NT)]

        work = [ctx.enter_context(nc.psum_tensor(f"work{n}", [P, S], F32)) for n in range(BANKS)]
        p_b = [ctx.enter_context(nc.psum_tensor(f"p_b{n}", [P, S], F32)) for n in range(2)]
        p_y = [ctx.enter_context(nc.psum_tensor(f"p_y{h}", [P, S], F32)) for h in range(HV)]

        x_in = [sem(f"x_in{i}") for i in range(NB)]
        wa_in, wb_in, wh_in, col_in, row_in = (sem(n) for n in ("wa_in", "wb_in", "wh_in", "col_in", "row_in"))
        const_set, const_made = sem("const_set"), sem("const_made")
        slots_zeroed = sem("slots_zeroed")
        a_ready, a_negated = sem("a_ready"), sem("a_negated")
        filled = sem("filled")
        emptied = {"act": sem("emptied_by_act"), "dve": sem("emptied_by_dve")}
        dve_step, act_step = sem("dve_step"), sem("act_step")
        var_ready, rstd_ready, xn_ready = sem("var_ready"), sem("rstd_ready"), sem("xn_ready")
        qk_ready, v_ready, sq_ready = sem("qk_ready"), sem("v_ready"), sem("sq_ready")
        x1_done = sem("x1_done")
        tap_ready, conv_ready, u1_ready = sem("tap_ready"), sem("conv_ready"), sem("u1_ready")
        bcs_ready = sem("bcs_ready")
        l_ready, du_ready = sem("l_ready"), sem("du_ready")
        c_out = sem("c_out")
        cs_in = [sem(f"cs_in{n}") for n in range(N_CS)]
        b_cast, decay_ready = sem("b_cast"), sem("decay_ready")
        drive_ready, state_ready, prod_ready, summed = (
            sem("drive_ready"), sem("state_ready"), sem("prod_ready"), sem("summed"))
        y_read, y_ready = sem("y_read"), sem("y_ready")
        soft_in, soft_exp = sem("soft_in"), sem("soft_exp")
        picked_ready = sem("picked_ready")
        xm_ready, pair_ready = sem("xm_ready"), sem("pair_ready")
        pair_sig, pair_out = sem("pair_sig"), sem("pair_out")
        pos_ready = sem("pos_ready")
        paired = sem("paired")
        scattered = [sem(f"scattered{g}") for g in range(NG)]
        w_in = [sem(f"w_in{n}") for n in range(N_W)]
        xg_in = [sem(f"xg_in{n}") for n in range(N_X)]
        y_out = [sem(f"y_out{n}") for n in range(3)]
        gathered = [sem(f"gathered{i}") for i in range(NB)]
        mix_ready, mix_silu, out_ready, stored = sem("mix_ready"), sem("mix_silu"), sem("out_ready"), sem("stored")

        def bank(item):
            return work[job_at[item] % BANKS]

        def wait_filled(eng, *items):
            eng.wait_ge(filled, max(job_at[item] for item in items) + 1)

        def wait_emptied(eng, item):
            eng.wait_ge(emptied[CONSUMER[item[0]]], emptied_at[item])

        def tiles(i):
            b = BATCHES[i]
            return slice(b * TB, (b + 1) * TB)

        def tokens(i):
            b = BATCHES[i]
            return slice(b * S, (b + 1) * S)

        def step_no(i, n):
            return i * NS + n

        def sums_upto(g):
            return sum(1 for k in range(g + 1) if k // NS not in PAIRED or k % 2)

        def pairs_upto(g):
            return sum(1 for k in range(g + 1) if k // NS in PAIRED and k % 2)

        def group_tiles(g):
            first = min(tiles(i).start for i in GROUPED[g])
            return slice(first, first + GT[g])

        def group_of(i):
            return next(g for g in range(NG) if i in GROUPED[g])

        def place(m):
            g = max(g for g in range(NG) if SLOT0[g] <= m)
            return g, m - SLOT0[g]

        def add_pair(eng, item):
            _, i, n = item
            if n % 2:
                g = step_no(i, n)
                eng.wait_ge(prod_ready, g + 1)
                eng.tensor_tensor(ring[:, g % N_RING], ring[:, g % N_RING], ring[:, (g - 1) % N_RING], ALU.add)\
                    .then_inc(paired, 1)

        softmaxes = {(0, 0): 0, (1, 0): 1, (1, 1): 2}

        block = ctx.enter_context(nc.Block())

        @block.sync
        def _(sp):
            for i in range(NB):
                sp.dma_start(X[:, tiles(i), :], x_v[:, tiles(i), :]).then_inc(x_in[i], 16)
                if i == 0:
                    sp.dma_start(wa[:, :], pack_a).then_inc(wa_in, 16)
            sp.dma_start(wb[:, :], pack_b).then_inc(wb_in, 16)
            sp.wait_ge(const_set, 2)
            for g in range(NG):
                sp.dma_start(slot_in[g].rearrange("s p d -> p s d"),
                             region[:, 0:D].unsqueeze(1).broadcast_to([P, SLOTS[g], D])).then_inc(slots_zeroed, 16)

            def load_weights(m):
                if m >= N_W:
                    wait_emptied(sp, ("slot_y", m - N_W))
                which = sp.value_load(slot_e[0:1, m:m + 1], min_val=0, max_val=E - 1)
                sp.dma_start(wst[m % N_W], experts[bass.ds(which, 1), :, :].rearrange("e p f -> (e p) f"))\
                    .then_inc(w_in[m % N_W], 16)

            def spread_c(i, n):
                g = step_no(i, n)
                if n == 0:
                    sp.wait_ge(c_out, 16 * (i + 1))
                if g >= N_CS:
                    sp.wait_ge(prod_ready, g - N_CS + 1)
                sp.dma_start(cs[:, g % N_CS, :], c_rows[i, n].partition_broadcast(P)).then_inc(cs_in[g % N_CS], 16)

            def load_rows(m):
                if m >= N_X:
                    wait_filled(sp, ("slot_t", m - N_X))
                g, k = place(m)
                sp.dma_start(xg[m % N_X], slot_in[g][k]).then_inc(xg_in[m % N_X], 16)

            for item in order:
                kind, m = item[0], item[-1]
                if kind == "xproj":
                    wait_emptied(sp, item)
                    sp.dma_start(c_rows[m], bc[NS:2 * NS, :]).then_inc(c_out, 16)
                elif kind == "cast" and m < 2:
                    spread_c(item[1], m)
                elif kind == "step" and m < NS - 2:
                    spread_c(item[1], m + 2)
                if kind == "open":
                    if m == 0:
                        sp.wait_ge(x1_done, NB)
                    sp.wait_ge(pos_ready, m + 1)
                    for k in range(N_W):
                        load_weights(SLOT0[m] + k)
                    sp.wait_ge(scattered[m], 16 * GT[m] * TOPK)
                    for k in range(N_X):
                        load_rows(SLOT0[m] + k)
                elif kind == "slot_y":
                    g, k = place(m)
                    end = SLOT0[g] + SLOTS[g]
                    wait_emptied(sp, item)
                    if m + N_W < end:
                        load_weights(m + N_W)
                    if m + N_X < end:
                        load_rows(m + N_X)
                    sp.dma_start(slot_out[g][k], ysb[m % 3]).then_inc(y_out[m % 3], 16)
                elif kind == "done":
                    sp.wait_ge(out_ready, m + 1)
                    sp.dma_start(out_v[:, tiles(m), :], X[:, tiles(m), :]).then_inc(stored, 16)
            sp.wait_ge(stored, 16 * NB)

        @block.gpsimd
        def _(pool):
            pool.memset(ident[:, :], 0.0).then_inc(const_set, 1)
            pool.wait_ge(const_set, 1)
            pool.affine_select(out=ident[:, :], in_=ident[:, :], compare_op=ALU.not_equal, fill=1.0, base=0,
                               pattern=[[-1, P]], channel_multiplier=1).then_inc(const_made, 1)
            pool.memset(region[:, 0:D], 0.0).then_inc(const_set, 1)
            for t, value in ((ones[:, :], 1.0), (upad[:, :, 0:TAPS - 1], 0.0), (decay[:, :, :, 0:1], 0.0),
                             (before4[:, :, :], 1.0), (before8[:, :, :], 1.0), (pick_state[:, :], 0.0), (bcs[:, :, :], 0.0),
                             (padded[:, 0:MOST - 1, :], 0.0),
                             (xm, 0.0), (ab[:, :, :], 0.0)):
                pool.memset(t, value).then_inc(const_set, 1)
            for t, pattern, step in ((row_no[:, :, :], [[2 * P, NT], [1, TOPK]], 2), (mult128[:, :], [[P, MOST]], 0),
                                     (slot_no[:, :], [[1, MOST_SLOTS]], 0)):
                pool.iota(t, pattern, base=0, channel_multiplier=step, allow_small_or_imprecise_dtypes=True)\
                    .then_inc(const_set, 1)
            pool.wait_ge(const_set, N_SET)
            pool.affine_select(out=upper[:, :], in_=ones[:, :], compare_op=ALU.is_gt, fill=0.0, base=0,
                               pattern=[[1, P]], channel_multiplier=-1).then_inc(const_made, 1)
            for m, n in ((before4, GROUPS), (before8, E)):
                pool.affine_select(out=m[:, :, :], in_=m[:, :, :], compare_op=ALU.is_gt, fill=0.0, base=0,
                                   pattern=[[1, n], [-1, n]], channel_multiplier=0).then_inc(const_made, 1)
            for j in range(3):
                pool.wait_ge(const_made, 4 + j)
                m = pick_state[2 * NS * j:2 * NS * (j + 1), :]
                pool.affine_select(out=m, in_=m, compare_op=ALU.not_equal, fill=1.0, base=0,
                                   pattern=[[-1, NS]], channel_multiplier=1).then_inc(const_made, 1)

            for item in order:
                kind = item[0]
                if kind == "step":
                    _, i, n = item
                    g = step_no(i, n)
                    pool.wait_ge(state_ready, g + 1)
                    pool.wait_ge(cs_in[g % N_CS], 16 * (g // N_CS + 1))
                    c = cs[:, g % N_CS, :].unsqueeze(1).broadcast_to([P, HV, S])
                    pool.tensor_tensor(ring[:, g % N_RING], ring[:, g % N_RING], c, ALU.mult)\
                        .then_inc(prod_ready, 1)
                elif kind == "sum" and item[1] in PAIRED & PAIRED_BY_POOL:
                    add_pair(pool, item)
                elif kind == "scatter":
                    _, g, q = item
                    if q == 0:
                        pool.wait_ge(pos_ready, g + 1)
                        pool.wait_ge(slots_zeroed, 16 * NG)
                        pool.wait_ge(xn_ready, NB + GROUPED[g][-1] + 1)
                    for t in range(group_tiles(g).start + 2 * q, group_tiles(g).start + 2 * q + 2):
                        for k in range(TOPK):
                            pool.indirect_dma_start(slot_in[g].rearrange("s p d -> (s p) d"),
                                                    bass.IndirectOffsetOnAxis(ap=pos[:, k, t:t + 1], axis=0),
                                                    XN[:, t, :], None).then_inc(scattered[g], 16)
                elif kind == "gather":
                    i = item[1]
                    g = group_of(i)
                    end = SLOT0[g] + SLOTS[g]
                    for n in range(3):
                        pool.wait_ge(y_out[n], 16 * len(range(n, end, 3)))
                    for t in range(tiles(i).start, tiles(i).stop):
                        for k in range(TOPK):
                            pool.indirect_dma_start(yk[k][:, t, :], None,
                                                    slot_out[g].rearrange("s p d -> (s p) d"),
                                                    bass.IndirectOffsetOnAxis(ap=pos[:, k, t:t + 1], axis=0))\
                                .then_inc(gathered[i], 16)

        @block.scalar
        def _(act):
            steps = 0

            def link(ins):
                nonlocal steps
                steps += 1
                ins.then_inc(act_step, 1)
                act.wait_ge(act_step, steps)

            held = None

            def table(name):
                nonlocal held
                if held != name:
                    act.preload_act_table_set(name)
                    held = name

            act.dma_start(col[:, :], cols).then_inc(col_in, 16)
            act.dma_start(row[:, :], rows.partition_broadcast(P)).then_inc(row_in, 16)
            act.dma_start(wh[:, :], pack_h).then_inc(wh_in, 16)
            table(EXP_LN)
            act.wait_ge(col_in, 16)
            act.activation(neg_a[:, :, :], col[:, C_ALOG:C_END].rearrange("p (h n) -> p h n", h=HV), ACT.Exp)\
                .then_inc(a_ready, 1)

            for item in order:
                kind = item[0]
                taken = emptied["act"]
                if kind == "stats":
                    _, l, i = item
                    act.wait_ge(var_ready, l * NB + i + 1)
                    table(EXP_LN)
                    link(act.activation(rstd[:, tiles(i)], veps[:, tiles(i)], ACT.Ln))
                    act.activation(rstd[:, tiles(i)], rstd[:, tiles(i)], ACT.Exp, scale=-0.5).then_inc(rstd_ready, 1)
                elif kind == "xt":
                    _, l, i = item
                    wait_filled(act, item)
                    if l == 0:
                        act.activation(XNT[:, tokens(i)], bank(item)[:, :], ACT.Copy).then_inc(taken, 1)
                    else:
                        if i:
                            wait_filled(act, ("logits", 1, i - 1), ("u1", i - 1, 1), ("gate1", i - 1, 1))
                        act.activation(XNT1[:, :], bank(item)[:, :], ACT.Copy).then_inc(taken, 1)
                elif kind == "base":
                    i = item[1]
                    wait_filled(act, item)
                    if i:
                        wait_filled(act, ("score", i - 1, TB - 1))
                    table(SILU)
                    act.activation(base[:, :], bank(item)[:, :], ACT.Silu, bias=col[:, C_BB:C_BB + 1])\
                        .then_inc(taken, 1)
                elif kind == "u0":
                    _, i, h = item
                    wait_filled(act, item)
                    if i:
                        wait_filled(act, ("wout", i - 1))
                    table(SILU)
                    act.activation(uT[:, h, :], bank(item)[:, :], ACT.Silu, bias=col[:, C_BU + h:C_BU + h + 1])\
                        .then_inc(taken, 1)
                elif kind == "sh_gate":
                    i = item[1]
                    wait_filled(act, item)
                    if i:
                        wait_filled(act, ("sh_out", i - 1))
                    table(SILU)
                    act.activation(sh_h[:, :], bank(item)[:, :], ACT.Silu).then_inc(taken, 1)
                elif kind == "v0":
                    _, i, j = item
                    wait_emptied(act, item)
                    table(SILU)
                    act.activation(v[:, 2 * j:2 * j + 2, :], v[:, 2 * j:2 * j + 2, :], ACT.Silu).then_inc(v_ready, 1)
                elif kind == "score":
                    _, i, m = item
                    wait_filled(act, item)
                    if i:
                        wait_filled(act, ("attn", i - 1, 1))
                    act.activation(sq[:, m, :], bank(item)[:, :], ACT.Relu, scale=1.0 / S).then_inc(taken, 1)
                    wait_emptied(act, item)
                    act.activation(sq[:, m, :], sq[:, m, :], ACT.Square).then_inc(sq_ready, 1)
                elif kind == "sh_out":
                    i = item[1]
                    wait_filled(act, item)
                    if i:
                        act.wait_ge(x1_done, i)
                    table(SILU)
                    act.activation(g0[:, :, :], bank(item)[:, :].rearrange("p (t d) -> p t d", t=TB), ACT.Silu)\
                        .then_inc(taken, 1)
                elif kind == "soft_a":
                    _, l, g = item
                    ts = group_tiles(g) if l else slice(0, NT)
                    act.wait_ge(soft_in, softmaxes[l, g] + 1)
                    table(EXP_LN)
                    act.activation(sc[:, ts, :], lg[:, l, ts, :], ACT.Exp).then_inc(soft_exp, 1)
                elif kind == "oct":
                    q = item[1]
                    wait_filled(act, item)
                    act.activation(pairT[:, q * S:(q + 1) * S], bank(item)[:, :], ACT.Copy).then_inc(taken, 1)
                elif kind == "pair_act":
                    n = item[1]
                    wait_emptied(act, ("pair_h", (n + 1) * NT // 4 - 1))
                    if n:
                        act.wait_ge(pair_out, n)
                    table(SILU)
                    act.activation(gate0, ph[:, :, 0:HID0], ACT.Silu).then_inc(pair_sig, 1)
                elif kind == "u1":
                    _, i, h = item
                    wait_filled(act, item)
                    if i:
                        act.wait_ge(conv_ready, 2 * (i - 1) + h + 1)
                    act.activation(upad[:, h, TAPS - 1:], bank(item)[:, :], ACT.Identity,
                                   bias=col[:, C_B1 + h:C_B1 + h + 1]).then_inc(taken, 1)
                    wait_emptied(act, item)
                    if i >= 2:
                        wait_filled(act, ("wo1", i - 2))
                    act.activation(u1[:, i % 2, h, :], upad[:, h, TAPS - 1:], ACT.Identity,
                                   scale=col[:, C_CW + TAPS * (h + 1) - 1:C_CW + TAPS * (h + 1)],
                                   bias=col[:, C_CB + h:C_CB + h + 1]).then_inc(tap_ready, 1)
                elif kind == "gate1":
                    _, i, h = item
                    wait_filled(act, item)
                    if i >= 2:
                        act.wait_ge(y_ready, i - 1)
                    table(SIGMOID)
                    act.activation(g1[:, i % 2, h, :], bank(item)[:, :], ACT.Sigmoid,
                                   bias=col[:, C_B2 + h:C_B2 + h + 1]).then_inc(taken, 1)
                elif kind == "u1_sig":
                    i = item[1]
                    act.wait_ge(conv_ready, 2 * i + 2)
                    table(SIGMOID)
                    act.activation(u1[:, i % 2], u1[:, i % 2], ACT.Sigmoid).then_inc(u1_ready, 1)
                elif kind == "xproj":
                    i = item[1]
                    wait_filled(act, item)
                    if i:
                        wait_filled(act, ("dt", i - 1, 1))
                        act.wait_ge(bcs_ready, i)
                        act.wait_ge(c_out, 16 * i)
                    act.activation(dtT[:, :], bank(item)[0:RANK, :], ACT.Copy)
                    act.activation(bc[:, :], bank(item)[RANK:RANK + 2 * NS, :], ACT.Copy).then_inc(taken, 1)
                elif kind == "dt":
                    _, i, h = item
                    wait_filled(act, item)
                    if i >= 2:
                        act.wait_ge(drive_ready, step_no(i - 1, 0))
                    act.activation(delta[:, i % 2, h, :], bank(item)[:, :], ACT.Identity,
                                   bias=col[:, C_DTB + h:C_DTB + h + 1])
                    act.activation(du[:, i % 2, h, :], bank(item)[:, :], ACT.Abs,
                                   bias=col[:, C_DTB + h:C_DTB + h + 1]).then_inc(taken, 1)
                elif kind == "softplus":
                    i = item[1]
                    table(EXP_LN)
                    wait_emptied(act, ("dt", i, 1))
                    link(act.activation(du[:, i % 2], du[:, i % 2], ACT.Exp, scale=-1.0))
                    act.activation(du[:, i % 2], du[:, i % 2], ACT.Ln, bias=1.0).then_inc(l_ready, 1)
                elif kind == "cast":
                    _, i, n = item
                    g = step_no(i, n)
                    table(EXP_LN)
                    if n == 0:
                        act.wait_ge(du_ready, i + 1)
                    if g >= N_DA:
                        act.wait_ge(state_ready, g - N_DA + 1)
                    if g == 0:
                        act.wait_ge(a_negated, 1)
                    for h in range(HV):
                        ins = act.activation(decay[:, g % N_DA, h, 1:S], delta[:, i % 2, h, 1:S], ACT.Exp,
                                             scale=neg_a[:, h, n:n + 1])
                    ins.then_inc(decay_ready, 1)
                elif kind == "slot_t":
                    m = item[1]
                    wait_filled(act, item)
                    if m >= 2:
                        wait_filled(act, ("slot_h", m - 2))
                    act.activation(xgT[m % 2], bank(item)[:, 0:P], ACT.Copy).then_inc(taken, 1)
                elif kind == "slot_h":
                    m = item[1]
                    wait_filled(act, item)
                    if m >= 2:
                        wait_filled(act, ("slot_y", m - 2))
                    for c in range(HC):
                        ins = act.activation(hT[m % 2][:, c, :], bank(item)[:, c * P:(c + 1) * P], ACT.Relu,
                                             bias=wst[m % N_W][:, X_B1 + c:X_B1 + c + 1])
                    ins.then_inc(taken, 1)
                elif kind == "mix":
                    i = item[1]
                    act.wait_ge(mix_ready, i + 1)
                    table(SILU)
                    act.activation(yk[0][:, tiles(i), :], yk[0][:, tiles(i), :], ACT.Silu).then_inc(mix_silu, 1)

        @block.tensor
        def _(pe):
            pe.wait_ge(const_made, 1)
            here = set()

            def need(*loads):
                for load in loads:
                    if load not in here:
                        pe.wait_ge(load, 16)
                        here.add(load)

            for item in order:
                kind = item[0]
                if kind in CONSUMER:
                    n = job_at[item]
                    if n >= BANKS:
                        wait_emptied(pe, jobs[n - BANKS])
                    dst = bank(item)
                if kind == "xt":
                    _, l, i = item
                    pe.wait_ge(xn_ready, l * NB + i + 1)
                    for t in range(TB):
                        ins = pe.transpose(dst[:, t * P:(t + 1) * P], XN[:, tiles(i).start + t, :], ident[:, :])
                    ins.then_inc(filled, 1)
                elif kind == "logits":
                    _, l, i = item
                    wait_emptied(pe, ("xt", l, i))
                    need(wa_in)
                    wg = wa[:, A_GATE1:A_END] if l else wa[:, A_GATE0:A_GATE1]
                    for t in range(TB):
                        lhs = XNT1[:, t * P:(t + 1) * P] if l else \
                            XNT[:, tokens(i).start + t * P:tokens(i).start + (t + 1) * P]
                        ins = pe.matmul(dst[:, t * E:(t + 1) * E], lhs, wg, start=True, stop=True)
                    ins.then_inc(filled, 1)
                elif kind in ("base", "u0", "sh_gate", "sh_up"):
                    i = item[1]
                    need(wa_in)
                    wait_emptied(pe, ("xt", 0, i))
                    at_col = {"base": A_UV + 2 * GE, "u0": A_UV + P * item[-1], "sh_gate": A_SW1, "sh_up": A_SW3}[kind]
                    pe.matmul(dst[:, :], wa[:, at_col:at_col + P], XNT[:, tokens(i)], start=True, stop=True)\
                        .then_inc(filled, 1)
                elif kind == "v0":
                    _, i, j = item
                    need(wa_in)
                    wait_emptied(pe, ("xt", 0, i))
                    for t in range(2):
                        tok = tokens(i).start + (2 * j + t) * P
                        ins = pe.matmul(dst[:, t * GE:(t + 1) * GE], XNT[:, tok:tok + P], wa[:, A_UV + GE:A_UV + 2 * GE],
                                        start=True, stop=True)
                    ins.then_inc(filled, 1)
                elif kind == "score":
                    _, i, m = item
                    pe.wait_ge(qk_ready, i + 1)
                    pe.matmul(dst[:, :], kT[:, m * P:(m + 1) * P], qT[:, :], start=True, stop=True)\
                        .then_inc(filled, 1)
                elif kind == "attn":
                    _, i, h = item
                    pe.wait_ge(v_ready, 2 * (i + 1))
                    for m in range(TB):
                        if h == 0:
                            pe.wait_ge(sq_ready, TB * i + m + 1)
                        ins = pe.matmul(dst[:, :], v[:, m, h * P:(h + 1) * P], sq[:, m, :],
                                        start=(m == 0), stop=(m == TB - 1))
                    ins.then_inc(filled, 1)
                elif kind == "wout":
                    i = item[1]
                    wait_emptied(pe, ("attn", i, 1))
                    for t in range(TB):
                        for h in range(2):
                            ins = pe.matmul(dst[:, t * D:(t + 1) * D], uT[:, h, t * P:(t + 1) * P],
                                            wa[:, A_WOUT + h * D:A_WOUT + (h + 1) * D], start=(h == 0), stop=(h == 1))
                    ins.then_inc(filled, 1)
                elif kind == "sh_out":
                    i = item[1]
                    wait_emptied(pe, ("sh_up", i))
                    if i == LAST:
                        wait_emptied(pe, ("pair_sum", 1))
                    for t in range(TB):
                        routed = i == LAST and t == 0
                        ins = pe.matmul(dst[:, t * D:(t + 1) * D], sh_h[:, t * P:(t + 1) * P],
                                        wa[:, A_SW2:A_SW2 + D], start=True, stop=not routed)
                        if routed:
                            need(wh_in)
                            for g in range(E):
                                ins = pe.matmul(dst[:, 0:D], htp[:, g, :], wh[:, H_W2 + g * D:H_W2 + (g + 1) * D],
                                                start=False, stop=(g == E - 1))
                    ins.then_inc(filled, 1)
                elif kind == "pair_in":
                    need(wb_in)
                    pe.wait_ge(xm_ready, 1)
                    for g in range(E):
                        ins = pe.matmul(dst[:, 0:P], xm[:, g * P:(g + 1) * P], wb[:, B_W13 + g * P:B_W13 + (g + 1) * P],
                                        start=(g == 0), stop=(g == E - 1))
                    ins.then_inc(filled, 1)
                elif kind == "count0":
                    pe.wait_ge(picked_ready, 1)
                    for t in range(NT):
                        ins = pe.matmul(dst[:, 0:E], ones[:, :], picked0[:, t, :], start=(t == 0), stop=(t == NT - 1))
                    ins.then_inc(filled, 1)
                elif kind == "oct":
                    q = item[1]
                    pe.wait_ge(pair_ready, 1)
                    for t in range(4):
                        ins = pe.transpose(dst[:, t * P:(t + 1) * P],
                                           pair[:, 4 * q + t, :, :].rearrange("p k c -> p (k c)"), ident[:, :])
                    ins.then_inc(filled, 1)
                elif kind == "pair_h":
                    q = item[1]
                    wait_emptied(pe, ("oct", q // 2))
                    wait_emptied(pe, ("pair_in",))
                    for t in range(2):
                        tok = (2 * q + t) * P
                        ins = pe.matmul(dst[:, t * 2 * P:(t + 1) * 2 * P], pairT[:, tok:tok + P],
                                        ab[:, :, :].rearrange("p k c -> p (k c)"), start=True, stop=True)
                    ins.then_inc(filled, 1)
                elif kind == "pair_sum":
                    n = item[1]
                    pe.wait_ge(pair_out, n + 1)
                    for j in range(NT):
                        ins = pe.matmul(dst[0:HID0, 0:E * E], ph[:, j, HID0:2 * HID0],
                                        pair[:, n * NT // 2 + j // TOPK, j % TOPK, :],
                                        start=(j == 0), stop=(j == NT - 1))
                    ins.then_inc(filled, 1)
                elif kind in ("u1", "gate1"):
                    _, i, h = item
                    need(wb_in)
                    wait_emptied(pe, ("xt", 1, i))
                    at_col = (B_W1 if kind == "u1" else B_W2) + h * P
                    pe.matmul(dst[:, :], wb[:, at_col:at_col + P], XNT1[:, :], start=True, stop=True)\
                        .then_inc(filled, 1)
                elif kind == "xproj":
                    i = item[1]
                    pe.wait_ge(u1_ready, i + 1)
                    n_out = RANK + 2 * NS
                    for h in range(HV):
                        ins = pe.matmul(dst[0:n_out, :], wb[:, B_XP + h * n_out:B_XP + (h + 1) * n_out],
                                        u1[:, i % 2, h, :], start=(h == 0), stop=(h == HV - 1))
                    ins.then_inc(filled, 1)
                elif kind == "dt":
                    _, i, h = item
                    need(wh_in)
                    wait_emptied(pe, ("xproj", i))
                    pe.matmul(dst[:, :], wh[:, H_DT + h * P:H_DT + (h + 1) * P], dtT[:, :], start=True, stop=True)\
                        .then_inc(filled, 1)
                elif kind == "cast":
                    _, i, n = item
                    g = step_no(i, n)
                    if g == 0:
                        pe.wait_ge(const_made, N_MADE)
                    if n == 0:
                        pe.wait_ge(bcs_ready, i + 1)
                    if g >= 2:
                        pe.wait_ge(drive_ready, g - 1)
                    pe.matmul(p_b[g % 2][:, :], pick_state[:, n:n + 1].broadcast_to([3 * 2 * NS, P]),
                              bcs[:, i % 2, :], start=True, stop=True).then_inc(b_cast, 1)
                elif kind == "sum":
                    _, i, n = item
                    g = step_no(i, n)
                    if i in PAIRED and n % 2 == 0:
                        continue
                    if n <= 1 and i:
                        pe.wait_ge(y_read, i)
                    if i in PAIRED:
                        pe.wait_ge(paired, pairs_upto(g))
                    else:
                        pe.wait_ge(prod_ready, g + 1)
                    for h in range(HV):
                        ins = pe.matmul(p_y[h][:, :], ident[:, :], ring[:, g % N_RING, h, :],
                                        start=(n <= 1 and (i in PAIRED or n == 0)), stop=(n == NS - 1))
                    ins.then_inc(summed, 1)
                elif kind == "wo1":
                    i = item[1]
                    pe.wait_ge(y_ready, i + 1)
                    for t in range(TB):
                        for h in range(HV):
                            ins = pe.matmul(dst[:, t * D:(t + 1) * D], u1[:, i % 2, h, t * P:(t + 1) * P],
                                            wb[:, B_WO + h * D:B_WO + (h + 1) * D], start=(h == 0), stop=(h == HV - 1))
                    ins.then_inc(filled, 1)
                elif kind == "rank1":
                    pe.wait_ge(picked_ready, item[1] + 2)
                    n = GT[item[1]]
                    for back in range(n):
                        tiles_before = padded[:, MOST - 1 - back:MOST - 1 - back + n, :].rearrange("p t e -> p (t e)")
                        ins = pe.matmul(dst[:, 0:n * E], ones[:, :] if back else upper[:, :], tiles_before,
                                        start=(back == 0), stop=(back == n - 1))
                    ins.then_inc(filled, 1)
                elif kind == "count1":
                    n = GT[item[1]]
                    for t in range(n):
                        ins = pe.matmul(dst[:, 0:E], ones[:, :], picked1[:, t, :], start=(t == 0), stop=(t == n - 1))
                    ins.then_inc(filled, 1)
                elif kind == "slot_t":
                    m = item[1]
                    pe.wait_ge(xg_in[m % N_X], 16 * (m // N_X + 1))
                    pe.transpose(dst[:, 0:P], xg[m % N_X], ident[:, :]).then_inc(filled, 1)
                elif kind == "slot_h":
                    m = item[1]
                    pe.wait_ge(w_in[m % N_W], 16 * (m // N_W + 1))
                    wait_emptied(pe, ("slot_t", m))
                    for c in range(HC):
                        ins = pe.matmul(dst[:, c * P:(c + 1) * P], wst[m % N_W][:, X_W1 + c * P:X_W1 + (c + 1) * P],
                                        xgT[m % 2], start=True, stop=True)
                    ins.then_inc(filled, 1)
                elif kind == "slot_y":
                    m = item[1]
                    wait_emptied(pe, ("slot_h", m))
                    for c in range(HC):
                        ins = pe.matmul(dst[:, 0:D], hT[m % 2][:, c, :],
                                        wst[m % N_W][:, X_W2 + c * D:X_W2 + (c + 1) * D],
                                        start=(c == 0), stop=(c == HC - 1))
                    ins.then_inc(filled, 1)

        @block.vector
        def _(dve):
            steps = 0

            def link(ins):
                nonlocal steps
                steps += 1
                ins.then_inc(dve_step, 1)
                dve.wait_ge(dve_step, steps)

            def rank_step(n, dst, of, width, before):
                nt = of.shape[1]
                a, b = cmp_a[:, 0:nt, 0:width, 0:width], cmp_b[:, 0:nt, 0:width, 0:width]
                vj = of.unsqueeze(2).broadcast_to([P, nt, width, width])
                vi = of.unsqueeze(3).broadcast_to([P, nt, width, width])
                if n == 0:
                    link(dve.tensor_tensor(a, vj, vi, ALU.is_gt))
                elif n == 1:
                    link(dve.tensor_tensor(b, vj, vi, ALU.is_equal))
                elif n == 2:
                    link(dve.tensor_tensor(b, b, before[:, :, :].unsqueeze(1).broadcast_to([P, nt, width, width]),
                                           ALU.mult))
                elif n == 3:
                    link(dve.tensor_tensor(a, a, b, ALU.add))
                else:
                    link(dve.tensor_reduce(dst, a, AX.X, ALU.add))

            def routed_tiles(l, g):
                return group_tiles(g) if l else slice(0, NT)

            dve.wait_ge(a_ready, 1)
            dve.tensor_scalar(neg_a[:, :, :], neg_a[:, :, :], -1.0, None, ALU.mult).then_inc(a_negated, 1)

            for item in order:
                kind = item[0]
                taken = emptied["dve"]
                if kind == "stats":
                    _, l, i = item
                    if l == 0:
                        dve.wait_ge(x_in[i], 16)
                    for t in range(TB):
                        ins = dve.bn_stats(stat[:, t, :], X[:, tiles(i).start + t, :])
                    link(ins)
                    for t in range(TB):
                        ins = dve.bn_aggr(mv[:, tiles(i).start + t, :], stat[:, t, :])
                    link(ins)
                    dve.tensor_scalar(veps[:, tiles(i)], mv[:, tiles(i), 1], EPS, None, ALU.add).then_inc(var_ready, 1)
                elif kind == "norm":
                    _, l, i = item
                    dve.wait_ge(rstd_ready, l * NB + i + 1)
                    for t in range(tiles(i).start, tiles(i).stop):
                        ins = dve.tensor_scalar(XN[:, t, :], X[:, t, :], mv[:, t, 0:1], rstd[:, t:t + 1],
                                                ALU.subtract, ALU.mult)
                    ins.then_inc(xn_ready, 1)
                elif kind == "logits":
                    _, l, i = item
                    wait_filled(dve, item)
                    src = bank(item)[:, 0:TB * E].rearrange("p (t e) -> p t e", t=TB)
                    if l == 0:
                        dve.tensor_copy(lg[:, 0, tiles(i), :], src).then_inc(taken, 1)
                    else:
                        dve.tensor_tensor(lg[:, 1, tiles(i), :], src,
                                          row[:, R_GB:R_END].unsqueeze(1).broadcast_to([P, TB, E]), ALU.add)\
                            .then_inc(taken, 1)
                elif kind == "base":
                    i = item[1]
                    wait_emptied(dve, item)
                    for n, t in enumerate((qT, kT)):
                        ins = dve.tensor_scalar(t[:, :], base[:, :], col[:, C_GAM + n:C_GAM + n + 1],
                                                col[:, C_BET + n:C_BET + n + 1], ALU.mult, ALU.add)
                    ins.then_inc(qk_ready, 1)
                elif kind == "sh_up":
                    i = item[1]
                    wait_filled(dve, item)
                    wait_emptied(dve, ("sh_gate", i))
                    dve.tensor_tensor(sh_h[:, :], sh_h[:, :], bank(item)[:, :], ALU.mult).then_inc(taken, 1)
                elif kind == "v0":
                    _, i, j = item
                    wait_filled(dve, item)
                    if i == 0 and j == 0:
                        dve.wait_ge(row_in, 16)
                    if i:
                        wait_filled(dve, ("attn", i - 1, 1))
                    dve.tensor_tensor(v[:, 2 * j:2 * j + 2, :], bank(item)[:, :].rearrange("p (t e) -> p t e", t=2),
                                      row[:, R_BV:R_BV + GE].unsqueeze(1).broadcast_to([P, 2, GE]), ALU.add)\
                        .then_inc(taken, 1)
                elif kind == "attn":
                    _, i, h = item
                    wait_filled(dve, item)
                    wait_emptied(dve, ("u0", i, h))
                    dve.tensor_tensor(uT[:, h, :], uT[:, h, :], bank(item)[:, :], ALU.mult).then_inc(taken, 1)
                elif kind == "wout":
                    wait_filled(dve, item)
                    dve.tensor_tensor(s0[:, :, :], bank(item)[:, :].rearrange("p (t d) -> p t d", t=TB),
                                      row[:, R_BOUT:R_BOUT + D].unsqueeze(1).broadcast_to([P, TB, D]), ALU.add)\
                        .then_inc(taken, 1)
                elif kind == "x1":
                    i = item[1]
                    wait_emptied(dve, ("sh_out", i))
                    wait_emptied(dve, ("wout", i))
                    link(dve.tensor_tensor(s0[:, :, :], s0[:, :, :], g0[:, :, :], ALU.mult))
                    dve.tensor_tensor(X[:, tiles(i), :], X[:, tiles(i), :], s0[:, :, :], ALU.add).then_inc(x1_done, 1)
                    dve.wait_ge(x1_done, i + 1)
                elif kind == "soft_a":
                    _, l, g = item
                    ts = routed_tiles(l, g)
                    wait_emptied(dve, ("logits", l, GROUPED[g][-1] if l else LAST))
                    link(dve.tensor_reduce(red[:, ts], lg[:, l, ts, :], AX.X, ALU.max))
                    n = ts.stop - ts.start
                    dve.tensor_tensor(lg[:, l, ts, :], lg[:, l, ts, :], red[:, ts].unsqueeze(2).broadcast_to([P, n, E]),
                                      ALU.subtract).then_inc(soft_in, 1)
                elif kind == "soft_b":
                    _, l, g = item
                    ts = routed_tiles(l, g)
                    n = ts.stop - ts.start
                    dve.wait_ge(soft_exp, softmaxes[l, g] + 1)
                    link(dve.tensor_reduce(red2[:, ts], sc[:, ts, :], AX.X, ALU.add))
                    link(dve.reciprocal(red2[:, ts], red2[:, ts]))
                    link(dve.tensor_tensor(sc[:, ts, :], sc[:, ts, :], red2[:, ts].unsqueeze(2).broadcast_to([P, n, E]),
                                           ALU.mult))
                    if l == 0:
                        link(dve.tensor_tensor(sel_s[:, :, :], sc[:, :, :],
                                               row[:, R_EB:R_EB + E].unsqueeze(1).broadcast_to([P, NT, E]), ALU.add))
                elif kind == "group":
                    pairs = sel_s[:, :, :].rearrange("p t (g c) -> p t g c", c=2)
                    if item[1] == 0:
                        dve.wait_ge(const_made, N_MADE)
                        link(dve.tensor_tensor(grp[:, :, :], sel_s[:, :, 0:E:2], sel_s[:, :, 1:E:2], ALU.add))
                        for n in range(2):
                            rank_step(n, keep[:, :, :], grp[:, :, :], GROUPS, before4)
                    elif item[1] == 1:
                        for n in range(2, 5):
                            rank_step(n, keep[:, :, :], grp[:, :, :], GROUPS, before4)
                        link(dve.tensor_scalar(keep[:, :, :], keep[:, :, :], 2.0, None, ALU.is_lt))
                    else:
                        link(dve.tensor_scalar(grp[:, :, :], keep[:, :, :], BIG, -BIG, ALU.mult, ALU.add))
                        link(dve.tensor_tensor(pairs, pairs, keep[:, :, :].unsqueeze(3)
                                               .broadcast_to([P, NT, GROUPS, 2]), ALU.mult))
                        link(dve.tensor_tensor(pairs, pairs, grp[:, :, :].unsqueeze(3)
                                               .broadcast_to([P, NT, GROUPS, 2]), ALU.add))
                elif kind == "rank":
                    _, l, g, n = item
                    ts = routed_tiles(l, g)
                    rank_step(n, rank[:, ts, :], sc[:, ts, :] if l else sel_s[:, :, :], E, before8)
                elif kind == "pick":
                    _, l, g, n = item
                    ts = routed_tiles(l, g)
                    nt = ts.stop - ts.start
                    if n == 0:
                        for k in range(TOPK):
                            ins = dve.tensor_scalar(pick[:, ts, k, :], rank[:, ts, :], float(k), None, ALU.is_equal)
                        link(ins)
                        if l and g:
                            wait_filled(dve, ("count1", g - 1))
                        dve.tensor_tensor(picked1[:, 0:nt, :] if l else picked0[:, :, :], pick[:, ts, 0, :], pick[:, ts, 1, :],
                                          ALU.add).then_inc(picked_ready, 1)
                    else:
                        link(dve.tensor_tensor(tmp8[:, ts, :, :], pick[:, ts, :, :],
                                               sc[:, ts, :].unsqueeze(2).broadcast_to([P, nt, TOPK, E]), ALU.mult))
                        link(dve.tensor_reduce(wgt[l][:, ts, :], tmp8[:, ts, :, :], AX.X, ALU.add))
                    if l == 0 and n == 1:
                        dve.wait_ge(const_set, N_SET)
                        wait_emptied(dve, ("xt", 0, LAST))
                        spread_x = xm.rearrange("p (g r) -> p g r", r=P + 1)[:, :, 0:P]
                        for k in range(TOPK):
                            ins = dve.tensor_copy(spread_x[:, :, k * E * E:(k + 1) * E * E:E],
                                                  XNT[:, 0:E].unsqueeze(1).broadcast_to([P, E, E]))
                        ins.then_inc(xm_ready, 1)
                elif kind == "count0":
                    wait_filled(dve, item)
                    dve.tensor_copy(cnt[:, :], bank(item)[:, 0:E]).then_inc(taken, 1)
                elif kind == "pairs":
                    if item[1] == 0:
                        wait_emptied(dve, ("count0",))
                        dve.memset(cum[:, 0:1], 0.0)
                        link(dve.tensor_tensor_scan(cum[:, 1:E + 1], cnt[:, :], cnt[:, :], 0.0, ALU.add, ALU.bypass))
                        link(dve.tensor_tensor(ge[:, :, :],
                                               row_no[:, :, :].rearrange("p t k -> p (t k)").unsqueeze(2)
                                               .broadcast_to([P, NT * TOPK, E + 1]),
                                               cum[:, :].unsqueeze(1).broadcast_to([P, NT * TOPK, E + 1]), ALU.is_ge))
                        link(dve.tensor_tensor(seg[:, :, :], ge[:, :, 0:E], ge[:, :, 1:E + 1], ALU.subtract))
                    else:
                        dve.wait_ge(slots_zeroed, 16 * NG)
                        dve.tensor_tensor(
                            pair.rearrange("p t k (e g) -> p (t k) e g", e=E),
                            pick[:, :, :, :].rearrange("p t k e -> p (t k) e").unsqueeze(3)
                            .broadcast_to([P, NT * TOPK, E, E]),
                            seg[:, :, :].unsqueeze(2).broadcast_to([P, NT * TOPK, E, E]), ALU.mult)\
                            .then_inc(pair_ready, 1)
                elif kind == "pair_in":
                    wait_filled(dve, item)
                    half = E * E
                    dve.tensor_copy(ab[0:half, 0, :], bank(item)[0:half, 0:P])
                    dve.tensor_copy(ab[half:2 * half, 1, :], bank(item)[half:2 * half, 0:P]).then_inc(taken, 1)
                elif kind == "pair_h":
                    q = item[1]
                    wait_filled(dve, item)
                    w = wgt[0][:, 2 * q:2 * q + 2, :].rearrange("p t k -> p (t k)").unsqueeze(2)
                    if q == NT // 4:
                        wait_filled(dve, ("pair_sum", 0))
                    j = 4 * q % NT
                    dve.tensor_tensor(ph[:, j:j + 4, :], bank(item)[:, :].rearrange("p (j c) -> p j c", j=4),
                                      w.broadcast_to([P, 4, 2 * HID0]), ALU.mult).then_inc(taken, 1)
                elif kind == "pair_act":
                    dve.wait_ge(pair_sig, item[1] + 1)
                    dve.tensor_tensor(ph[:, :, HID0:2 * HID0], ph[:, :, HID0:2 * HID0], gate0, ALU.mult)\
                        .then_inc(pair_out, 1)
                elif kind == "pair_sum":
                    n = item[1]
                    wait_filled(dve, item)
                    sums = bank(item)[0:HID0, 0:E * E].rearrange("p (e g) -> p g e", e=E)
                    if n == 0:
                        link(dve.memset(htp, 0.0))
                        dve.tensor_copy(htp[:, :, 0:E], sums).then_inc(taken, 1)
                    else:
                        wait_emptied(dve, ("pair_sum", 0))
                        dve.tensor_tensor(htp[:, :, 0:E], htp[:, :, 0:E], sums, ALU.add).then_inc(taken, 1)
                elif kind == "u1":
                    _, i, h = item
                    dve.wait_ge(tap_ready, 2 * i + h + 1)
                    if i == 0:
                        dve.wait_ge(const_set, N_SET)
                    dst = u1[:, i % 2, h, :]

                    def tap(k):
                        return col[:, C_CW + TAPS * h + k:C_CW + TAPS * h + k + 1]
                    for k in range(TAPS - 1):
                        ins = dve.scalar_tensor_tensor(dst, upad[:, h, k:k + S], tap(k), dst, ALU.mult, ALU.add)
                        if k < TAPS - 2:
                            link(ins)
                    ins.then_inc(conv_ready, 1)
                elif kind == "xproj":
                    i = item[1]
                    wait_emptied(dve, item)
                    if i >= 2:
                        dve.wait_ge(b_cast, step_no(i - 2, NS - 1) + 1)
                    parts = [bcs[2 * NS * j:2 * NS * j + NS, i % 2, :] for j in range(3)]
                    rest, mid = bc[0:NS, :], bc_mid[:, :]
                    link(dve.tensor_copy(parts[0], rest))
                    link(dve.tensor_tensor(rest, rest, parts[0], ALU.subtract))
                    link(dve.tensor_copy(mid, rest))
                    dve.tensor_copy(parts[1], mid)
                    dve.tensor_tensor(parts[2], rest, mid, ALU.subtract).then_inc(bcs_ready, 1)
                elif kind == "softplus":
                    i = item[1]
                    z, l, uu = delta[:, i % 2], du[:, i % 2], u1[:, i % 2]
                    dve.wait_ge(l_ready, i + 1)
                    link(dve.scalar_tensor_tensor(z, z, 0.0, l, ALU.max, ALU.add))
                    dve.wait_ge(u1_ready, i + 1)
                    dve.tensor_tensor(l, z, uu, ALU.mult).then_inc(du_ready, 1)
                    dve.wait_ge(du_ready, i + 1)
                elif kind == "cast":
                    _, i, n = item
                    g = step_no(i, n)
                    dve.wait_ge(b_cast, g + 1)
                    last = g - N_RING
                    if last >= 0:
                        if last // NS in PAIRED and last % 2 == 0:
                            dve.wait_ge(paired, pairs_upto(last + 1))
                        else:
                            dve.wait_ge(summed, sums_upto(last))
                    dve.tensor_tensor(ring[:, g % N_RING], du[:, i % 2],
                                      p_b[g % 2][:, :].unsqueeze(1).broadcast_to([P, HV, S]), ALU.mult)\
                        .then_inc(drive_ready, 1)
                elif kind == "step":
                    _, i, n = item
                    g = step_no(i, n)
                    dve.wait_ge(decay_ready, g + 1)
                    dve.wait_ge(drive_ready, g + 1)
                    if g == 0:
                        dve.wait_ge(const_set, N_SET)
                    flat = ring[:, g % N_RING].rearrange("p h t -> p (h t)")
                    dve.tensor_tensor_scan(flat, decay[:, g % N_DA].rearrange("p h t -> p (h t)"), flat, 0.0,
                                           ALU.mult, ALU.add).then_inc(state_ready, 1)
                elif kind == "sum" and item[1] in PAIRED - PAIRED_BY_POOL:
                    add_pair(dve, item)
                elif kind == "scan_out":
                    i = item[1]
                    dve.wait_ge(summed, sums_upto(step_no(i, NS - 1)))
                    for h in range(HV):
                        ins = dve.scalar_tensor_tensor(u1[:, i % 2, h, :], u1[:, i % 2, h, :],
                                                       col[:, C_D + h:C_D + h + 1], p_y[h][:, :], ALU.mult, ALU.add)
                    ins.then_inc(y_read, 1)
                    dve.wait_ge(y_read, i + 1)
                    wait_emptied(dve, ("gate1", i, 1))
                    dve.tensor_tensor(u1[:, i % 2], u1[:, i % 2], g1[:, i % 2], ALU.mult).then_inc(y_ready, 1)
                elif kind == "wo1":
                    i = item[1]
                    wait_filled(dve, item)
                    dve.tensor_tensor(s1[:, tiles(i), :], bank(item)[:, :].rearrange("p (t d) -> p t d", t=TB),
                                      row[:, R_BO:R_BO + D].unsqueeze(1).broadcast_to([P, TB, D]), ALU.add)\
                        .then_inc(taken, 1)
                elif kind == "rank1":
                    wait_filled(dve, item)
                    n = GT[item[1]]
                    dve.tensor_copy(rank[:, group_tiles(item[1]), :],
                                    bank(item)[:, 0:n * E].rearrange("p (t e) -> p t e", t=n)).then_inc(taken, 1)
                elif kind == "count1":
                    wait_filled(dve, item)
                    dve.tensor_copy(cnt[:, :], bank(item)[:, 0:E]).then_inc(taken, 1)
                    wait_emptied(dve, item)
                elif kind == "route1_slots":
                    _, g, n = item
                    ts = group_tiles(g)
                    nt, ns = GT[g], SLOTS[g]
                    if n == 0:
                        link(dve.tensor_tensor(cmp_t[:, :, 0:nt], cnt[:, :].unsqueeze(2).broadcast_to([P, E, nt]),
                                               mult128[:, 0:nt].unsqueeze(1).broadcast_to([P, E, nt]), ALU.is_gt))
                        link(dve.tensor_reduce(ntile[:, :], cmp_t[:, :, 0:nt], AX.X, ALU.add))
                        link(dve.tensor_tensor_scan(ctile[:, :], ntile[:, :], ntile[:, :], 0.0, ALU.add, ALU.bypass))
                        link(dve.tensor_tensor(cmp_s[:, 0:ns, :], slot_no[:, 0:ns].unsqueeze(2).broadcast_to([P, ns, E]),
                                               ctile[:, :].unsqueeze(1).broadcast_to([P, ns, E]), ALU.is_ge))
                        link(dve.tensor_reduce(slot_f[:, 0:ns], cmp_s[:, 0:ns, :], AX.X, ALU.add))
                        dve.tensor_scalar(slot_e[:, SLOT0[g]:SLOT0[g] + ns], slot_f[:, 0:ns], float(E - 1), None,
                                          ALU.min)
                    else:
                        link(dve.tensor_tensor(first_row[:, :], ctile[:, :], ntile[:, :], ALU.subtract))
                        link(dve.tensor_scalar(first_row[:, :], first_row[:, :], float(P), None, ALU.mult))
                        link(dve.tensor_tensor(rank[:, ts, :], rank[:, ts, :],
                                               first_row[:, :].unsqueeze(1).broadcast_to([P, nt, E]), ALU.add))
                        link(dve.tensor_tensor(tmp8[:, ts, :, :], pick[:, ts, :, :],
                                               rank[:, ts, :].unsqueeze(2).broadcast_to([P, nt, TOPK, E]), ALU.mult))
                        link(dve.tensor_reduce(pos_f[:, ts, :], tmp8[:, ts, :, :], AX.X, ALU.add))
                        dve.tensor_copy(pos[:, :, ts], pos_f[:, ts, :].rearrange("p t k -> p k t"))\
                            .then_inc(pos_ready, 1)
                elif kind == "slot_y":
                    m = item[1]
                    wait_filled(dve, item)
                    if m >= 3:
                        dve.wait_ge(y_out[m % 3], 16 * (m // 3))
                    dve.tensor_tensor(ysb[m % 3], bank(item)[:, 0:D], wst[m % N_W][:, X_B2:X_END], ALU.add)\
                        .then_inc(taken, 1)
                elif kind == "mix":
                    i = item[1]
                    dve.wait_ge(gathered[i], 16 * TB * TOPK)
                    for t in range(tiles(i).start, tiles(i).stop):
                        ins = dve.tensor_scalar(yk[0][:, t, :], yk[0][:, t, :], wgt[1][:, t, 0:1], None, ALU.mult)
                    link(ins)
                    for t in range(tiles(i).start, tiles(i).stop):
                        ins = dve.scalar_tensor_tensor(yk[0][:, t, :], yk[1][:, t, :], wgt[1][:, t, 1:2],
                                                       yk[0][:, t, :], ALU.mult, ALU.add)
                    ins.then_inc(mix_ready, 1)
                elif kind == "done":
                    i = item[1]
                    dve.wait_ge(mix_silu, i + 1)
                    wait_emptied(dve, ("wo1", i))
                    link(dve.tensor_tensor(s1[:, tiles(i), :], s1[:, tiles(i), :], yk[0][:, tiles(i), :], ALU.mult))
                    dve.tensor_tensor(X[:, tiles(i), :], X[:, tiles(i), :], s1[:, tiles(i), :], ALU.add)\
                        .then_inc(out_ready, 1)


def _host_layout(inputs):
    import numpy as np

    a = {k: np.asarray(v) for k, v in inputs.items()}

    def cat(*parts):
        return np.ascontiguousarray(np.concatenate(parts, axis=1))

    def chunks(w):
        c = w.shape[0] // P
        return w.reshape(c, P, -1).transpose(1, 0, 2).reshape(P, -1)

    def per_partition(v):
        return v.reshape(-1, P).T

    pack_a = cat(a["L0_attn_W_uv"], a["L0_ffn_sw1"].T, a["L0_ffn_sw3"].T, a["L0_ffn_sw2"].T,
                 chunks(a["L0_attn_W_out"]), a["L0_ffn_w_gate"].T, a["L1_ffn_gate_w"])
    w13 = np.concatenate([a["L0_ffn_w1"], a["L0_ffn_w3"]], axis=2).transpose(1, 0, 2).reshape(D, -1)
    pack_b = cat(w13, a["L1_attn_W1"], a["L1_attn_W2"], chunks(a["L1_attn_x_proj_w"]), chunks(a["L1_attn_Wo"]))
    pack_h = cat(a["L0_ffn_w2"].transpose(1, 0, 2).reshape(HID0, -1), a["L1_attn_dt_proj_w"])
    b_uv = a["L0_attn_b_uv"]
    cols = cat(per_partition(b_uv[0:GE]), per_partition(b_uv[2 * GE:]), a["L0_attn_gamma"].T, a["L0_attn_beta"].T,
               per_partition(a["L1_attn_b1"]), per_partition(a["L1_attn_b2"]), chunks(a["L1_attn_conv_w"]),
               per_partition(a["L1_attn_conv_b"]), per_partition(a["L1_attn_dt_proj_b"]),
               per_partition(a["L1_attn_D_skip"]), chunks(a["L1_attn_A_log"]))
    rows = np.ascontiguousarray(np.concatenate(
        [b_uv[GE:2 * GE], a["L0_attn_b_out"], a["L0_ffn_expert_bias"], a["L1_attn_bo"], a["L1_ffn_gate_b"]]))
    experts = np.ascontiguousarray(np.concatenate([
        a["L1_ffn_w1"],
        a["L1_ffn_w2"].reshape(E, HC, P, D).transpose(0, 2, 1, 3).reshape(E, P, HC * D),
        a["L1_ffn_b1"].reshape(E, HC, P).transpose(0, 2, 1),
        np.broadcast_to(a["L1_ffn_b2"][:, None, :], (E, P, D))], axis=2))
    x = np.ascontiguousarray(a["L0_attn_inputs"])
    return {"x": x, "pack_a": pack_a, "pack_b": pack_b, "pack_h": pack_h, "cols": cols, "rows": rows,
            "experts": experts}


def kernel(**inputs):
    import concourse.bacc as _bacc
    from concourse.bass_utils import run_bass_kernel_spmd as _run

    nc = _bacc.Bacc("TRN2", target_bir_lowering=False, num_devices=1)
    arrays = _host_layout(inputs)
    args = {n: nc.dram_tensor(n, v.shape, mybir.dt.from_np(v.dtype), kind="ExternalInput").ap()
            for n, v in arrays.items()}
    out = nc.dram_tensor("out", (NB, S, D), F32, kind="ExternalOutput").ap()
    slot_in, slot_out = ([nc.dram_tensor(f"slot_{way}{g}", (SLOTS[g], P, D), F32, kind="Internal").ap()
                          for g in range(NG)] for way in ("in", "out"))
    c_rows = nc.dram_tensor("c_rows", (NB, NS, S), F32, kind="Internal").ap()
    build(nc, args["x"], args["pack_a"], args["pack_b"], args["pack_h"], args["cols"], args["rows"],
          args["experts"], out, slot_in, slot_out, c_rows)
    r = _run(nc, [arrays], core_ids=[0])
    return r.results[0]["out"]
```
